# Optimizing a Trainium2 kernel written in Bass

```python
import numpy as np
import jax
import jax.numpy as jnp

def _softmax(x, axis=-1):
    return jax.nn.softmax(x, axis=axis)

def _gelu(x):
    return jax.nn.gelu(x, approximate=True)

def _silu(x):
    return jax.nn.silu(x)

def _sigmoid(x):
    return jax.nn.sigmoid(x)

def _layernorm(x, axis=-1, eps=1e-05):
    m = jnp.mean(x, axis=axis, keepdims=True)
    v = jnp.var(x, axis=axis, keepdims=True)
    return (x - m) / jnp.sqrt(v + eps)

def _scatter_add(tgt, idx, src, axis=0):
    return tgt.at[idx].add(src)

def _segment_sum(src, seg, n):
    return jax.ops.segment_sum(src, seg, n)
kernel_name = 'mk_lm_tower_d2_tok_ids512_r4_c00010'

def setup_inputs(seed: int=0):
    np.random.seed(seed)
    _w = jnp.asarray

    def _rec_inputs():
        import jax
        import jax.numpy as jnp
        _rk = jax.random.key(seed)
        x = jax.random.randint(jax.random.fold_in(_rk, 1), (16, 128), 0, 7, jnp.int32)
        itok_BS_0_1439 = jax.random.randint(jax.random.fold_in(_rk, 21), (16, 128), 0, 360, jnp.int32)
        fside_BS_durations = 995.805 + 576.683 * jax.random.normal(jax.random.fold_in(_rk, 22), (16, 128), jnp.float32)
        itok_BS_0_7 = jax.random.randint(jax.random.fold_in(_rk, 23), (16, 128), 0, 8, jnp.int32)
        return (x, itok_BS_0_1439, fside_BS_durations, itok_BS_0_7)
    x, itok_BS_0_1439, fside_BS_durations, itok_BS_0_7 = _rec_inputs()

    def _L0_tok_setup():
        import jax, jax.numpy as jnp
        import numpy as np
        import math
        B, L, HIDDEN = (32, 1024, 128)
        FEAT = 12 + 12 + 8 + 8 + 2
        LN_EPS = 1e-05
        key = jax.random.key(seed)
        ks = jax.random.split(key, 12)
        weekdays = jax.random.randint(ks[0], (B, L), 0, 7, dtype=jnp.int32)
        start_mins = jax.random.randint(ks[1], (B, L), 0, 360, dtype=jnp.int32)
        durations = jax.random.uniform(ks[2], (B, L), dtype=jnp.float32) * 2000.0
        time_diffs = jax.random.randint(ks[3], (B, L), 0, 8, dtype=jnp.int32)
        W_weekday = jax.random.normal(ks[4], (7, 12), dtype=jnp.float32)
        W_hour = jax.random.normal(ks[5], (24, 12), dtype=jnp.float32)
        W_dur = jax.random.normal(ks[6], (10, 8), dtype=jnp.float32)
        W_tdiff = jax.random.normal(ks[7], (8, 8), dtype=jnp.float32)
        dur_boundaries = jnp.linspace(0.0, 8.0, 10, dtype=jnp.float32)
        proj_w = jax.random.normal(ks[8], (HIDDEN, FEAT), dtype=jnp.float32) / np.sqrt(FEAT)
        proj_b = jax.random.normal(ks[9], (HIDDEN,), dtype=jnp.float32) * 0.01
        ln_w = jnp.ones((HIDDEN,), dtype=jnp.float32)
        ln_b = jnp.zeros((HIDDEN,), dtype=jnp.float32)
        return {'weekdays': weekdays, 'start_mins': start_mins, 'durations': durations, 'time_diffs': time_diffs, 'W_weekday': W_weekday, 'W_hour': W_hour, 'W_dur': W_dur, 'W_tdiff': W_tdiff, 'dur_boundaries': dur_boundaries, 'proj_w': proj_w, 'proj_b': proj_b, 'ln_w': ln_w, 'ln_b': ln_b}
    _L0_tok_all = _L0_tok_setup()
    _L0_tok_in = {k: v for k, v in _L0_tok_all.items() if k in ('W_weekday', 'W_hour', 'W_dur', 'W_tdiff', 'dur_boundaries', 'proj_w', 'proj_b', 'ln_w', 'ln_b')}
    del _L0_tok_all

    def _L0_attn_setup():
        import jax, jax.numpy as jnp
        import numpy as np
        HEADS = 8
        DIM_HEAD = 64
        MAX_POS_EMB = 128
        DIM = 128
        INNER = HEADS * DIM_HEAD
        SCALE = DIM_HEAD ** (-0.5)
        key = jax.random.key(seed)
        ks = jax.random.split(key, 6)
        B, N = (4, 512)
        x = jax.random.normal(ks[0], (B, N, DIM), dtype=jnp.float32)
        Wq = jax.random.normal(ks[1], (DIM, INNER), dtype=jnp.float32) * DIM ** (-0.5)
        Wkv = jax.random.normal(ks[2], (DIM, 2 * INNER), dtype=jnp.float32) * DIM ** (-0.5)
        Wo = jax.random.normal(ks[3], (INNER, DIM), dtype=jnp.float32) * INNER ** (-0.5)
        bo = jax.random.normal(ks[4], (DIM,), dtype=jnp.float32) * 0.02
        rel_emb = jax.random.normal(ks[5], (2 * MAX_POS_EMB + 1, DIM_HEAD), dtype=jnp.float32) * 0.02
        return {'x': x, 'Wq': Wq, 'Wkv': Wkv, 'Wo': Wo, 'bo': bo, 'rel_emb': rel_emb}
    _L0_attn_all = _L0_attn_setup()
    _L0_attn_in = {k: v for k, v in _L0_attn_all.items() if k in ('Wq', 'Wkv', 'Wo', 'bo', 'rel_emb')}
    del _L0_attn_all

    def _L0_ffn_setup():
        import jax, jax.numpy as jnp
        import numpy as np
        EPS = 1e-05
        TOP_K = 2

        def _moe_forward(x, Wg, W1, b1, W2, b2, gamma, beta):
            B, S, D = x.shape
            xf = x.reshape(-1, D)
            logits = xf @ Wg
            topv, topi = jax.lax.top_k(logits, TOP_K)
            gate_w = jax.nn.softmax(topv, axis=-1)
            h = jax.nn.relu(jnp.einsum('td,edh->teh', xf, W1) + b1[None])
            y = jnp.einsum('teh,ehd->ted', h, W2) + b2[None]
            mu = jnp.mean(y, axis=-1, keepdims=True)
            var = jnp.mean((y - mu) ** 2, axis=-1, keepdims=True)
            y = (y - mu) / jnp.sqrt(var + EPS) * gamma[None] + beta[None]
            y_sel = jnp.take_along_axis(y, topi[:, :, None], axis=1)
            out = jnp.sum(gate_w[:, :, None] * y_sel, axis=1)
            return out.reshape(B, S, D)
        key = jax.random.key(seed)
        ks = jax.random.split(key, 8)
        B, S, D, H, E = (4, 512, 128, 128, 8)
        sd = lambda fan_in: 1.0 / np.sqrt(fan_in)
        x = jax.random.normal(ks[0], (B, S, D), dtype=jnp.float32)
        Wg = jax.random.uniform(ks[1], (D, E), jnp.float32, -sd(D), sd(D))
        W1 = jax.random.uniform(ks[2], (E, D, H), jnp.float32, -sd(D), sd(D))
        b1 = jax.random.uniform(ks[3], (E, H), jnp.float32, -sd(D), sd(D))
        W2 = jax.random.uniform(ks[4], (E, H, D), jnp.float32, -sd(H), sd(H))
        b2 = jax.random.uniform(ks[5], (E, D), jnp.float32, -sd(H), sd(H))
        gamma = jnp.ones((E, D), jnp.float32)
        beta = jnp.zeros((E, D), jnp.float32)
        return {'x': x, 'Wg': Wg, 'W1': W1, 'b1': b1, 'W2': W2, 'b2': b2, 'gamma': gamma, 'beta': beta}
    _L0_ffn_all = _L0_ffn_setup()
    _L0_ffn_in = {k: v for k, v in _L0_ffn_all.items() if k in ('Wg', 'W1', 'b1', 'W2', 'b2', 'gamma', 'beta')}
    del _L0_ffn_all

    def _L1_attn_setup():
        import jax, jax.numpy as jnp
        import numpy as np
        import math
        D_MODEL = 128
        N_HEADS = 8
        HEAD_DIM = D_MODEL // N_HEADS
        WINDOW = 128
        LOCAL_BLOCK = 64
        LATENT_TOKENS = 64
        LATENT_D = 64
        LATENT_HEADS = 4
        LATENT_HEAD_DIM = LATENT_D // LATENT_HEADS

        def _local_attention(q, k, v):
            B, H, S, Dh = q.shape
            block = min(S, max(WINDOW, LOCAL_BLOCK))
            nb = S // block
            pad = WINDOW - 1
            kp = jnp.pad(k, ((0, 0), (0, 0), (pad, 0), (0, 0)))
            vp = jnp.pad(v, ((0, 0), (0, 0), (pad, 0), (0, 0)))
            scale = 1.0 / math.sqrt(Dh)

            def one_block(i):
                qs = i * block
                qb = jax.lax.dynamic_slice_in_dim(q, qs, block, axis=2)
                kb = jax.lax.dynamic_slice_in_dim(kp, qs, block + pad, axis=2)
                vb = jax.lax.dynamic_slice_in_dim(vp, qs, block + pad, axis=2)
                qpos = qs + jnp.arange(block)
                kpos = qs - pad + jnp.arange(block + pad)
                dist = qpos[:, None] - kpos[None, :]
                allowed = (dist >= 0) & (dist < WINDOW) & (kpos[None, :] >= 0)
                scores = jnp.einsum('bhqd,bhkd->bhqk', qb, kb) * scale
                scores = jnp.where(allowed[None, None], scores, -jnp.inf)
                attn = jax.nn.softmax(scores, axis=-1)
                return jnp.einsum('bhqk,bhkd->bhqd', attn, vb)
            out = jax.vmap(one_block)(jnp.arange(nb))
            return out.transpose(1, 2, 0, 3, 4).reshape(B, H, S, Dh)
        key = jax.random.key(seed)
        ks = jax.random.split(key, 20)
        B, S, D = (4, 2048, D_MODEL)

        def lin(k, din, dout):
            kw, kb = jax.random.split(k)
            W = jax.random.normal(kw, (din, dout), jnp.float32) * (1.0 / math.sqrt(din))
            b = jax.random.normal(kb, (dout,), jnp.float32) * 0.01
            return (W, b)
        x = jax.random.normal(ks[0], (B, S, D), jnp.float32)
        Wq, bq = lin(ks[1], D, D)
        Wk, bk = lin(ks[2], D, D)
        Wv, bv = lin(ks[3], D, D)
        Wrq, brq = lin(ks[4], D, LATENT_D)
        Wrk, brk = lin(ks[5], D, LATENT_D)
        Wrv, brv = lin(ks[6], D, LATENT_D)
        Wro, bro = lin(ks[7], LATENT_D, D)
        Wo, bo = lin(ks[8], D, D)
        Wg, bg = lin(ks[9], 2 * D, 1)
        return dict(x=x, Wq=Wq, bq=bq, Wk=Wk, bk=bk, Wv=Wv, bv=bv, Wrq=Wrq, brq=brq, Wrk=Wrk, brk=brk, Wrv=Wrv, brv=brv, Wro=Wro, bro=bro, Wo=Wo, bo=bo, Wg=Wg, bg=bg)
    _L1_attn_all = _L1_attn_setup()
    _L1_attn_in = {k: v for k, v in _L1_attn_all.items() if k in ('Wq', 'bq', 'Wk', 'bk', 'Wv', 'bv', 'Wrq', 'brq', 'Wrk', 'brk', 'Wrv', 'brv', 'Wro', 'bro', 'Wo', 'bo', 'Wg', 'bg')}
    del _L1_attn_all

    def _L1_ffn_setup():
        import jax, jax.numpy as jnp
        import numpy as np
        B, N, DIM = (1, 512, 128)
        DH, H = (64, 8)
        E, FF = (8, 512)

        def _layernorm(x, g, b, eps=1e-05):
            mu = jnp.mean(x, axis=-1, keepdims=True)
            var = jnp.mean(jnp.square(x - mu), axis=-1, keepdims=True)
            return (x - mu) * jax.lax.rsqrt(var + eps) * g + b

        def _l2norm(x, eps=1e-12):
            return x / jnp.sqrt(jnp.sum(jnp.square(x), axis=-1, keepdims=True) + eps)
        key = jax.random.key(seed)
        ks = jax.random.split(key, 12)
        g = lambda k, shape: jax.random.normal(k, shape, jnp.float32) * 0.02
        return {'x': jax.random.normal(ks[0], (B, N, DIM), jnp.float32), 'ln_g': jnp.ones((DIM,), jnp.float32), 'ln_b': jnp.zeros((DIM,), jnp.float32), 'Wq': g(ks[1], (DIM, DIM)), 'Wk': g(ks[2], (DIM, DIM)), 'Wv': g(ks[3], (DIM, DIM)), 'Wo': g(ks[4], (DIM, DIM)), 'qn_g': jnp.ones((DH,), jnp.float32), 'kn_g': jnp.ones((DH,), jnp.float32), 'gate_W': g(ks[5], (DIM, E)), 'gate_b': jnp.zeros((E,), jnp.float32), 'W1': g(ks[6], (E, DIM, FF)), 'b1': jnp.zeros((E, FF), jnp.float32), 'W2': g(ks[7], (E, FF, DIM)), 'b2': jnp.zeros((E, DIM), jnp.float32)}
    _L1_ffn_all = _L1_ffn_setup()
    _L1_ffn_in = {k: v for k, v in _L1_ffn_all.items() if k in ('ln_g', 'ln_b', 'Wq', 'Wk', 'Wv', 'Wo', 'qn_g', 'kn_g', 'gate_W', 'gate_b', 'W1', 'b1', 'W2', 'b2')}
    del _L1_ffn_all
    return {'x': x, 'itok_BS_0_1439': itok_BS_0_1439, 'fside_BS_durations': fside_BS_durations, 'itok_BS_0_7': itok_BS_0_7, 'L0_tok_W_weekday': _L0_tok_in['W_weekday'], 'L0_tok_W_hour': _L0_tok_in['W_hour'], 'L0_tok_W_dur': _L0_tok_in['W_dur'], 'L0_tok_W_tdiff': _L0_tok_in['W_tdiff'], 'L0_tok_dur_boundaries': _L0_tok_in['dur_boundaries'], 'L0_tok_proj_w': _L0_tok_in['proj_w'], 'L0_tok_proj_b': _L0_tok_in['proj_b'], 'L0_tok_ln_w': _L0_tok_in['ln_w'], 'L0_tok_ln_b': _L0_tok_in['ln_b'], 'L0_attn_Wq': _L0_attn_in['Wq'], 'L0_attn_Wkv': _L0_attn_in['Wkv'], 'L0_attn_Wo': _L0_attn_in['Wo'], 'L0_attn_bo': _L0_attn_in['bo'], 'L0_attn_rel_emb': _L0_attn_in['rel_emb'], 'L0_ffn_Wg': _L0_ffn_in['Wg'], 'L0_ffn_W1': _L0_ffn_in['W1'], 'L0_ffn_b1': _L0_ffn_in['b1'], 'L0_ffn_W2': _L0_ffn_in['W2'], 'L0_ffn_b2': _L0_ffn_in['b2'], 'L0_ffn_gamma': _L0_ffn_in['gamma'], 'L0_ffn_beta': _L0_ffn_in['beta'], 'L1_attn_Wq': _L1_attn_in['Wq'], 'L1_attn_bq': _L1_attn_in['bq'], 'L1_attn_Wk': _L1_attn_in['Wk'], 'L1_attn_bk': _L1_attn_in['bk'], 'L1_attn_Wv': _L1_attn_in['Wv'], 'L1_attn_bv': _L1_attn_in['bv'], 'L1_attn_Wrq': _L1_attn_in['Wrq'], 'L1_attn_brq': _L1_attn_in['brq'], 'L1_attn_Wrk': _L1_attn_in['Wrk'], 'L1_attn_brk': _L1_attn_in['brk'], 'L1_attn_Wrv': _L1_attn_in['Wrv'], 'L1_attn_brv': _L1_attn_in['brv'], 'L1_attn_Wro': _L1_attn_in['Wro'], 'L1_attn_bro': _L1_attn_in['bro'], 'L1_attn_Wo': _L1_attn_in['Wo'], 'L1_attn_bo': _L1_attn_in['bo'], 'L1_attn_Wg': _L1_attn_in['Wg'], 'L1_attn_bg': _L1_attn_in['bg'], 'L1_ffn_ln_g': _L1_ffn_in['ln_g'], 'L1_ffn_ln_b': _L1_ffn_in['ln_b'], 'L1_ffn_Wq': _L1_ffn_in['Wq'], 'L1_ffn_Wk': _L1_ffn_in['Wk'], 'L1_ffn_Wv': _L1_ffn_in['Wv'], 'L1_ffn_Wo': _L1_ffn_in['Wo'], 'L1_ffn_qn_g': _L1_ffn_in['qn_g'], 'L1_ffn_kn_g': _L1_ffn_in['kn_g'], 'L1_ffn_gate_W': _L1_ffn_in['gate_W'], 'L1_ffn_gate_b': _L1_ffn_in['gate_b'], 'L1_ffn_W1': _L1_ffn_in['W1'], 'L1_ffn_b1': _L1_ffn_in['b1'], 'L1_ffn_W2': _L1_ffn_in['W2'], 'L1_ffn_b2': _L1_ffn_in['b2']}

def reference(x, itok_BS_0_1439, fside_BS_durations, itok_BS_0_7, L0_tok_W_weekday, L0_tok_W_hour, L0_tok_W_dur, L0_tok_W_tdiff, L0_tok_dur_boundaries, L0_tok_proj_w, L0_tok_proj_b, L0_tok_ln_w, L0_tok_ln_b, L0_attn_Wq, L0_attn_Wkv, L0_attn_Wo, L0_attn_bo, L0_attn_rel_emb, L0_ffn_Wg, L0_ffn_W1, L0_ffn_b1, L0_ffn_W2, L0_ffn_b2, L0_ffn_gamma, L0_ffn_beta, L1_attn_Wq, L1_attn_bq, L1_attn_Wk, L1_attn_bk, L1_attn_Wv, L1_attn_bv, L1_attn_Wrq, L1_attn_brq, L1_attn_Wrk, L1_attn_brk, L1_attn_Wrv, L1_attn_brv, L1_attn_Wro, L1_attn_bro, L1_attn_Wo, L1_attn_bo, L1_attn_Wg, L1_attn_bg, L1_ffn_ln_g, L1_ffn_ln_b, L1_ffn_Wq, L1_ffn_Wk, L1_ffn_Wv, L1_ffn_Wo, L1_ffn_qn_g, L1_ffn_kn_g, L1_ffn_gate_W, L1_ffn_gate_b, L1_ffn_W1, L1_ffn_b1, L1_ffn_W2, L1_ffn_b2):
    import jax
    import jax.numpy as jnp

    def _L0_tok_ref(weekdays, start_mins, durations, time_diffs, W_weekday, W_hour, W_dur, W_tdiff, dur_boundaries, proj_w, proj_b, ln_w, ln_b):
        import jax, jax.numpy as jnp
        import numpy as np
        import math
        B, L, HIDDEN = (32, 1024, 128)
        FEAT = 12 + 12 + 8 + 8 + 2
        LN_EPS = 1e-05
        weekday_emb = W_weekday[weekdays]
        hours = jnp.clip(start_mins // 60, 0, 23)
        hour_emb = W_hour[hours]
        theta = start_mins.astype(jnp.float32) / 1440.0 * (2.0 * math.pi)
        time_sin = jnp.sin(theta)[..., None]
        time_cos = jnp.cos(theta)[..., None]
        log_dur = jnp.log1p(durations)
        dur_bins = jnp.clip(jnp.searchsorted(dur_boundaries, log_dur, side='left') - 1, 0, 9)
        dur_emb = W_dur[dur_bins]
        time_diff_emb = W_tdiff[time_diffs]
        features = jnp.concatenate([weekday_emb, hour_emb, time_sin, time_cos, dur_emb, time_diff_emb], axis=-1)
        x = jnp.einsum('blf,hf->blh', features, proj_w) + proj_b
        mu = jnp.mean(x, axis=-1, keepdims=True)
        var = jnp.mean(jnp.square(x - mu), axis=-1, keepdims=True)
        return (x - mu) * jax.lax.rsqrt(var + LN_EPS) * ln_w + ln_b

    def _L0_attn_ref(x, Wq, Wkv, Wo, bo, rel_emb):
        import jax, jax.numpy as jnp
        import numpy as np
        HEADS = 8
        DIM_HEAD = 64
        MAX_POS_EMB = 128
        DIM = 128
        INNER = HEADS * DIM_HEAD
        SCALE = DIM_HEAD ** (-0.5)
        B, N, _ = x.shape
        q = x @ Wq
        kv = x @ Wkv
        k, v = jnp.split(kv, 2, axis=-1)

        def split_heads(t):
            return t.reshape(B, N, HEADS, DIM_HEAD).transpose(0, 2, 1, 3)
        q, k, v = (split_heads(q), split_heads(k), split_heads(v))
        dots = jnp.einsum('bhnd,bhrd->bhnr', q, k) * SCALE
        seq = jnp.arange(N)
        dist = jnp.clip(seq[:, None] - seq[None, :], -MAX_POS_EMB, MAX_POS_EMB) + MAX_POS_EMB
        rel = rel_emb[dist]
        pos_attn = jnp.einsum('bhnd,nrd->bhnr', q, rel) * SCALE
        attn = jax.nn.softmax(dots + pos_attn, axis=-1)
        out = jnp.einsum('bhij,bhjd->bhid', attn, v)
        out = out.transpose(0, 2, 1, 3).reshape(B, N, INNER)
        return out @ Wo + bo

    def _L0_ffn_ref(x, Wg, W1, b1, W2, b2, gamma, beta):
        import jax, jax.numpy as jnp
        import numpy as np
        EPS = 1e-05
        TOP_K = 2

        def _moe_forward(x, Wg, W1, b1, W2, b2, gamma, beta):
            B, S, D = x.shape
            xf = x.reshape(-1, D)
            logits = xf @ Wg
            topv, topi = jax.lax.top_k(logits, TOP_K)
            gate_w = jax.nn.softmax(topv, axis=-1)
            h = jax.nn.relu(jnp.einsum('td,edh->teh', xf, W1) + b1[None])
            y = jnp.einsum('teh,ehd->ted', h, W2) + b2[None]
            mu = jnp.mean(y, axis=-1, keepdims=True)
            var = jnp.mean((y - mu) ** 2, axis=-1, keepdims=True)
            y = (y - mu) / jnp.sqrt(var + EPS) * gamma[None] + beta[None]
            y_sel = jnp.take_along_axis(y, topi[:, :, None], axis=1)
            out = jnp.sum(gate_w[:, :, None] * y_sel, axis=1)
            return out.reshape(B, S, D)
        return _moe_forward(x, Wg, W1, b1, W2, b2, gamma, beta)

    def _L1_attn_ref(x, Wq, bq, Wk, bk, Wv, bv, Wrq, brq, Wrk, brk, Wrv, brv, Wro, bro, Wo, bo, Wg, bg):
        import jax, jax.numpy as jnp
        import numpy as np
        import math
        D_MODEL = 128
        N_HEADS = 8
        HEAD_DIM = D_MODEL // N_HEADS
        WINDOW = 128
        LOCAL_BLOCK = 64
        LATENT_TOKENS = 64
        LATENT_D = 64
        LATENT_HEADS = 4
        LATENT_HEAD_DIM = LATENT_D // LATENT_HEADS

        def _local_attention(q, k, v):
            B, H, S, Dh = q.shape
            block = min(S, max(WINDOW, LOCAL_BLOCK))
            nb = S // block
            pad = WINDOW - 1
            kp = jnp.pad(k, ((0, 0), (0, 0), (pad, 0), (0, 0)))
            vp = jnp.pad(v, ((0, 0), (0, 0), (pad, 0), (0, 0)))
            scale = 1.0 / math.sqrt(Dh)

            def one_block(i):
                qs = i * block
                qb = jax.lax.dynamic_slice_in_dim(q, qs, block, axis=2)
                kb = jax.lax.dynamic_slice_in_dim(kp, qs, block + pad, axis=2)
                vb = jax.lax.dynamic_slice_in_dim(vp, qs, block + pad, axis=2)
                qpos = qs + jnp.arange(block)
                kpos = qs - pad + jnp.arange(block + pad)
                dist = qpos[:, None] - kpos[None, :]
                allowed = (dist >= 0) & (dist < WINDOW) & (kpos[None, :] >= 0)
                scores = jnp.einsum('bhqd,bhkd->bhqk', qb, kb) * scale
                scores = jnp.where(allowed[None, None], scores, -jnp.inf)
                attn = jax.nn.softmax(scores, axis=-1)
                return jnp.einsum('bhqk,bhkd->bhqd', attn, vb)
            out = jax.vmap(one_block)(jnp.arange(nb))
            return out.transpose(1, 2, 0, 3, 4).reshape(B, H, S, Dh)
        B, S, D = x.shape
        H, Dh = (N_HEADS, HEAD_DIM)
        LH, LDh = (LATENT_HEADS, LATENT_HEAD_DIM)
        q = (x @ Wq + bq).reshape(B, S, H, Dh).transpose(0, 2, 1, 3)
        k = (x @ Wk + bk).reshape(B, S, H, Dh).transpose(0, 2, 1, 3)
        v = (x @ Wv + bv).reshape(B, S, H, Dh).transpose(0, 2, 1, 3)
        chunks = min(LATENT_TOKENS, S)
        chunk_size = -(-S // chunks)
        pad_len = chunks * chunk_size - S
        xp = jnp.pad(x, ((0, 0), (0, pad_len), (0, 0))) if pad_len > 0 else x
        pooled = xp.reshape(B, chunks, chunk_size, D).mean(axis=2)
        chunk_ids = jnp.arange(S) // chunk_size
        gk = (pooled @ Wrk + brk).reshape(B, chunks, LH, LDh).transpose(0, 2, 1, 3)
        gv = (pooled @ Wrv + brv).reshape(B, chunks, LH, LDh).transpose(0, 2, 1, 3)
        rq = (x @ Wrq + brq).reshape(B, S, LH, LDh).transpose(0, 2, 1, 3)
        local_out = _local_attention(q, k, v)
        scores = jnp.einsum('bhqd,bhld->bhql', rq, gk) / math.sqrt(LDh)
        causal_masked = jnp.arange(chunks)[None, :] >= chunk_ids[:, None]
        scores = jnp.where(causal_masked[None, None], -jnp.inf, scores)
        valid = chunk_ids > 0
        scores = jnp.where(valid[None, None, :, None], scores, 0.0)
        attn = jax.nn.softmax(scores, axis=-1) * valid[None, None, :, None].astype(scores.dtype)
        latent_out = jnp.einsum('bhql,bhld->bhqd', attn, gv)
        local_flat = local_out.transpose(0, 2, 1, 3).reshape(B, S, D)
        gate = jax.nn.sigmoid(jnp.concatenate([x, local_flat], axis=-1) @ Wg + bg)
        remote = latent_out.transpose(0, 2, 1, 3).reshape(B, S, LATENT_D) @ Wro + bro
        fused = gate * local_flat + (1.0 - gate) * remote
        return fused @ Wo + bo

    def _L1_ffn_ref(x, ln_g, ln_b, Wq, Wk, Wv, Wo, qn_g, kn_g, gate_W, gate_b, W1, b1, W2, b2):
        import jax, jax.numpy as jnp
        import numpy as np
        B, N, DIM = (1, 512, 128)
        DH, H = (64, 8)
        E, FF = (8, 512)

        def _layernorm(x, g, b, eps=1e-05):
            mu = jnp.mean(x, axis=-1, keepdims=True)
            var = jnp.mean(jnp.square(x - mu), axis=-1, keepdims=True)
            return (x - mu) * jax.lax.rsqrt(var + eps) * g + b

        def _l2norm(x, eps=1e-12):
            return x / jnp.sqrt(jnp.sum(jnp.square(x), axis=-1, keepdims=True) + eps)
        b, n, d = x.shape
        dh = qn_g.shape[0]
        h = d // dh
        hx = _layernorm(x, ln_g, ln_b)
        q = (hx @ Wq).reshape(b, n, h, dh).transpose(0, 2, 1, 3)
        k = (hx @ Wk).reshape(b, n, h, dh).transpose(0, 2, 1, 3)
        v = (hx @ Wv).reshape(b, n, h, dh).transpose(0, 2, 1, 3)
        scale = jnp.sqrt(jnp.float32(dh))
        q = _l2norm(q) * scale * qn_g
        k = _l2norm(k) * scale * kn_g
        scores = jnp.einsum('bhqd,bhkd->bhqk', q, k) * dh ** (-0.5)
        causal = jnp.tril(jnp.ones((n, n), bool))
        scores = jnp.where(causal, scores, jnp.finfo(scores.dtype).min)
        attn = jax.nn.softmax(scores, axis=-1)
        o = jnp.einsum('bhqk,bhkd->bhqd', attn, v)
        y = o.transpose(0, 2, 1, 3).reshape(b, n, d) @ Wo
        gate = jax.nn.softmax(y @ gate_W + gate_b, axis=-1)
        hid = jax.nn.gelu(jnp.einsum('bnd,edf->bnef', y, W1) + b1)
        eo = jnp.einsum('bnef,efd->bned', hid, W2) + b2
        out = jnp.einsum('bned,bne->bnd', eo, gate)
        return out
    h = _L0_tok_ref(x, itok_BS_0_1439, fside_BS_durations, itok_BS_0_7, L0_tok_W_weekday, L0_tok_W_hour, L0_tok_W_dur, L0_tok_W_tdiff, L0_tok_dur_boundaries, L0_tok_proj_w, L0_tok_proj_b, L0_tok_ln_w, L0_tok_ln_b)
    h = h + _L0_attn_ref(_layernorm(h, axis=-1), L0_attn_Wq, L0_attn_Wkv, L0_attn_Wo, L0_attn_bo, L0_attn_rel_emb)
    h = h + _L0_ffn_ref(_layernorm(h, axis=-1), L0_ffn_Wg, L0_ffn_W1, L0_ffn_b1, L0_ffn_W2, L0_ffn_b2, L0_ffn_gamma, L0_ffn_beta)
    h = h + _L1_attn_ref(_layernorm(h, axis=-1), L1_attn_Wq, L1_attn_bq, L1_attn_Wk, L1_attn_bk, L1_attn_Wv, L1_attn_bv, L1_attn_Wrq, L1_attn_brq, L1_attn_Wrk, L1_attn_brk, L1_attn_Wrv, L1_attn_brv, L1_attn_Wro, L1_attn_bro, L1_attn_Wo, L1_attn_bo, L1_attn_Wg, L1_attn_bg)
    h = h + _L1_ffn_ref(_layernorm(h, axis=-1), L1_ffn_ln_g, L1_ffn_ln_b, L1_ffn_Wq, L1_ffn_Wk, L1_ffn_Wv, L1_ffn_Wo, L1_ffn_qn_g, L1_ffn_kn_g, L1_ffn_gate_W, L1_ffn_gate_b, L1_ffn_W1, L1_ffn_b1, L1_ffn_W2, L1_ffn_b2)
    return h

_drawn_inputs = setup_inputs


def setup_inputs(seed=0):
    import zlib

    import numpy as np

    out = dict(_drawn_inputs(seed))
    spreads = {'L0_tok_ln_w': (1.0, 0.2),
     'L0_tok_ln_b': (0.0, 0.1),
     'L0_ffn_gamma': (1.0, 0.2),
     'L0_ffn_beta': (0.0, 0.1),
     'L1_ffn_ln_g': (1.0, 0.6),
     'L1_ffn_ln_b': (0.0, 0.8),
     'L1_ffn_qn_g': (1.0, 0.6),
     'L1_ffn_kn_g': (1.0, 0.6),
     'L1_ffn_gate_b': (0.0, 0.8),
     'L1_ffn_b1': (0.0, 0.8),
     'L1_ffn_b2': (0.0, 1.566)}
    factors = {'L0_attn_rel_emb': 3.758,
     'L1_attn_bq': 38.671,
     'L1_attn_bk': 64.0,
     'L1_attn_bv': 8.0,
     'L1_attn_brq': 64.0,
     'L1_attn_brk': 64.0,
     'L1_attn_brv': 8.0,
     'L1_attn_bro': 8.0,
     'L1_attn_bo': 8.0,
     'L1_ffn_Wq': 8.0,
     'L1_ffn_Wk': 8.0,
     'L1_ffn_Wv': 8.0,
     'L1_ffn_Wo': 8.0,
     'L1_ffn_gate_W': 8.0,
     'L1_ffn_W1': 8.0,
     'L1_ffn_W2': 8.0}
    for name, (base, spread) in spreads.items():
        noise = np.random.default_rng([zlib.crc32(name.encode()), seed]).standard_normal(out[name].shape)
        drawn = base * np.exp(spread * noise) if base else spread * noise
        out[name] = jnp.asarray(drawn.astype(out[name].dtype))
    for name, factor in factors.items():
        out[name] = (out[name] * factor).astype(out[name].dtype)
    return out
```

```python
from contextlib import ExitStack

import numpy as np

import concourse.bass as bass
from concourse import mybir

F32 = mybir.dt.float32
I32 = mybir.dt.int32
BF16 = mybir.dt.bfloat16
ALU = mybir.AluOpType
ACT = mybir.ActivationFunctionType
AX = mybir.AxisListType

P = 128
NB = 16
NG, GB = 4, 4
BANK = 512
EPS = 1e-5
WEEK, HOUR, DUR, DIFF = (0, 7), (7, 24), (31, 10), (41, 8)
NF = 52
MINUTES = 1440.0
ROUND = 12582912.0
H0, D0 = 8, 64
NT0 = H0 * D0 // P
NREL = 257
E0 = 8
H1, D1 = 8, 16
LH, LD, CH = 4, 16, 64
H2, D2 = 2, 64
E2, FF = 8, 512
NC2 = FF // P


def bounds_by_column():
    lo, hi = np.zeros(49, np.float32), np.zeros(49, np.float32)
    for first, n in (WEEK, DIFF):
        lo[first:first + n] = np.arange(n) - 0.5
        hi[first:first + n] = np.arange(n) + 0.5
    first, n = HOUR
    lo[first:first + n] = 60.0 * np.arange(n) - 0.5
    hi[first:first + n] = 60.0 * np.arange(n) + 59.5
    lo[first], hi[first + n - 1] = -3e38, 3e38
    return lo, hi


def build(nc, d, out):
    ctx = ExitStack()
    with ctx:
        def sb(name, shape, dt=F32):
            return ctx.enter_context(nc.sbuf_tensor(name, shape, dt))

        sems = {}

        def sem(*names):
            for name in names:
                sems[name] = ctx.enter_context(nc.semaphore(name))

        psum = ctx.enter_context(nc.psum_tensor("psum", [P, 8, BANK], F32))
        bank = [psum[:, i, :] for i in range(8)]

        arena = sb("arena", [P, 11024])
        used = {"att0": 0, "att1": 0}

        def carve(part, shape):
            n = int(np.prod(shape))
            view = arena[:, used[part]:used[part] + n]
            used[part] += n
            names = "abcd"[:len(shape)]
            assert used[part] <= 11024
            return view.rearrange(f"p ({' '.join(names)}) -> p {' '.join(names)}", **dict(zip(names, shape))) if len(shape) > 1 else view

        ident = sb("ident", [P, P])
        ids = sb("ids", [NB, 3, P], I32)
        dur = sb("dur", [NB, P])
        tab_l = sb("tab_l", [43, NF])
        tab_r = sb("tab_r", [43, P])
        table = sb("table", [NF, P])
        valT = sb("valT", [P, 6, NB])
        onehot = sb("onehot", [P, 2, NF])
        onehotT = sb("onehotT", [NF, 2, P])
        minus_half = sb("minus_half", [P, 8])
        eps = sb("eps", [P, 8])
        h = sb("h", [P, NB, P])
        xT_all = sb("xT_all", [P, NB, P])
        stats = sb("stats", [P, 2, 6])
        mv = sb("mv", [P, 2, 2])
        var_eps = sb("var_eps", [P, 2, 1])
        rstd = sb("rstd", [P, 2, 1])
        tok_st = sb("tok_st", [P, 2, 6])
        tok_mv = sb("tok_mv", [P, 2, 2])
        tok_rstd = sb("tok_rstd", [P, 2, 1])
        xhat = sb("xhat", [P, 2, P])
        wq0 = sb("wq0", [P, H0 * D0])
        wkv0 = sb("wkv0", [P, 2 * H0 * D0])
        wo0 = sb("wo0", [P, NT0, P])
        bo0 = sb("bo0", [P, P])
        relT = sb("relT", [P, NREL])
        relw = sb("relw", [P, 2, P + 7])
        big = sb("big", [P, NB * H0 * P + NB * NT0 * P])
        posT = big[:, 0:NB * H0 * P].rearrange("p (b h n) -> p b h n", b=NB, h=H0)
        qT_all = big[:, NB * H0 * P:].rearrange("p (t b n) -> p t b n", t=NT0, b=NB)
        qTs = carve("att0", [2, NT0, P])
        posTs = carve("att0", [2, H0, P])
        xTs = carve("att0", [2, P])
        kTs = carve("att0", [2, NT0, P])
        vs = sb("vs", [P, 2, H0, D0 + 1])
        negmax = carve("att0", [2, 2, NT0])
        probs = carve("att0", [2, 2, NT0, P])
        probsT = carve("att0", [2, 2, NT0, P])
        rsum = carve("att0", [2, 2, NT0])
        o0 = carve("att0", [2, H0 * D0])
        oT0 = carve("att0", [2, NT0, P])

        qn = arena[:, 0:2048 // 2].rearrange("p (v i c) -> p v i c", v=2, i=8)
        val = arena[0:NB, 1024:1792].rearrange("p (f n) -> p f n", f=6)
        tmp = arena[0:NB, 1792:2560].rearrange("p (f n) -> p f n", f=6)
        ln0 = arena[:, 2816:3072].rearrange("p (k n) -> p k n", k=2)
        lohi = arena[:, 3072:3170].rearrange("p (k n) -> p k n", k=2)
        tokx = arena[:, 2560:2816].rearrange("p (v n) -> p v n", v=2)
        above = arena[:, 8192:8192 + NB * NF].rearrange("p (b f) -> p b f", b=NB)
        upto = arena[:, 9216:9216 + NB * NF].rearrange("p (b f) -> p b f", b=NB)
        ysum = arena[:, 9400:9656].rearrange("p (v n) -> p v n", v=2)
        glog = arena[:, 9660:9788].rearrange("p (b e) -> p b e", b=NB)
        g2 = arena[:, 9792:9920].rearrange("p (b e) -> p b e", b=NB)
        top = arena[:, 9984:10496].rearrange("p (k b e) -> p k b e", k=4, b=NB)
        acc = arena[:, 10512:11024].rearrange("p (b n) -> p b n", b=GB)
        w1m = sb("w1m", [P, E0, P])
        w2m = sb("w2m", [P, E0, P])
        b2m = sb("b2m", [P, E0, P])
        gamma = sb("gamma", [P, E0, P])
        beta = sb("beta", [E0, P])
        b1m = sb("b1m", [P, E0])
        wgm = sb("wgm", [P, E0])
        centre = sb("centre", [P, 2, E0])
        iota = sb("iota", [P, E0])
        lgT = big[0:E0, 12288:14336]
        lg = sb("lg", [P, NB, E0])
        tops = sb("tops", [P, 6, NB])
        gates = sb("gates", [P, NB, E0])
        gT = big[0:E0, 4096:6144]
        hid = big[:, 0:2 * E0 * 2 * P].rearrange("p (v e n) -> p v e n", v=2, e=E0)
        work = big[:, 8192:]
        ym = work[:, 0:2048].rearrange("p (v e n) -> p v e n", v=2, e=E0)
        ysq = work[:, 2048:4096].rearrange("p (v e n) -> p v e n", v=2, e=E0)
        yg = work[:, 4096:6144].rearrange("p (v e n) -> p v e n", v=2, e=E0)
        yc = work[:, 6144:8192].rearrange("p (v e n) -> p v e n", v=2, e=E0)
        ysum2 = sb("ysum2", [P, 2, E0])
        yvar = sb("yvar", [P, 2, E0])
        yrstd = sb("yrstd", [P, 2, E0])
        ycoef = sb("ycoef", [P, 2, E0])
        LAT = LH * CH
        wqk1 = sb("wqk1", [P, 4, P])
        wv1 = sb("wv1", [P, P + 1])
        wrv1 = sb("wrv1", [P, LH * LD])
        b1a = sb("b1a", [P, 4])
        qscale = sb("qscale", [P, 3])
        qbias = sb("qbias", [P, 3])
        bv1 = sb("bv1", [P, P])
        brv1 = sb("brv1", [P, LH * LD])
        wg1 = sb("wg1", [P, P])
        nbg1 = sb("nbg1", [P, 1])
        valid = sb("valid", [P, 1])
        wroT = sb("wroT", [P, LH * LD + 1])
        wo1 = sb("wo1", [P, P])
        wro1 = sb("wro1", [LH * LD + 1, P])
        bo1 = sb("bo1", [P, P])
        identb = sb("identb", [P, P], BF16)
        maskb = sb("maskb", [P, 2 * P + CH], BF16)
        xT1 = carve("att1", [2, P])
        pool1 = carve("att1", [2, 2, CH])
        qT1 = carve("att1", [2, 2, P])
        kT1 = carve("att1", [2, P])
        rqT1 = carve("att1", [2, P])
        gkT1 = carve("att1", [2, CH])
        v1 = sb("v1", [P, 2, H1, D1 + 1])
        gv1 = sb("gv1", [P, 2, 2, 2, LD + 1])
        gx1 = carve("att1", [2, 1])
        max1 = carve("att1", [2, H1 + LH])
        e1 = big[:, 4096:6656].rearrange("p (v n) -> p v n", v=2)
        pT1 = big[:, 6656:9216].rearrange("p (v n) -> p v n", v=2)
        sum1 = carve("att1", [2, H1 + LH])
        loc1 = carve("att1", [2, P])
        lat1 = carve("att1", [2, LH * LD])
        gw1 = carve("att1", [2, P])
        gd1 = carve("att1", [2, 4])
        cat1 = carve("att1", [2, P + LH * LD + 1])
        catT1 = carve("att1", [2, 2, P])
        wqkv2 = sb("wqkv2", [P, 3 * P])
        wo2 = sb("wo2", [P, P])
        col2 = sb("col2", [P, 4])
        gw2 = sb("gw2", [P, E2])
        gb2 = sb("gb2", [P, E2])
        b1f = sb("b1f", [P, E2, NC2])
        b2f = sb("b2f", [E2, P])
        w1f = big[:, 16384:20480].rearrange("p (e n) -> p e n", e=E2)
        w2f = big[:, 20480:24576].rearrange("p (e f n) -> p e f n", e=E2, f=NC2)
        xT2 = carve("att1", [2, P])
        sq2 = carve("att1", [2, 2 * P])
        ss2 = carve("att1", [2, 2 * H2])
        rn2 = carve("att1", [2, 2 * H2])
        qk2 = carve("att1", [2, 2 * P])
        v2 = sb("v2", [P, 2, H2, D2 + 1])
        qkT2 = carve("att1", [2, 2, P])
        max2 = carve("att1", [2, H2])
        p2 = carve("att1", [2, H2, P])
        pT2 = carve("att1", [2, H2, P])
        sum2 = carve("att1", [2, H2])
        o2 = carve("att1", [2, P])
        oT2 = carve("att1", [2, P])
        yT2 = carve("att1", [2, P])
        yT_all = xT_all
        gsum = sb("gsum", [P, 2, NB])
        g2T = big[0:E2, 12288:14336]
        hidf = big[:, 0:4096].rearrange("p (v f n) -> p v f n", v=2, f=NC2)

        sem("ld_moe0", "ld_att1", "ld_att2", "ld_moe1", "centred", "lgT_psum", "lgT", "lg_psum", "tops",
            "topexp", "gates", "gT_psum", "gT", "beta_psum", "h_beta", "hid_psum", "hid", "y_psum", "ym", "ysq", "yvar",
            "yrstd", "ycoef", "yg", "yc", "ysum", "h_moe0", "ready1", "wro_psum", "wro1", "xT1", "pool1", "proj1_psum",
            "v1_psum", "k1", "v1", "s1_psum", "max1", "sub1", "e1", "pT1_psum", "latT_psum", "pT1", "latT1", "o1_psum",
            "rsum1", "o1", "gd1", "ge1", "gate1a", "gate1b", "gate1c", "gate1", "cat1", "catT1_psum", "catT1", "y1_psum",
            "y1_added", "h1")
        sem("xT2", "qkv2_psum", "sq2", "ss2", "ss2e", "rn2", "qk2", "qkT2_psum", "qkT2", "s2_psum", "max2", "p2",
            "pT2_psum", "pT2", "o2_psum", "rsum2", "o2", "oT2_psum", "oT2", "yT2_psum", "yT2", "yT_all", "gl2_psum",
            "gl2", "act4", "chain4", "g2", "g2T_psum", "g2T", "b2_psum", "acc0", "hf_psum", "hf", "eo_psum", "acc",
            "out_acc")
        sem("ld_tok", "ld_const", "ld_att0", "chain", "trig_in", "log_in", "trig", "log", "val_ready", "valT_psum",
            "table_psum", "table_ready", "onehot", "onehotT_psum", "onehotT", "tok_psum", "tok_stats", "tok_mv",
            "tok_var", "tok_rstd", "tok_xhat", "tok_scaled", "tok_h", "const_ready", "vs_ones", "ln_stats", "ln_mv",
            "ln_var", "ln_rstd", "ln_xhat", "ln_xT_psum", "ln_xT", "q_psum", "q_all", "relw", "qn", "pos_psum",
            "pos_even", "pos_odd", "att0_in0", "att0_in1", "k0_psum", "k0", "v0_psum", "v0", "s0_psum", "negmax0", "p0",
            "pT0_psum", "pT0", "o0_psum", "rsum0", "o0", "oT0_psum", "oT0", "y0_psum", "y0_added", "h0", "stored",
            "waited_pe", "waited_dve")
        g = sems

        def steps(eng, lag, step, n=NB):
            first = (lag + 3) // 2
            for t in range(2 * first):
                step(t, t // 2, t % 2)
            with eng.Fori(first, n // 2) as j:
                for u in range(2):
                    step(2 * j + u, j, u)
            for t in range(n, n + lag):
                step(t, t // 2, t % 2)

        def live(t, k, n=NB):
            return not isinstance(t, int) or 0 <= t - k < n

        def later(b, n):
            return not isinstance(b, int) or b >= n

        def apart(eng):
            eng.sem_inc(g["waited_" + ("pe" if eng is nc.tensor else "dve")], 1)

        with nc.Block() as block:

            @block.sync
            def _(sp):
                for i, name in enumerate(("x", "itok_BS_0_1439", "itok_BS_0_7")):
                    sp.dma_start(ids[:, i, :], d[name]).then_inc(g["ld_tok"], 16)
                sp.dma_start(dur[:], d["fside_BS_durations"]).then_inc(g["ld_tok"], 16)
                sp.dma_start(ident[:], d["ident"]).then_inc(g["ld_const"], 16)
                sp.dma_start(lohi.rearrange("p a b -> p (a b)"), d["bounds"].partition_broadcast(P)).then_inc(g["ld_const"], 16)
                sp.dma_start(tab_l[:], d["tab_l"]).then_inc(g["ld_const"], 16)
                sp.dma_start(tab_r[:], d["tab_r"]).then_inc(g["ld_const"], 16)
                sp.dma_start(ln0[:, 0, :], d["L0_tok_ln_w"].partition_broadcast(P)).then_inc(g["ld_const"], 16)
                sp.dma_start(ln0[:, 1, :], d["L0_tok_ln_b"].partition_broadcast(P)).then_inc(g["ld_const"], 16)
                sp.dma_start(wq0[:], d["L0_attn_Wq"]).then_inc(g["ld_att0"], 16)
                sp.dma_start(relT[:], d["relT"]).then_inc(g["ld_att0"], 16)
                sp.dma_start(wkv0[:], d["L0_attn_Wkv"]).then_inc(g["ld_att0"], 16)
                sp.dma_start(wo0[:], d["L0_attn_Wo"].rearrange("(t p) n -> p t n", p=P)).then_inc(g["ld_att0"], 16)
                sp.dma_start(bo0[:], d["L0_attn_bo"].partition_broadcast(P)).then_inc(g["ld_att0"], 16)

                for dst, name in ((w1m[:], "w1m"), (w2m[:], "w2m"), (b2m[:].rearrange("p e n -> p (e n)"), "L0_ffn_b2"),
                                  (gamma[:].rearrange("p e n -> p (e n)"), "L0_ffn_gamma"), (beta[:], "L0_ffn_beta"), (b1m[:], "b1m"),
                                  (wgm[:], "L0_ffn_Wg"), (iota[:], "iota")):
                    src = d[name].partition_broadcast(P) if name in ("L0_ffn_b2", "L0_ffn_gamma", "iota") else d[name]
                    sp.dma_start(dst, src).then_inc(g["ld_moe0"], 16)
                for dst, name in ((wqk1[:], "wqk1"), (wv1[:], "wv1"), (wrv1[:], "L1_attn_Wrv"), (b1a[:], "b1a"), (qscale[:], "qscale"),
                                  (bv1[:], "L1_attn_bv"), (brv1[:], "L1_attn_brv"), (wg1[:], "wg1"), (nbg1[:], "L1_attn_bg"),
                                  (valid[:], "valid"), (wroT[:], "wroT"), (wo1[:], "L1_attn_Wo"), (bo1[:], "L1_attn_bo"),
                                  (identb[:], "identb"), (maskb[:], "maskb")):
                    src = d[name].partition_broadcast(P) if name in ("L1_attn_bv", "L1_attn_brv", "wg1", "L1_attn_bg", "L1_attn_bo") else d[name]
                    sp.dma_start(dst, src).then_inc(g["ld_att1"], 16)
                for dst, name in ((wqkv2[:], "wqkv2"), (wo2[:], "L1_ffn_Wo"), (col2[:], "col2"), (gw2[:], "L1_ffn_gate_W"),
                                  (gb2[:], "L1_ffn_gate_b")):
                    src = d[name].partition_broadcast(P) if name == "L1_ffn_gate_b" else d[name]
                    sp.dma_start(dst, src).then_inc(g["ld_att2"], 16)

                sp.wait_ge(g["pos_even"], NB)
                sp.wait_ge(g["pos_odd"], NB)

                def step(t, j, u):
                    if live(t, 0):
                        if later(t, 2):
                            sp.wait_ge(g["s0_psum"], t - 1)
                            sp.wait_ge(g["v0_psum"], t - 1)
                        arrived = g[f"att0_in{u}"]
                        sp.dma_start(xTs[:, u, :], xT_all[:, t, :]).then_inc(arrived, 16)
                        sp.dma_start(qTs[:, u], qT_all[:, :, t, :]).then_inc(arrived, 16)
                        sp.dma_start(posTs[:, u], posT[:, t]).then_inc(arrived, 16)
                steps(sp, 0, step)

                sp.wait_ge(g["s0_psum"], NB)
                for dst, name in ((b1f[:], "b1f"), (b2f[:], "L1_ffn_b2"), (w1f, "w1f"), (w2f, "w2f")):
                    sp.dma_start(dst, d[name]).then_inc(g["ld_moe1"], 16)

                sp.wait_ge(g["ld_moe1"], 64)
                sp.wait_ge(g["ld_att1"], 240)
                sp.wait_ge(g["ld_att2"], 80)

                def store(grp):
                    sp.wait_ge(g["out_acc"], grp + 1)
                    sp.dma_start(out[bass.ds(GB * grp, GB)].rearrange("b p n -> p b n"), acc[:]).then_inc(g["stored"], 16)
                store(0)
                with sp.Fori(1, NG) as grp:
                    store(grp)
                sp.wait_ge(g["stored"], 16 * NG)

            @block.gpsimd
            def _(pool):
                pool.memset(minus_half[:], -0.5).then_inc(g["const_ready"], 1)
                pool.memset(eps[:, 0:1], EPS)
                pool.memset(eps[:, 1:2], 1.0 + EPS)
                pool.memset(eps[:, 2:3], EPS * EPS)
                pool.memset(eps[:, 4:8], 1e-12).then_inc(g["const_ready"], 1)
                pool.memset(v1[:, :, :, D1:D1 + 1], 1.0)
                pool.memset(v2[:, :, :, D2:D2 + 1], 1.0)
                pool.memset(gv1[:], 0.0).then_inc(g["vs_ones"], 1)
                pool.memset(above[:, :, 51:52], 1.0).then_inc(g["const_ready"], 1)
                pool.memset(upto[:, :, 49:52], 1.0).then_inc(g["const_ready"], 1)
                pool.memset(vs[:, :, :, D0:D0 + 1], 1.0).then_inc(g["vs_ones"], 1)
                for odd in range(2):
                    pool.wait_ge(g["vs_ones"], 2 + odd)
                    pool.memset(gv1[CH * odd:CH * odd + CH, :, :, odd, LD:LD + 1], 1.0).then_inc(g["vs_ones"], 1)
                pool.wait_ge(g["vs_ones"], 4)
                pool.wait_ge(g["const_ready"], 4)

                def tok_rstd_of(b, v):
                    pool.wait_ge(g["tok_mv"], b + 1)
                    pool.tensor_tensor(tok_rstd[:, v], tok_mv[:, v, 1:2], eps[:, 0:1], ALU.add).then_inc(g["tok_var"], 1)
                    pool.wait_ge(g["tok_var"], b + 1)
                    pool.tensor_tensor(tok_rstd[:, v], tok_rstd[:, v], minus_half[:, 0:1], ALU.pow).then_inc(g["tok_rstd"], 1)

                def ln_rstd(phase, b, v):
                    n = NB * phase + b + 1
                    pool.wait_ge(g["ln_mv"], n)
                    pool.tensor_tensor(var_eps[:, v], mv[:, v, 1:2], eps[:, 0:1], ALU.add).then_inc(g["ln_var"], 1)
                    pool.wait_ge(g["ln_var"], n)
                    pool.tensor_tensor(rstd[:, v], var_eps[:, v], minus_half[:, 0:1], ALU.pow).then_inc(g["ln_rstd"], 1)

                def tok(t, j, u):
                    if live(t, 1):
                        tok_rstd_of(t - 1, 1 - u)
                    if live(t, 2):
                        ln_rstd(0, t - 2, u)
                steps(pool, 4, tok)

                pool.wait_ge(g["q_all"], NB)
                def copy_q(c, u):
                    if later(c, 2):
                        pool.wait_ge(g["pos_psum"], c - 1)
                    pool.tensor_copy(relw[:, u, :], relT[:, bass.ds(P - 7 - 8 * c, P + 7)]).then_inc(g["relw"], 1)
                    pool.tensor_copy(qn[:, u].rearrange("p i c -> p c i"),
                                     big[:, NB * H0 * P:].rearrange("p (c n) -> p c n", n=P)[:, :, bass.ds(8 * c, 8)]).then_inc(g["qn"], 1)
                for c in range(2):
                    copy_q(c, c)
                with pool.Fori(1, NB // 2) as j:
                    for u in range(2):
                        copy_q(2 * j + u, u)

                def att0(t, j, u):
                    if live(t, 3):
                        ln_rstd(1, t - 3, 1 - u)
                steps(pool, 4, att0)

                def moe0(t, j, u):
                    if live(t, 1):
                        b, v = t - 1, 1 - u
                        pool.wait_ge(g["yvar"], b + 1)
                        if later(b, 2):
                            pool.wait_ge(g["ycoef"], b - 1)
                        pool.tensor_tensor(yrstd[:, v], yvar[:, v], minus_half[:], ALU.pow).then_inc(g["yrstd"], 1)
                    if live(t, 0):
                        pool.wait_ge(g["ym"], t + 1)
                        if later(t, 2):
                            pool.wait_ge(g["yc"], t - 1)
                        pool.tensor_tensor(yg[:, u], ym[:, u], gamma[:], ALU.mult).then_inc(g["yg"], 1)
                steps(pool, 1, moe0)

                def att1(t, j, u):
                    if live(t, 0):
                        ln_rstd(2, t, u)
                steps(pool, 4, att1)

                def att2(t, j, u):
                    if live(t, 0):
                        n = 3 * NB + t + 1
                        pool.wait_ge(g["ln_mv"], n)
                        pool.tensor_tensor(var_eps[:, u], mv[:, u, 1:2], eps[:, 1:2], ALU.mult).then_inc(g["ln_var"], 1)
                        pool.wait_ge(g["ln_var"], 3 * NB + 2 * t + 1)
                        pool.tensor_tensor(var_eps[:, u], var_eps[:, u], eps[:, 2:3], ALU.add).then_inc(g["ln_var"], 1)
                        pool.wait_ge(g["ln_var"], 3 * NB + 2 * t + 2)
                        pool.tensor_tensor(rstd[:, u], var_eps[:, u], minus_half[:, 0:1], ALU.pow).then_inc(g["ln_rstd"], 1)
                    if live(t, 1):
                        v, n = 1 - u, t
                        pool.wait_ge(g["ss2"], n)
                        pool.tensor_tensor(rn2[:, v], ss2[:, v], eps[:, 4:8], ALU.add).then_inc(g["ss2e"], 1)
                        pool.wait_ge(g["ss2e"], n)
                        pool.tensor_tensor(rn2[:, v], rn2[:, v], minus_half[:, 0:4], ALU.pow).then_inc(g["rn2"], 1)
                steps(pool, 4, att2)

            @block.scalar
            def _(act):
                act.wait_ge(g["log_in"], 1)
                act.activation(tmp[:, 1, :], tmp[:, 0, :], ACT.Ln).then_inc(g["log"], 1)
                act.wait_ge(g["trig_in"], 1)
                act.activation(val[:, 4:6, :], tmp[:, 4:6, :], ACT.Sin).then_inc(g["trig"], 1)
                act.wait_ge(g["table_psum"], 1)
                act.activation(table[:], bank[1][0:NF, 0:P], ACT.Copy).then_inc(g["table_ready"], 1)

                def tok(t, j, u):
                    if live(t, 0):
                        act.wait_ge(g["onehotT_psum"], t + 1)
                        if later(t, 2):
                            act.wait_ge(g["tok_psum"], t - 1)
                        act.activation(onehotT[:, u, :], bank[u][0:NF, 0:P], ACT.Copy).then_inc(g["onehotT"], 1)
                    if live(t, 3):
                        b = t - 3
                        act.wait_ge(g["ln_xT_psum"], b + 1)
                        act.activation(xT_all[:, b, :], bank[5 - u][:, 0:P], ACT.Copy).then_inc(g["ln_xT"], 1)
                    if live(t, 4):
                        b = t - 4
                        act.wait_ge(g["q_psum"], b + 1)
                        act.activation(qT_all[:, :, b, :], bank[6 + u].rearrange("p (t n) -> p t n", t=NT0), ACT.Copy,
                                       scale=float(D0) ** -0.5).then_inc(g["q_all"], 1)
                steps(act, 4, tok)

                def pos(c, u):
                    act.wait_ge(g["pos_psum"], c + 1)
                    act.activation(posT[:, :, 0:H0:2, bass.ds(8 * c, 8)],
                                   bank[2 * u].rearrange("p (i t b) -> p b t i", i=8, t=NT0), ACT.Copy).then_inc(g["pos_even"], 1)
                for c in range(2):
                    pos(c, c)
                with act.Fori(1, NB // 2) as j:
                    for u in range(2):
                        pos(2 * j + u, u)

                def att0(t, j, u):
                    if live(t, 3):
                        b, v = t - 3, 1 - u
                        act.wait_ge(g["oT0_psum"], b + 1)
                        if later(b, 2):
                            act.wait_ge(g["y0_psum"], b - 1)
                        act.activation(oT0[:, v], bank[0].rearrange("p (t n) -> p t n", t=NT0), ACT.Copy).then_inc(g["oT0"], 1)
                    if live(t, 1):
                        b, v = t - 1, 1 - u
                        act.wait_ge(g["negmax0"], b + 1)
                        if later(b, 2):
                            act.wait_ge(g["pT0_psum"], b - 1)
                        for odd in range(2):
                            for tile in range(NT0):
                                e = act.activation(probs[:, v, odd, tile, :], bank[2 + odd][:, tile * P:(tile + 1) * P],
                                                   ACT.Exp, bias=negmax[:, v, odd, tile:tile + 1])
                        e.then_inc(g["p0"], 1)
                    if live(t, 4):
                        b = t - 4
                        act.wait_ge(g["ln_xT_psum"], NB + b + 1)
                        act.activation(xT_all[:, b, :], bank[7][:, 3 * P:], ACT.Copy).then_inc(g["ln_xT"], 1)
                    if live(t, 0):
                        act.wait_ge(g["k0_psum"], t + 1)
                        if later(t, 2):
                            act.wait_ge(g["s0_psum"], t - 1)
                        act.activation(kTs[:, u], bank[0].rearrange("p (t n) -> p t n", t=NT0), ACT.Copy).then_inc(g["k0"], 1)
                steps(act, 4, att0)

                act.wait_ge(g["lgT_psum"], 1)
                act.activation(lgT.rearrange("p (a n) -> p a n", a=NG), psum[0:E0, 2:6, :], ACT.Copy).then_inc(g["lgT"], 1)
                act.wait_ge(g["tops"], 1)
                act.activation(tops[:, 4, :], tops[:, 3, :], ACT.Exp).then_inc(g["topexp"], 1)
                act.wait_ge(g["ld_moe0"], 128)

                def moe0(t, j, u):
                    for half in range(2):
                        if live(t, 0, NB // 2):
                            for pair in (2 * half, 2 * half + 1):
                                act.wait_ge(g["hid_psum"], 4 * t + pair + 1)
                                if pair == 0 and later(t, 2):
                                    act.wait_ge(g["y_psum"], 2 * t - 2)
                                for e in (2 * pair, 2 * pair + 1):
                                    last = act.activation(hid[:, u, e, :], bank[pair % 2][:, e % 2 * 2 * P:(e % 2 + 1) * 2 * P], ACT.Relu,
                                                          bias=b1m[:, e:e + 1])
                                last.then_inc(g["hid"], 1)
                        if live(t, 1, NB // 2):
                            b = 2 * t - 2 + half
                            act.wait_ge(g["ym"], b + 1)
                            if later(t, 2):
                                act.wait_ge(g["yvar"], b - 1)
                            for e in range(E0):
                                last = act.activation(ysq[:, half, e], ym[:, half, e], ACT.Square, accum_out=ysum2[:, half, e:e + 1])
                            last.then_inc(g["ysq"], 1)
                steps(act, 1, moe0, NB // 2)
                act.wait_ge(g["gT_psum"], 1)
                for a in range(NG):
                    last = act.activation(gT[:, a * GB * P:(a + 1) * GB * P], bank[(0, 1, 6, 7)[a]][0:E0, :], ACT.Copy)
                last.then_inc(g["gT"], 1)

                act.wait_ge(g["ready1"], 1)
                act.wait_ge(g["wro_psum"], 1)
                act.activation(wro1[:], bank[0][0:LH * LD + 1, 0:P], ACT.Copy).then_inc(g["wro1"], 1)

                def att1(t, j, u):
                    if live(t, 4):
                        b, v = t - 4, u
                        act.wait_ge(g["catT1_psum"], b + 1)
                        if later(b, 2):
                            act.wait_ge(g["y1_psum"], b - 1)
                        act.activation(catT1[:, v, 0, :], bank[0][:, 0:P], ACT.Copy)
                        act.activation(catT1[0:LH * LD + 1, v, 1, :], bank[0][0:LH * LD + 1, P:2 * P], ACT.Copy).then_inc(g["catT1"], 1)
                    if live(t, 3):
                        b, v = t - 3, 1 - u
                        act.wait_ge(g["pT1_psum"], b + 1)
                        if later(b, 2):
                            act.wait_ge(g["o1_psum"], b - 1)
                        act.activation(pT1[:, v, 0:H1 * P], psum[:, 6:8, :].rearrange("p a c -> p (a c)"), ACT.Copy).then_inc(g["pT1"], 1)
                        act.wait_ge(g["latT_psum"], b + 1)
                        if live(t, 0):
                            act.wait_ge(g["ln_xT_psum"], 2 * NB + t + 1)
                        act.activation(pT1[:, v, H1 * P:], bank[1][:, 0:LAT], ACT.Copy).then_inc(g["latT1"], 1)
                    if live(t, 0):
                        act.wait_ge(g["ln_xT_psum"], 2 * NB + t + 1)
                        if later(t, 2):
                            act.wait_ge(g["v1_psum"], t - 1)
                        act.activation(xT1[:, u, :], bank[1][:, LAT:LAT + P], ACT.Copy).then_inc(g["xT1"], 1)
                    if live(t, 1):
                        b, v = t - 1, 1 - u
                        act.wait_ge(g["proj1_psum"], b + 1)
                        if later(b, 2):
                            act.wait_ge(g["s1_psum"], b - 1)
                        for odd in range(2):
                            act.activation(qT1[:, v, odd, :], bank[0][:, 0:P], ACT.Identity, scale=qscale[:, odd:odd + 1], bias=qbias[:, odd:odd + 1])
                        act.activation(kT1[:, v, :], bank[0][:, P:2 * P], ACT.Identity, bias=b1a[:, 1:2])
                        act.activation(rqT1[:, v, :], bank[0][:, 2 * P:3 * P], ACT.Identity, scale=0.25, bias=qbias[:, 2:3])
                        act.activation(gkT1[:, v, :], bank[0][:, 3 * P:3 * P + CH], ACT.Identity, scale=0.5, bias=b1a[:, 3:4]).then_inc(g["k1"], 1)
                    if live(t, 2):
                        b, v = t - 2, u
                        act.wait_ge(g["sub1"], b + 1)
                        act.activation(e1[:, v, :], e1[:, v, :], ACT.Exp).then_inc(g["e1"], 1)
                    if live(t, 3):
                        b, v = t - 3, 1 - u
                        act.wait_ge(g["gd1"], b + 1)
                        act.activation(gd1[:, v, 1:2], gd1[:, v, 0:1], ACT.Exp, scale=-1.0, bias=nbg1[:]).then_inc(g["ge1"], 1)
                steps(act, 4, att1)

                def att2(t, j, u):
                    if live(t, 1):
                        b, v = t - 1, 1 - u
                        act.wait_ge(g["qkv2_psum"], b + 1)
                        if later(b, 2):
                            act.wait_ge(g["ss2"], b - 1)
                        act.activation(sq2[:, v, :], bank[0][:, 0:2 * P], ACT.Square).then_inc(g["sq2"], 1)
                    if live(t, 2):
                        b, v = t - 2, u
                        act.wait_ge(g["qkT2_psum"], b + 1)
                        if later(b, 2):
                            act.wait_ge(g["s2_psum"], b - 1)
                        for i in range(2):
                            last = act.activation(qkT2[:, v, i, :], bank[1][:, i * P:(i + 1) * P], ACT.Identity, scale=col2[:, 2 + i:3 + i])
                        last.then_inc(g["qkT2"], 1)
                    if live(t, 4):
                        b, v = t - 4, u
                        act.wait_ge(g["oT2_psum"], b + 1)
                        if later(b, 2):
                            act.wait_ge(g["yT2_psum"], b - 1)
                        act.activation(oT2[:, v, :], bank[6][:, 0:P], ACT.Copy).then_inc(g["oT2"], 1)
                        act.wait_ge(g["yT2_psum"], b + 1)
                        if later(b, 2):
                            act.wait_ge(g["gl2_psum"], b - 1)
                        act.activation(yT2[:, v, :], bank[6][:, 0:P], ACT.Copy).then_inc(g["yT2"], 1)
                        act.activation(yT_all[:, b, :], bank[6][:, 0:P], ACT.Copy).then_inc(g["yT_all"], 1)
                    if live(t, 0):
                        act.wait_ge(g["ln_xT_psum"], 3 * NB + t + 1)
                        if later(t, 2):
                            act.wait_ge(g["qkv2_psum"], t - 1)
                        act.activation(xT2[:, u, :], bank[7][:, 0:P], ACT.Identity, scale=col2[:, 0:1], bias=col2[:, 1:2]).then_inc(g["xT2"], 1)
                    if live(t, 2):
                        b, v = t - 2, u
                        act.wait_ge(g["max2"], b + 1)
                        if later(b, 2):
                            act.wait_ge(g["pT2_psum"], b - 1)
                        for hd in range(H2):
                            last = act.activation(p2[:, v, hd, :], bank[2 + hd][:, 0:P], ACT.Exp, bias=max2[:, v, hd:hd + 1])
                        last.then_inc(g["p2"], 1)
                steps(act, 4, att2)
                act.wait_ge(g["chain4"], 2)
                act.activation(g2, glog, ACT.Exp).then_inc(g["act4"], 1)
                act.wait_ge(g["g2T_psum"], 1)
                act.activation(g2T.rearrange("p (a n) -> p a n", a=NG), psum[0:E2, 2:6, :], ACT.Copy).then_inc(g["g2T"], 1)

                def hiddenf(grp):
                    for e in range(E2):
                        for f in range(NC2):
                            act.wait_ge(g["hf_psum"], FF // P * (E2 * grp + e) + f + 1)
                            if f == 0 and (e >= 2 or later(grp, 1)):
                                act.wait_ge(g["eo_psum"], E2 * grp + e - 1)
                            act.activation(hidf[:, e % 2, f, :], bank[f], ACT.Gelu_apprx_tanh, bias=b1f[:, e, f:f + 1]).then_inc(g["hf"], 1)
                hiddenf(0)
                with act.Fori(1, NG) as grp:
                    hiddenf(grp)

            @block.vector
            def _(dve):
                chained = [0]

                def link(ins):
                    chained[0] += 1
                    ins.then_inc(g["chain"], 1)
                    dve.wait_ge(g["chain"], chained[0])

                dve.wait_ge(g["ld_tok"], 64)
                link(dve.tensor_scalar(tmp[:, 2, :], dur[:], -1.0, None, ALU.max))
                link(dve.tensor_scalar(tmp[:, 3, :], tmp[:, 2, :], 1.0, None, ALU.add))
                dve.tensor_scalar(tmp[:, 0, :], tmp[:, 3, :], 2.0 ** -64, 2.0 ** 64, ALU.max, ALU.min).then_inc(g["log_in"], 1)
                dve.tensor_copy(val[:, 0:2, :], ids[:, 0:2, :])
                link(dve.tensor_copy(val[:, 3, :], ids[:, 2, :]))
                link(dve.tensor_scalar(tmp[:, 5, :], val[:, 1, :], 1.0 / MINUTES, ROUND, ALU.mult, ALU.add))
                link(dve.tensor_scalar(tmp[:, 5, :], tmp[:, 5, :], ROUND, -MINUTES, ALU.subtract, ALU.mult))
                link(dve.tensor_tensor(tmp[:, 5, :], tmp[:, 5, :], val[:, 1, :], ALU.add))
                link(dve.tensor_scalar(tmp[:, 5, :], tmp[:, 5, :], 2.0 * np.pi / MINUTES, None, ALU.mult))
                link(dve.tensor_scalar(tmp[:, 4, :], tmp[:, 5, :], 3.1415925, -3.1415925, ALU.min, ALU.max))
                link(dve.scalar_tensor_tensor(tmp[:, 5, :], tmp[:, 5, :], -1.0, tmp[:, 5, :], ALU.mult, ALU.max))
                dve.tensor_scalar(tmp[:, 5, :], tmp[:, 5, :], -1.0, np.pi / 2, ALU.mult, ALU.add).then_inc(g["trig_in"], 1)
                link(dve.tensor_scalar(tmp[:, 3, :], tmp[:, 3, :], -1.0, None, ALU.add))
                link(dve.tensor_scalar(val[:, 2, :], tmp[:, 3, :], 0.0, None, ALU.is_equal))
                link(dve.tensor_tensor(tmp[:, 3, :], tmp[:, 3, :], val[:, 2, :], ALU.add))
                link(dve.reciprocal(tmp[:, 3, :], tmp[:, 3, :]))
                link(dve.tensor_tensor(tmp[:, 3, :], tmp[:, 3, :], tmp[:, 2, :], ALU.mult))
                link(dve.tensor_tensor(val[:, 2, :], val[:, 2, :], tmp[:, 2, :], ALU.mult))
                dve.wait_ge(g["log"], 1)
                link(dve.tensor_tensor(tmp[:, 3, :], tmp[:, 3, :], tmp[:, 1, :], ALU.mult))
                link(dve.tensor_tensor(val[:, 2, :], val[:, 2, :], tmp[:, 3, :], ALU.add))
                link(dve.tensor_scalar(tmp[:, 3, :], dur[:], -1.0, 1e30, ALU.is_lt, ALU.mult))
                dve.tensor_tensor(val[:, 2, :], val[:, 2, :], tmp[:, 3, :], ALU.add).then_inc(g["val_ready"], 1)
                dve.wait_ge(g["valT_psum"], 1)
                link(dve.tensor_copy(valT[:], bank[0][:, 0:6 * NB].rearrange("p (f b) -> p f b", f=6)))
                dve.wait_ge(g["ld_const"], 96)
                dve.wait_ge(g["const_ready"], 4)
                for f, (first, n) in enumerate((WEEK, HOUR, DUR, DIFF)):
                    value = valT[:, f, :].unsqueeze(2).to_broadcast([P, NB, n])
                    for dst, side, op in ((above, 0, ALU.is_gt), (upto, 1, ALU.is_le)):
                        limit = lohi[:, side, first:first + n].unsqueeze(1).to_broadcast([P, NB, n])
                        dve.tensor_tensor(dst[:, :, first:first + n], value, limit, op)
                link(dve.tensor_copy(above[:, :, 49:51], valT[:, 4:6, :].rearrange("p f b -> p b f")))

                def ln_stats(phase, b, v):
                    n = NB * phase + b + 1
                    apart(dve)
                    dve.bn_stats(stats[:, v, :], h[:, b, :]).then_inc(g["ln_stats"], 1)
                    dve.wait_ge(g["ln_stats"], n)
                    apart(dve)
                    dve.bn_aggr(mv[:, v, :], stats[:, v, :]).then_inc(g["ln_mv"], 1)

                def ln_xhat(phase, b, v):
                    n = NB * phase + b + 1
                    dve.wait_ge(g["ln_rstd"], n)
                    if phase or later(b, 2):
                        dve.wait_ge(g["ln_xT_psum"], n - 2)
                    dve.tensor_scalar(xhat[:, v, :], h[:, b, :], mv[:, v, 0:1], rstd[:, v], ALU.subtract, ALU.mult).then_inc(g["ln_xhat"], 1)

                def tok(t, j, u):
                    if live(t, 0):
                        if later(t, 2):
                            dve.wait_ge(g["onehotT_psum"], t - 1)
                        dve.tensor_tensor(onehot[:, u, :], above[:, t, :], upto[:, t, :], ALU.mult).then_inc(g["onehot"], 1)
                    if live(t, 1):
                        b, v = t - 1, 1 - u
                        dve.wait_ge(g["tok_psum"], b + 1)
                        apart(dve)
                        dve.bn_stats(tok_st[:, v, :], bank[2 + v][:, 0:P]).then_inc(g["tok_stats"], 1)
                        dve.wait_ge(g["tok_stats"], b + 1)
                        apart(dve)
                        dve.bn_aggr(tok_mv[:, v, :], tok_st[:, v, :]).then_inc(g["tok_mv"], 1)
                    if live(t, 2):
                        b, v = t - 2, u
                        dve.wait_ge(g["tok_rstd"], b + 1)
                        dve.tensor_scalar(tokx[:, v, :], bank[2 + v][:, 0:P], tok_mv[:, v, 0:1], tok_rstd[:, v],
                                          ALU.subtract, ALU.mult).then_inc(g["tok_xhat"], 1)
                        dve.wait_ge(g["tok_xhat"], b + 1)
                        dve.tensor_tensor(tokx[:, v, :], tokx[:, v, :], ln0[:, 0, :], ALU.mult).then_inc(g["tok_scaled"], 1)
                        dve.wait_ge(g["tok_scaled"], b + 1)
                        dve.tensor_tensor(h[:, b, :], tokx[:, v, :], ln0[:, 1, :], ALU.add).then_inc(g["tok_h"], 1)
                        dve.wait_ge(g["tok_h"], b + 1)
                        ln_stats(0, b, v)
                    if live(t, 3):
                        ln_xhat(0, t - 3, 1 - u)
                steps(dve, 4, tok)

                def pos(c, u):
                    dve.wait_ge(g["pos_psum"], c + 1)
                    dve.tensor_copy(posT[:, :, 1:H0:2, bass.ds(8 * c, 8)],
                                    bank[2 * u + 1].rearrange("p (i t b) -> p b t i", i=8, t=NT0)).then_inc(g["pos_odd"], 1)
                for c in range(2):
                    pos(c, c)
                with dve.Fori(1, NB // 2) as j:
                    for u in range(2):
                        pos(2 * j + u, u)

                dve.wait_ge(g["ld_att0"], 80)
                dve.wait_ge(g["vs_ones"], 4)

                def att0(t, j, u):
                    if live(t, 4):
                        ln_xhat(1, t - 4, u)
                    if live(t, 1):
                        b, v = t - 1, 1 - u
                        dve.wait_ge(g["s0_psum"], b + 1)
                        dve.tensor_reduce(negmax[:, v], psum[:, 2:4, :].rearrange("p a (t r) -> p a t r", r=P), AX.X, ALU.max,
                                          negate=True).then_inc(g["negmax0"], 1)
                        dve.wait_ge(g["v0_psum"], b + 1)
                        if later(b, 2):
                            dve.wait_ge(g["o0_psum"], b - 1)
                        dve.tensor_copy(vs[:, v, :, 0:D0], bank[1].rearrange("p (h e) -> p h e", h=H0)).then_inc(g["v0"], 1)
                    if live(t, 2):
                        b, v = t - 2, u
                        dve.wait_ge(g["pT0_psum"], b + 1)
                        if later(b, 2):
                            dve.wait_ge(g["o0_psum"], b - 1)
                        dve.tensor_copy(probsT[:, v].rearrange("p a t r -> p (a t r)"), psum[:, 4:6, :].rearrange("p a c -> p (a c)")).then_inc(g["pT0"], 1)
                    if live(t, 3):
                        b, v = t - 3, 1 - u
                        dve.wait_ge(g["y0_psum"], b + 1)
                        dve.tensor_tensor(h[:, b, :], h[:, b, :], bank[1][:, 0:P], ALU.add).then_inc(g["y0_added"], 1)
                        dve.wait_ge(g["y0_added"], b + 1)
                        dve.tensor_tensor(h[:, b, :], h[:, b, :], bo0[:], ALU.add).then_inc(g["h0"], 1)
                        dve.wait_ge(g["h0"], b + 1)
                        ln_stats(1, b, v)
                    if live(t, 2):
                        b, v = t - 2, u
                        dve.wait_ge(g["o0_psum"], b + 1)
                        part = psum[:, 6:8, 0:NT0 * (D0 + 1)].rearrange("p a (t e) -> p a t e", t=NT0)
                        dve.reciprocal(rsum[:, v].unsqueeze(3), part[:, :, :, D0:D0 + 1]).then_inc(g["rsum0"], 1)
                        dve.wait_ge(g["rsum0"], b + 1)
                        if later(b, 2):
                            dve.wait_ge(g["oT0_psum"], b - 1)
                        dve.tensor_tensor(o0[:, v].rearrange("p (t a e) -> p a t e", t=NT0, a=2), part[:, :, :, 0:D0],
                                          rsum[:, v].unsqueeze(3).to_broadcast([P, 2, NT0, D0]), ALU.mult).then_inc(g["o0"], 1)
                steps(dve, 4, att0)

                dve.wait_ge(g["ld_moe0"], 128)
                dve.tensor_reduce(centre[:, 0, :], w2m[:], AX.X, ALU.add)
                link(dve.tensor_reduce(centre[:, 1, :], b2m[:], AX.X, ALU.add))
                link(dve.tensor_scalar(centre[:], centre[:], 1.0 / P, None, ALU.mult))
                dve.tensor_tensor(w2m[:], w2m[:], centre[:, 0, :].unsqueeze(2).to_broadcast([P, E0, P]), ALU.subtract)
                dve.tensor_tensor(b2m[:], b2m[:], centre[:, 1, :].unsqueeze(2).to_broadcast([P, E0, P]), ALU.subtract).then_inc(g["centred"], 1)
                dve.wait_ge(g["centred"], 1)

                dve.wait_ge(g["lg_psum"], 1)
                link(dve.tensor_copy(lg[:].rearrange("p b e -> p (b e)"), bank[6][:, 0:NB * E0]))
                experts = iota[:].unsqueeze(1).to_broadcast([P, NB, E0])

                def over(x):
                    return x.unsqueeze(2).to_broadcast([P, NB, E0])

                for k, scores in ((0, lg[:]), (1, top[:, 3])):
                    chosen = top[:, k]
                    link(dve.tensor_reduce(tops[:, k, :], scores, AX.X, ALU.max))
                    link(dve.tensor_tensor(chosen, scores, over(tops[:, k, :]), ALU.is_equal))
                    link(dve.scalar_tensor_tensor(chosen, chosen, -1000.0, experts, ALU.mult, ALU.add))
                    link(dve.tensor_reduce(tops[:, 2, :], chosen, AX.X, ALU.min))
                    link(dve.tensor_tensor(chosen, chosen, over(tops[:, 2, :]), ALU.is_equal))
                    if k == 0:
                        link(dve.scalar_tensor_tensor(top[:, 3], chosen, -3e38, lg[:], ALU.mult, ALU.add))
                dve.tensor_tensor(tops[:, 3, :], tops[:, 1, :], tops[:, 0, :], ALU.subtract).then_inc(g["tops"], 1)
                dve.wait_ge(g["topexp"], 1)
                link(dve.tensor_scalar(tops[:, 5, :], tops[:, 4, :], 1.0, None, ALU.add))
                link(dve.reciprocal(tops[:, 5, :], tops[:, 5, :]))
                link(dve.tensor_tensor(tops[:, 4, :], tops[:, 4, :], tops[:, 5, :], ALU.mult))
                dve.tensor_tensor(top[:, 0], top[:, 0], over(tops[:, 5, :]), ALU.mult)
                link(dve.tensor_tensor(top[:, 1], top[:, 1], over(tops[:, 4, :]), ALU.mult))
                dve.tensor_tensor(gates[:], top[:, 0], top[:, 1], ALU.add).then_inc(g["gates"], 1)

                def moe0(t, j, u):
                    if live(t, 1):
                        b, v = t - 1, 1 - u
                        dve.wait_ge(g["ysq"], b + 1)
                        dve.tensor_scalar(yvar[:, v], ysum2[:, v], 1.0 / P, EPS, ALU.mult, ALU.add).then_inc(g["yvar"], 1)
                    if live(t, 0):
                        dve.wait_ge(g["y_psum"], t + 1)
                        if later(t, 2):
                            dve.wait_ge(g["yg"], t - 1)
                            dve.wait_ge(g["ysq"], t - 1)
                        dve.tensor_tensor(ym[:, u].rearrange("p e n -> p (e n)"), psum[:, 2 + 2 * u:4 + 2 * u, :].rearrange("p a c -> p (a c)"),
                                          b2m[:].rearrange("p e n -> p (e n)"), ALU.add).then_inc(g["ym"], 1)
                    if live(t, 2):
                        b, v = t - 2, u
                        dve.wait_ge(g["yc"], b + 1)
                        dve.tensor_reduce(ysum[:, v, :], yc[:, v].rearrange("p e n -> p n e"), AX.X, ALU.add).then_inc(g["ysum"], 1)
                        dve.wait_ge(g["ysum"], b + 1)
                        dve.tensor_tensor(h[:, b, :], h[:, b, :], ysum[:, v, :], ALU.add).then_inc(g["h_moe0"], 1)
                    if live(t, 1):
                        b, v = t - 1, 1 - u
                        dve.wait_ge(g["yrstd"], b + 1)
                        dve.tensor_tensor(ycoef[:, v], yrstd[:, v], gates[:, b, :], ALU.mult).then_inc(g["ycoef"], 1)
                    if live(t, 1):
                        b, v = t - 1, 1 - u
                        dve.wait_ge(g["ycoef"], b + 1)
                        dve.wait_ge(g["yg"], b + 1)
                        dve.tensor_tensor(yc[:, v], yg[:, v], ycoef[:, v].unsqueeze(2).to_broadcast([P, E0, P]), ALU.mult).then_inc(g["yc"], 1)
                steps(dve, 2, moe0)
                dve.wait_ge(g["beta_psum"], 1)
                dve.wait_ge(g["h_moe0"], NB)
                for part in range(2):
                    last = dve.tensor_tensor(h[:, 8 * part:8 * part + 8, :], h[:, 8 * part:8 * part + 8, :],
                                             psum[:, 6 * part:6 * part + 2, :].rearrange("p a (b n) -> p (a b) n", n=P), ALU.add)
                last.then_inc(g["h_beta"], 1)

                dve.wait_ge(g["ld_att1"], 240)
                link(dve.tensor_scalar(nbg1[:], nbg1[:], -1.0, None, ALU.mult))
                dve.tensor_tensor(qbias[:, 0:2], qscale[:, 0:2], b1a[:, 0:1].to_broadcast([P, 2]), ALU.mult)
                dve.tensor_tensor(qbias[:, 2:3], qscale[:, 2:3], b1a[:, 2:3], ALU.mult).then_inc(g["ready1"], 1)
                dve.wait_ge(g["h_beta"], 1)

                def att1(t, j, u):
                    if live(t, 0):
                        ln_stats(2, t, u)
                    if live(t, 4):
                        b, v = t - 4, u
                        dve.wait_ge(g["ge1"], b + 1)
                        dve.tensor_scalar(gd1[:, v, 2:3], gd1[:, v, 1:2], 1.0, None, ALU.add).then_inc(g["gate1a"], 1)
                        dve.wait_ge(g["gate1a"], b + 1)
                        dve.reciprocal(gd1[:, v, 2:3], gd1[:, v, 2:3]).then_inc(g["gate1b"], 1)
                        dve.wait_ge(g["gate1b"], b + 1)
                        dve.tensor_scalar(gd1[:, v, 3:4], gd1[:, v, 2:3], -1.0, 1.0, ALU.mult, ALU.add).then_inc(g["gate1"], 1)
                        if later(b, 2):
                            dve.wait_ge(g["catT1_psum"], b - 1)
                        dve.tensor_scalar(cat1[:, v, 0:P], loc1[:, v, :], gd1[:, v, 2:3], None, ALU.mult)
                        dve.wait_ge(g["gate1"], b + 1)
                        dve.tensor_scalar(cat1[:, v, P:P + LH * LD], lat1[:, v, :], gd1[:, v, 3:4], None, ALU.mult)
                        dve.tensor_copy(cat1[:, v, P + LH * LD:], gd1[:, v, 3:4]).then_inc(g["cat1"], 1)
                    if live(t, 0):
                        ln_xhat(2, t, u)
                    if live(t, 2):
                        b, v = t - 2, u
                        dve.wait_ge(g["v1_psum"], b + 1)
                        if later(b, 2):
                            dve.wait_ge(g["o1_psum"], b - 1)
                        dve.tensor_tensor(v1[:, v, :, 0:D1], bank[1][:, 0:P].rearrange("p (h e) -> p h e", h=H1),
                                          bv1[:].rearrange("p (h e) -> p h e", h=H1), ALU.add)
                        dve.tensor_copy(gx1[:, v, :], bank[1][:, P:P + 1])
                        for odd in range(2):
                            rows = slice(CH * odd, CH * odd + CH)
                            heads = bank[1][rows, P + 1:P + 1 + LH * LD].rearrange("p (a o e) -> p a o e", a=2, o=2)[:, :, odd, :]
                            bias = brv1[rows, :].rearrange("p (a o e) -> p a o e", a=2, o=2)[:, :, odd, :]
                            last = dve.scalar_tensor_tensor(gv1[rows, v, :, odd, 0:LD], heads, 0.5, bias, ALU.mult, ALU.add)
                        last.then_inc(g["v1"], 1)
                    if live(t, 2):
                        b, v = t - 2, u
                        dve.wait_ge(g["s1_psum"], b + 1)
                        local = psum[:, 2:6, 0:2 * P].rearrange("p a (o r) -> p a o r", o=2)
                        latent = psum[:, 2:6, 2 * P:2 * P + CH]
                        dve.tensor_reduce(max1[:, v, 0:H1].rearrange("p (a o) -> p a o", o=2), local, AX.X, ALU.max)
                        dve.tensor_reduce(max1[:, v, H1:], latent, AX.X, ALU.max).then_inc(g["max1"], 1)
                    if live(t, 4):
                        b, v = t - 4, u
                        dve.wait_ge(g["y1_psum"], b + 1)
                        dve.tensor_tensor(h[:, b, :], h[:, b, :], bank[0][:, 0:P], ALU.add).then_inc(g["y1_added"], 1)
                        dve.wait_ge(g["y1_added"], b + 1)
                        dve.tensor_tensor(h[:, b, :], h[:, b, :], bo1[:], ALU.add).then_inc(g["h1"], 1)
                    if live(t, 2):
                        b, v = t - 2, u
                        dve.wait_ge(g["max1"], b + 1)
                        if later(b, 2):
                            dve.wait_ge(g["latT_psum"], b - 1)
                        dve.tensor_tensor(e1[:, v, 0:H1 * P].rearrange("p (a o r) -> p a o r", a=4, o=2), local,
                                          max1[:, v, 0:H1].rearrange("p (a o) -> p a o", o=2).unsqueeze(3).to_broadcast([P, 4, 2, P]), ALU.subtract)
                        dve.tensor_tensor(e1[:, v, H1 * P:].rearrange("p (a r) -> p a r", a=4), latent,
                                          max1[:, v, H1:].unsqueeze(2).to_broadcast([P, LH, CH]), ALU.subtract).then_inc(g["sub1"], 1)
                    if live(t, 0):
                        dve.wait_ge(g["xT1"], t + 1)
                        if later(t, 2):
                            dve.wait_ge(g["v1_psum"], t - 1)
                        pairs = xT1[:, u, :].rearrange("p (c o) -> p c o", o=2)
                        for i in range(2):
                            last = dve.tensor_tensor(pool1[:, u, i, :].unsqueeze(2), pairs[:, :, 0:1], pairs[:, :, 1:2], ALU.add)
                        last.then_inc(g["pool1"], 1)
                    if live(t, 3):
                        b, v = t - 3, 1 - u
                        dve.wait_ge(g["o1_psum"], b + 1)
                        heads = bank[1][:, 0:(H1 + LH) * (D1 + 1)].rearrange("p (h e) -> p h e", h=H1 + LH)
                        dve.reciprocal(sum1[:, v, :].unsqueeze(2), heads[:, :, D1:D1 + 1]).then_inc(g["rsum1"], 1)
                        dve.wait_ge(g["rsum1"], b + 1)
                        dve.tensor_tensor(loc1[:, v, :].rearrange("p (h e) -> p h e", h=H1), heads[:, 0:H1, 0:D1],
                                          sum1[:, v, 0:H1].unsqueeze(2).to_broadcast([P, H1, D1]), ALU.mult)
                        dve.scalar_tensor_tensor(lat1[:, v, :].rearrange("p (h e) -> p h e", h=LH), heads[:, H1:, 0:D1], valid[:],
                                                 sum1[:, v, H1:].unsqueeze(2).to_broadcast([P, LH, LD]), ALU.mult, ALU.mult).then_inc(g["o1"], 1)
                        dve.wait_ge(g["o1"], b + 1)
                        dve.scalar_tensor_tensor(gw1[:, v, :], loc1[:, v, :], 1.0, wg1[:], ALU.mult, ALU.mult,
                                                 accum_out=gd1[:, v, 0:1]).then_inc(g["gate1c"], 1)
                        dve.wait_ge(g["gate1c"], b + 1)
                        dve.tensor_tensor(gd1[:, v, 0:1], gd1[:, v, 0:1], gx1[:, v, :], ALU.add).then_inc(g["gd1"], 1)
                steps(dve, 4, att1)

                dve.wait_ge(g["h1"], NB)
                dve.wait_ge(g["ld_att2"], 80)
                link(dve.tensor_scalar(col2[:, 2:3], col2[:, 2:3], float(D2) ** 0.5, None, ALU.mult))

                def att2(t, j, u):
                    if live(t, 0):
                        ln_stats(3, t, u)
                    if live(t, 1):
                        b, v = t - 1, 1 - u
                        dve.wait_ge(g["sq2"], b + 1)
                        dve.tensor_reduce(ss2[:, v], sq2[:, v].rearrange("p (h e) -> p h e", e=D2), AX.X, ALU.add).then_inc(g["ss2"], 1)
                    if live(t, 0):
                        ln_xhat(3, t, u)
                    if live(t, 3):
                        b, v = t - 3, 1 - u
                        dve.wait_ge(g["pT2_psum"], b + 1)
                        if later(b, 2):
                            dve.wait_ge(g["o2_psum"], b - 1)
                        dve.tensor_copy(pT2[:, v].rearrange("p h r -> p (h r)"), bank[4][:, 0:2 * P]).then_inc(g["pT2"], 1)
                        dve.wait_ge(g["o2_psum"], b + 1)
                        heads = bank[5][:, 0:H2 * (D2 + 1)].rearrange("p (h e) -> p h e", h=H2)
                        dve.reciprocal(sum2[:, v, :].unsqueeze(2), heads[:, :, D2:D2 + 1]).then_inc(g["rsum2"], 1)
                        dve.wait_ge(g["rsum2"], b + 1)
                        if later(b, 2):
                            dve.wait_ge(g["oT2_psum"], b - 1)
                        dve.tensor_tensor(o2[:, v, :].rearrange("p (h e) -> p h e", h=H2), heads[:, :, 0:D2],
                                          sum2[:, v, :].unsqueeze(2).to_broadcast([P, H2, D2]), ALU.mult).then_inc(g["o2"], 1)
                    if live(t, 1):
                        b, v = t - 1, 1 - u
                        dve.wait_ge(g["rn2"], b + 1)
                        if later(b, 2):
                            dve.wait_ge(g["qkT2_psum"], b - 1)
                            dve.wait_ge(g["o2_psum"], b - 1)
                        dve.tensor_tensor(qk2[:, v].rearrange("p (h e) -> p h e", e=D2), bank[0][:, 0:2 * P].rearrange("p (h e) -> p h e", e=D2),
                                          rn2[:, v].unsqueeze(2).to_broadcast([P, 2 * H2, D2]), ALU.mult)
                        dve.tensor_copy(v2[:, v, :, 0:D2], bank[0][:, 2 * P:3 * P].rearrange("p (h e) -> p h e", e=D2)).then_inc(g["qk2"], 1)
                    if live(t, 2):
                        b, v = t - 2, u
                        dve.wait_ge(g["s2_psum"], b + 1)
                        dve.tensor_reduce(max2[:, v], psum[:, 2:4, 0:P], AX.X, ALU.max, negate=True).then_inc(g["max2"], 1)
                    if live(t, 4):
                        b, v = t - 4, u
                        dve.wait_ge(g["gl2_psum"], b + 1)
                        dve.tensor_tensor(glog[:, b, :], bank[6][:, 0:E2], gb2[:], ALU.add).then_inc(g["gl2"], 1)
                steps(dve, 4, att2)

                dve.wait_ge(g["gl2"], NB)
                dve.tensor_reduce(gsum[:, 0, :], glog, AX.X, ALU.max).then_inc(g["chain4"], 1)
                dve.wait_ge(g["chain4"], 1)
                dve.tensor_tensor(glog, glog, over(gsum[:, 0, :]), ALU.subtract).then_inc(g["chain4"], 1)
                dve.wait_ge(g["act4"], 1)
                link(dve.tensor_reduce(gsum[:, 1, :], g2, AX.X, ALU.add))
                link(dve.reciprocal(gsum[:, 1, :], gsum[:, 1, :]))
                dve.tensor_tensor(g2, g2, over(gsum[:, 1, :]), ALU.mult).then_inc(g["g2"], 1)
                dve.wait_ge(g["b2_psum"], 1)
                dve.tensor_tensor(h[:], h[:], psum[:, 2:6, :].rearrange("p a (b n) -> p (a b) n", n=P), ALU.add).then_inc(g["acc0"], 1)

                dve.wait_ge(g["acc0"], 1)

                def experts2(grp):
                    for e in range(E2):
                        n = E2 * grp + e
                        dve.wait_ge(g["eo_psum"], n + 1)
                        if e > 0:
                            dve.wait_ge(g["acc"], n)
                        elif later(grp, 1):
                            dve.wait_ge(g["stored"], 16 * grp)
                        for u in range(GB):
                            b = GB * grp + u
                            last = dve.scalar_tensor_tensor(acc[:, u, :], bank[4 + e % 2][:, u * P:(u + 1) * P], g2[:, b, e:e + 1],
                                                            h[:, b, :] if e == 0 else acc[:, u, :], ALU.mult, ALU.add)
                        last.then_inc(g["acc"], 1)
                    dve.wait_ge(g["acc"], E2 * grp + E2)
                    dve.sem_inc(g["out_acc"], 1)
                experts2(0)
                with dve.Fori(1, NG) as grp:
                    experts2(grp)

            @block.tensor
            def _(pe):
                pe.wait_ge(g["ld_const"], 96)
                pe.matmul(bank[1][0:NF, 0:P], tab_l[:], tab_r[:], start=True, stop=True).then_inc(g["table_psum"], 1)
                pe.wait_ge(g["trig"], 1)
                pe.wait_ge(g["val_ready"], 1)
                for f in range(6):
                    last = pe.transpose(bank[0][:, f * NB:(f + 1) * NB], val[:, f, :], ident[0:NB, 0:NB])
                last.then_inc(g["valT_psum"], 1)
                pe.wait_ge(g["table_ready"], 1)
                pe.wait_ge(g["ld_att0"], 80)

                def ln_transpose(phase, b, v, dst):
                    pe.wait_ge(g["ln_xhat"], NB * phase + b + 1)
                    pe.transpose(dst[:, 0:P], xhat[:, v, :], ident[:]).then_inc(g["ln_xT_psum"], 1)

                def tok(t, j, u):
                    if live(t, 0):
                        pe.wait_ge(g["onehot"], t + 1)
                        if later(t, 2):
                            pe.wait_ge(g["onehotT"], t - 1)
                        apart(pe)
                        pe.transpose(bank[u][0:NF, 0:P], onehot[:, u, :], ident[:]).then_inc(g["onehotT_psum"], 1)
                    if live(t, 1):
                        b, v = t - 1, 1 - u
                        pe.wait_ge(g["onehotT"], b + 1)
                        if later(b, 2):
                            pe.wait_ge(g["tok_xhat"], b - 1)
                        pe.matmul(bank[2 + v][:, 0:P], onehotT[:, v, :], table[:], start=True, stop=True).then_inc(g["tok_psum"], 1)
                    if live(t, 3):
                        b, v = t - 3, 1 - u
                        if later(b, 2):
                            pe.wait_ge(g["ln_xT"], b - 1)
                        ln_transpose(0, b, v, bank[4 + v])
                    if live(t, 4):
                        b = t - 4
                        pe.wait_ge(g["ln_xT"], b + 1)
                        if later(b, 2):
                            pe.wait_ge(g["q_all"], b - 1)
                        for tile in range(NT0):
                            last = pe.matmul(bank[6 + u][:, tile * P:(tile + 1) * P], wq0[:, tile * P:(tile + 1) * P],
                                             xT_all[:, b, :], start=True, stop=True)
                        last.then_inc(g["q_psum"], 1)
                steps(pe, 4, tok)

                def pos(c, u):
                    pe.wait_ge(g["qn"], c + 1)
                    pe.wait_ge(g["relw"], c + 1)
                    if later(c, 2):
                        pe.wait_ge(g["pos_even"], c - 1)
                        pe.wait_ge(g["pos_odd"], c - 1)
                    for i in range(8):
                        for odd in range(2):
                            rows = slice(64 * odd, 64 * odd + 64)
                            last = pe.matmul(bank[2 * u + odd][:, i * 64:(i + 1) * 64], relw[rows, u, 7 - i:7 - i + P],
                                             qn[rows, u, i, :], start=True, stop=True)
                    last.then_inc(g["pos_psum"], 1)
                for c in range(2):
                    pos(c, c)
                with pe.Fori(1, NB // 2) as j:
                    for u in range(2):
                        pos(2 * j + u, u)

                pe.wait_ge(g["pos_even"], NB)
                pe.wait_ge(g["pos_odd"], NB)

                def att0(t, j, u):
                    if live(t, 1):
                        b, v = t - 1, 1 - u
                        pe.wait_ge(g[f"att0_in{1 - u}"], 48 * (j + u))
                        pe.wait_ge(g["k0"], b + 1)
                        if later(b, 1):
                            pe.wait_ge(g["p0"], b)
                        for odd in range(2):
                            for tile in range(NT0):
                                pe.matmul(bank[2 + odd][:, tile * P:(tile + 1) * P], posTs[:, v, 2 * tile + odd, :], ident[:],
                                          start=(tile == 0), stop=False, skip_group_check=True)
                        for tile in range(NT0):
                            for odd in range(2):
                                rows = slice(64 * odd, 64 * odd + 64)
                                last = pe.matmul(bank[2 + odd][:, tile * P:(tile + 1) * P], qTs[rows, v, tile, :],
                                                 kTs[rows, v, tile, :], start=False, stop=(tile == NT0 - 1), skip_group_check=True)
                        last.then_inc(g["s0_psum"], 1)
                    if live(t, 3):
                        b, v = t - 3, 1 - u
                        pe.wait_ge(g["o0"], b + 1)
                        for tile in range(NT0):
                            last = pe.transpose(bank[0][:, tile * P:(tile + 1) * P], o0[:, v, tile * P:(tile + 1) * P], ident[:])
                        last.then_inc(g["oT0_psum"], 1)
                    if live(t, 1):
                        if later(t, 4):
                            pe.wait_ge(g["y0_added"], t - 3)
                        elif later(t, 2):
                            pe.wait_ge(g["v0"], t - 1)
                        pe.matmul(bank[1], xTs[:, 1 - u, :], wkv0[:, H0 * D0:], start=True, stop=True).then_inc(g["v0_psum"], 1)
                    if live(t, 2):
                        b, v = t - 2, u
                        pe.wait_ge(g["p0"], b + 1)
                        if later(b, 1):
                            pe.wait_ge(g["pT0"], b)
                        for odd in range(2):
                            for tile in range(NT0):
                                last = pe.transpose(bank[4 + odd][:, tile * P:(tile + 1) * P], probs[:, v, odd, tile, :], ident[:])
                        last.then_inc(g["pT0_psum"], 1)
                    if live(t, 4):
                        b = t - 4
                        pe.wait_ge(g["o0"], (t - 2) if live(t, 3) else NB)
                        if later(b, 1):
                            pe.wait_ge(g["ln_xT"], NB + b)
                        ln_transpose(1, b, u, bank[7][:, 3 * P:])
                    if live(t, 0):
                        if later(t, 3):
                            pe.wait_ge(g["oT0"], t - 2)
                        elif later(t, 1):
                            pe.wait_ge(g["k0"], t)
                        if not isinstance(t, int) or t < 2:
                            pe.wait_ge(g["q_all"], NB)
                        for tile in range(NT0):
                            last = pe.matmul(bank[0][:, tile * P:(tile + 1) * P], wkv0[:, tile * P:(tile + 1) * P],
                                             xT_all[:, t, :], start=True, stop=True)
                        last.then_inc(g["k0_psum"], 1)
                    if live(t, 3):
                        b, v = t - 3, 1 - u
                        pe.wait_ge(g["oT0"], b + 1)
                        pe.wait_ge(g["v0"], t if live(t, 1) else NB)
                        if not live(t, 1) and later(b, 1):
                            pe.wait_ge(g["y0_added"], b)
                        for tile in range(NT0):
                            last = pe.matmul(bank[1][:, 0:P], oT0[:, v, tile, :], wo0[:, tile, :], start=(tile == 0), stop=(tile == NT0 - 1))
                        last.then_inc(g["y0_psum"], 1)
                    if live(t, 2):
                        b, v = t - 2, u
                        pe.wait_ge(g["pT0"], b + 1)
                        pe.wait_ge(g["v0"], b + 1)
                        if later(b, 1):
                            pe.wait_ge(g["o0"], b)
                        if live(t, 4):
                            pe.wait_ge(g["ln_xT"], NB + t - 3)
                        for odd in range(2):
                            for tile in range(NT0):
                                last = pe.matmul(bank[6 + odd][:, tile * (D0 + 1):(tile + 1) * (D0 + 1)], probsT[:, v, odd, tile, :],
                                                 vs[:, v, 2 * tile + odd, :], start=True, stop=True)
                        last.then_inc(g["o0_psum"], 1)
                steps(pe, 4, att0)

                pe.wait_ge(g["ld_moe0"], 128)
                pe.wait_ge(g["ln_xT"], 2 * NB)
                pe.wait_ge(g["p0"], NB)
                pe.wait_ge(g["pT0"], NB)
                pe.wait_ge(g["o0"], NB)
                for grp in range(NG):
                    last = pe.matmul(bank[2 + grp][0:E0, :], wgm[:], xT_all[:, GB * grp:GB * grp + GB, :], start=True, stop=True)
                last.then_inc(g["lgT_psum"], 1)
                pe.wait_ge(g["lgT"], 1)
                for b in range(NB):
                    last = pe.transpose(bank[6][:, b * E0:(b + 1) * E0], lgT[:, b * P:(b + 1) * P], ident[0:E0, 0:E0])
                last.then_inc(g["lg_psum"], 1)
                pe.wait_ge(g["centred"], 1)
                pe.wait_ge(g["h0"], NB)

                def moe0(t, j, u):
                    for half in range(2):
                        if live(t, 0, NB // 2):
                            for pair in (2 * half, 2 * half + 1):
                                if pair >= 2 or later(t, 1):
                                    pe.wait_ge(g["hid"], 4 * t + pair - 1)
                                for e in (2 * pair, 2 * pair + 1):
                                    last = pe.matmul(bank[pair % 2][:, e % 2 * 2 * P:(e % 2 + 1) * 2 * P], w1m[:, e, :],
                                                     xT_all[:, bass.ds(2 * t, 2), :], start=True, stop=True)
                                last.then_inc(g["hid_psum"], 1)
                        if live(t, 1, NB // 2):
                            if half == 0:
                                pe.wait_ge(g["hid"], 4 * t)
                            if later(t, 2):
                                pe.wait_ge(g["ym"], 2 * t - 3 + half)
                            for e in range(E0):
                                last = pe.matmul(bank[2 + 2 * half + e // 4][:, e % 4 * P:(e % 4 + 1) * P],
                                                 hid[:, 1 - u, e, half * P:(half + 1) * P], w2m[:, e, :], start=True, stop=True)
                            last.then_inc(g["y_psum"], 1)
                steps(pe, 1, moe0, NB // 2)
                pe.wait_ge(g["hid"], 2 * NB)
                pe.wait_ge(g["gates"], 1)
                for b in range(NB):
                    last = pe.transpose(bank[(0, 1, 6, 7)[b // GB]][0:E0, b % GB * P:(b % GB + 1) * P], gates[:, b, :], ident[:])
                last.then_inc(g["gT_psum"], 1)
                pe.wait_ge(g["gT"], 1)
                for b in range(NB):
                    last = pe.matmul(bank[(0, 1, 6, 7)[b // GB]][:, b % GB * P:(b % GB + 1) * P], gT[:, b * P:(b + 1) * P], beta[:],
                                     start=True, stop=True)
                last.then_inc(g["beta_psum"], 1)

                pe.wait_ge(g["ld_att1"], 240)
                pe.wait_ge(g["ym"], NB)
                pe.wait_ge(g["h_beta"], 1)
                pe.matmul(bank[0][0:LH * LD + 1, 0:P], wroT[:], wo1[:], start=True, stop=True).then_inc(g["wro_psum"], 1)
                pe.wait_ge(g["wro1"], 1)

                def att1(t, j, u):
                    if live(t, 2):
                        b, v = t - 2, u
                        pe.wait_ge(g["k1"], b + 1)
                        if later(b, 1):
                            pe.wait_ge(g["sub1"], b)
                        for a in range(4):
                            pe.matmul(bank[2 + a][:, 0:2 * P + CH], identb[:], maskb[:], start=True, stop=False, skip_group_check=True)
                        for o in range(3):
                            for a in range(4):
                                rows = slice(32 * a, 32 * a + 32)
                                if o < 2:
                                    last = pe.matmul(bank[2 + a][:, o * P:(o + 1) * P], qT1[rows, v, o, :], kT1[rows, v, :],
                                                     start=False, stop=False, skip_group_check=True)
                                else:
                                    last = pe.matmul(bank[2 + a][:, 2 * P:2 * P + CH], rqT1[rows, v, :], gkT1[rows, v, :],
                                                     start=False, stop=True, skip_group_check=True)
                        last.then_inc(g["s1_psum"], 1)
                    if live(t, 4):
                        b, v = t - 4, u
                        pe.wait_ge(g["cat1"], b + 1)
                        if not live(t, 2):
                            pe.wait_ge(g["y1_added"], b)
                        pe.transpose(bank[0][:, 0:P], cat1[:, v, 0:P], ident[:])
                        pe.transpose(bank[0][0:LH * LD + 1, P:2 * P], cat1[:, v, P:], ident[:]).then_inc(g["catT1_psum"], 1)
                    if live(t, 2):
                        b, v = t - 2, u
                        if later(t, 4):
                            pe.wait_ge(g["o1"], t - 3)
                        elif later(b, 1):
                            pe.wait_ge(g["v1"], b)
                        pe.matmul(bank[1][:, 0:P + 1], xT1[:, v, :], wv1[:], start=True, stop=True)
                        pe.matmul(bank[1][:, P + 1:P + 1 + LH * LD], pool1[:, v].rearrange("p a c -> p (a c)"), wrv1[:], start=True, stop=True).then_inc(g["v1_psum"], 1)
                    if live(t, 3):
                        b, v = t - 3, 1 - u
                        pe.wait_ge(g["e1"], b + 1)
                        if later(b, 1):
                            pe.wait_ge(g["pT1"], b)
                        for hd in range(H1):
                            last = pe.transpose(bank[6 + hd // 4][:, hd % 4 * P:(hd % 4 + 1) * P], e1[:, v, hd * P:(hd + 1) * P], ident[:])
                        last.then_inc(g["pT1_psum"], 1)
                        if live(t, 2):
                            pe.wait_ge(g["v1"], t - 1)
                        elif later(b, 1):
                            pe.wait_ge(g["o1"], b)
                        for i in range(2):
                            last = pe.transpose(bank[1][:, i * P:(i + 1) * P], e1[:, v, (H1 + i) * P:(H1 + i + 1) * P], ident[:])
                        last.then_inc(g["latT_psum"], 1)
                    if live(t, 0):
                        if live(t, 2) and not live(t, 3):
                            pe.wait_ge(g["v1"], t - 1)
                        if later(t, 1):
                            pe.wait_ge(g["xT1"], t)
                        ln_transpose(2, t, u, bank[1][:, LAT:])
                    if live(t, 4):
                        b, v = t - 4, u
                        pe.wait_ge(g["catT1"], b + 1)
                        pe.matmul(bank[0][:, 0:P], catT1[:, v, 0, :], wo1[:], start=True, stop=False)
                        pe.matmul(bank[0][:, 0:P], catT1[0:LH * LD + 1, v, 1, :], wro1[:], start=False, stop=True).then_inc(g["y1_psum"], 1)
                    if live(t, 1):
                        b, v = t - 1, 1 - u
                        pe.wait_ge(g["xT1"], b + 1)
                        pe.wait_ge(g["pool1"], b + 1)
                        if later(t, 4):
                            pe.wait_ge(g["y1_added"], t - 3)
                        elif later(b, 1):
                            pe.wait_ge(g["k1"], b)
                        for i in range(3):
                            pe.matmul(bank[0][:, i * P:(i + 1) * P], wqk1[:, i, :], xT1[:, v, :], start=True, stop=True)
                        pe.matmul(bank[0][:, 3 * P:3 * P + CH], wqk1[:, 3, :], pool1[:, v, 0, :], start=True, stop=True).then_inc(g["proj1_psum"], 1)
                    if live(t, 3):
                        b, v = t - 3, 1 - u
                        pe.wait_ge(g["pT1"], b + 1)
                        pe.wait_ge(g["latT1"], b + 1)
                        pe.wait_ge(g["v1"], b + 1)
                        if live(t, 0):
                            pe.wait_ge(g["xT1"], t + 1)
                        for hd in range(H1):
                            pe.matmul(bank[1][:, hd * (D1 + 1):(hd + 1) * (D1 + 1)], pT1[:, v, hd * P:(hd + 1) * P], v1[:, v, hd, :], start=True, stop=True)
                        for i in range(2):
                            c = (H1 + 2 * i) * (D1 + 1)
                            last = pe.matmul(bank[1][:, c:c + 2 * (LD + 1)], pT1[:, v, (H1 + i) * P:(H1 + i + 1) * P],
                                             gv1[:, v, i].rearrange("p o e -> p (o e)"), start=True, stop=True)
                        last.then_inc(g["o1_psum"], 1)
                steps(pe, 4, att1)

                pe.wait_ge(g["ld_att2"], 80)
                pe.wait_ge(g["h1"], NB)

                def att2(t, j, u):
                    if live(t, 2):
                        b, v = t - 2, u
                        pe.wait_ge(g["qk2"], b + 1)
                        if later(b, 1):
                            pe.wait_ge(g["qkT2"], b)
                        for i in range(2):
                            last = pe.transpose(bank[1][:, i * P:(i + 1) * P], qk2[:, v, i * P:(i + 1) * P], ident[:])
                        last.then_inc(g["qkT2_psum"], 1)
                    if live(t, 1):
                        b, v = t - 1, 1 - u
                        pe.wait_ge(g["xT2"], b + 1)
                        if later(b, 1):
                            pe.wait_ge(g["qk2"], b)
                        pe.matmul(bank[0][:, 0:3 * P], xT2[:, v, :], wqkv2[:], start=True, stop=True).then_inc(g["qkv2_psum"], 1)
                    if live(t, 4):
                        b, v = t - 4, u
                        pe.wait_ge(g["o2"], b + 1)
                        if later(b, 1):
                            pe.wait_ge(g["gl2"], b)
                        pe.transpose(bank[6][:, 0:P], o2[:, v, :], ident[:]).then_inc(g["oT2_psum"], 1)
                    if live(t, 3):
                        b, v = t - 3, 1 - u
                        pe.wait_ge(g["p2"], b + 1)
                        if later(b, 1):
                            pe.wait_ge(g["pT2"], b)
                        for hd in range(H2):
                            last = pe.transpose(bank[4][:, hd * P:(hd + 1) * P], p2[:, v, hd, :], ident[:])
                        last.then_inc(g["pT2_psum"], 1)
                    if live(t, 4):
                        b, v = t - 4, u
                        pe.wait_ge(g["oT2"], b + 1)
                        pe.matmul(bank[6][:, 0:P], wo2[:], oT2[:, v, :], start=True, stop=True).then_inc(g["yT2_psum"], 1)
                    if live(t, 2):
                        b, v = t - 2, u
                        pe.wait_ge(g["qkT2"], b + 1)
                        if later(b, 1):
                            pe.wait_ge(g["p2"], b)
                        for hd in range(H2):
                            pe.matmul(bank[2 + hd][:, 0:P], identb[:], maskb[:, 0:P], start=True, stop=False, skip_group_check=True)
                        for hd in range(H2):
                            rows = slice(D2 * hd, D2 * hd + D2)
                            last = pe.matmul(bank[2 + hd][:, 0:P], qkT2[rows, v, 0, :], qkT2[rows, v, 1, :], start=False, stop=True, skip_group_check=True)
                        last.then_inc(g["s2_psum"], 1)
                    if live(t, 0):
                        if later(t, 1):
                            pe.wait_ge(g["xT2"], t)
                        ln_transpose(3, t, u, bank[7])
                    if live(t, 3):
                        b, v = t - 3, 1 - u
                        pe.wait_ge(g["pT2"], b + 1)
                        pe.wait_ge(g["qk2"], b + 1)
                        if later(b, 1):
                            pe.wait_ge(g["o2"], b)
                        for hd in range(H2):
                            last = pe.matmul(bank[5][:, hd * (D2 + 1):(hd + 1) * (D2 + 1)], pT2[:, v, hd, :], v2[:, v, hd, :], start=True, stop=True)
                        last.then_inc(g["o2_psum"], 1)
                    if live(t, 4):
                        b, v = t - 4, u
                        pe.wait_ge(g["yT2"], b + 1)
                        pe.wait_ge(g["yT_all"], b + 1)
                        pe.matmul(bank[6][:, 0:E2], yT2[:, v, :], gw2[:], start=True, stop=True).then_inc(g["gl2_psum"], 1)
                steps(pe, 4, att2)

                pe.wait_ge(g["ld_moe1"], 64)
                pe.wait_ge(g["g2"], 1)
                for b in range(NB):
                    last = pe.transpose(bank[2 + b // GB][0:E2, b % GB * P:(b % GB + 1) * P], g2[:, b, :], ident[:])
                last.then_inc(g["g2T_psum"], 1)
                pe.wait_ge(g["g2T"], 1)
                for b in range(NB):
                    last = pe.matmul(bank[2 + b // GB][:, b % GB * P:(b % GB + 1) * P], g2T[:, b * P:(b + 1) * P], b2f[:], start=True, stop=True)
                last.then_inc(g["b2_psum"], 1)

                pe.wait_ge(g["acc0"], 1)

                def up(grp, e):
                    for f in range(NC2):
                        n = NC2 * (E2 * grp + e) + f
                        if e > 0 or later(grp, 1):
                            pe.wait_ge(g["hf"], n - NC2 + 1)
                        pe.matmul(bank[f], w1f[:, e, f * P:(f + 1) * P], yT_all[:, bass.ds(GB * grp, GB), :], start=True, stop=True).then_inc(g["hf_psum"], 1)

                def down(grp, e):
                    n = E2 * grp + e
                    pe.wait_ge(g["hf"], NC2 * n + NC2)
                    if e >= 2 or later(grp, 1):
                        pe.wait_ge(g["acc"], n - 1)
                    for u in range(GB):
                        for f in range(NC2):
                            last = pe.matmul(bank[4 + e % 2][:, u * P:(u + 1) * P], hidf[:, e % 2, f, u * P:(u + 1) * P], w2f[:, e, f, :],
                                             start=(f == 0), stop=(f == NC2 - 1))
                    last.then_inc(g["eo_psum"], 1)

                def group(grp):
                    up(grp, 0)
                    for e in range(E2):
                        if e + 1 < E2:
                            up(grp, e + 1)
                        down(grp, e)
                group(0)
                with pe.Fori(1, NG) as grp:
                    group(grp)


def kernel(**inputs):
    import concourse.bacc as bacc
    import ml_dtypes
    from concourse.bass_utils import run_bass_kernel_spmd

    a = {k: np.asarray(v) for k, v in inputs.items()}

    tab_l = np.zeros((43, NF), np.float32)
    tab_l[0:12, 0:7] = a["L0_tok_W_weekday"].T
    tab_l[12:24, 7:31] = a["L0_tok_W_hour"].T
    tab_l[26:34, 31:41] = a["L0_tok_W_dur"].T
    tab_l[34:42, 41:49] = a["L0_tok_W_tdiff"].T
    tab_l[24, 49] = tab_l[25, 50] = tab_l[42, 51] = 1.0
    tab_r = np.concatenate([a["L0_tok_proj_w"].T, a["L0_tok_proj_b"][None, :]])
    bounds = np.stack(bounds_by_column())
    first, n = DUR
    edges = a["L0_tok_dur_boundaries"]
    bounds[0, first], bounds[1, first + n - 1] = -3e38, 3e38
    bounds[0, first + 1:first + n] = edges[1:]
    bounds[1, first:first + n - 1] = edges[1:]
    rel = a["L0_attn_rel_emb"][::-1].T
    bf16 = ml_dtypes.bfloat16

    def heads_apart(w):
        out = np.zeros((*w.shape[:-1], LH, 32), w.dtype)
        out[..., :LD] = w.reshape(*w.shape[:-1], LH, LD)
        return out.reshape(*w.shape[:-1], P)

    q = "L1_attn_"
    even = (np.arange(P) // D1 % 2 == 0).astype(np.float32)
    token, key, chunk = np.arange(P)[:, None], np.arange(P)[None, :], np.arange(CH)[None, :]
    causal = np.where(key <= token, 0.0, -1e30)
    before = np.where(chunk < token // 2, 0.0, -1e30)
    laid = dict(
        a, ident=np.eye(P, dtype=np.float32), tab_l=tab_l, tab_r=tab_r, bounds=bounds.reshape(-1), relT=np.concatenate([rel, rel]),
        w1m=a["L0_ffn_W1"].transpose(1, 0, 2), w2m=a["L0_ffn_W2"].transpose(1, 0, 2), L0_ffn_b2=a["L0_ffn_b2"].reshape(-1),
        L0_ffn_gamma=a["L0_ffn_gamma"].reshape(-1), b1m=a["L0_ffn_b1"].T, iota=np.arange(E0, dtype=np.float32),
        wqk1=np.stack([a[q + "Wq"], a[q + "Wk"], heads_apart(a[q + "Wrq"]), heads_apart(a[q + "Wrk"])], 1),
        wv1=np.concatenate([a[q + "Wv"], a[q + "Wg"][:P]], 1),
        b1a=np.stack([a[q + "bq"], a[q + "bk"], heads_apart(a[q + "brq"]), heads_apart(a[q + "brk"])], 1),
        qscale=np.stack([0.25 * even, 0.25 * (1 - even), np.full(P, 0.25)], 1).astype(np.float32),
        wg1=a[q + "Wg"][P:, 0], valid=(np.arange(P) >= 2).astype(np.float32)[:, None],
        wroT=np.concatenate([a[q + "Wro"], a[q + "bro"][None, :]]).T,
        identb=np.eye(P).astype(bf16), maskb=np.concatenate([causal, causal, before], 1).astype(bf16),
        wqkv2=np.concatenate([a["L1_ffn_Wq"], a["L1_ffn_Wk"], a["L1_ffn_Wv"]], 1),
        col2=np.stack([a["L1_ffn_ln_g"], a["L1_ffn_ln_b"], np.tile(a["L1_ffn_qn_g"], H2), np.tile(a["L1_ffn_kn_g"], H2)], 1),
        b1f=a["L1_ffn_b1"].reshape(E2, NC2, P).transpose(2, 0, 1),
        w1f=a["L1_ffn_W1"].transpose(1, 0, 2), w2f=a["L1_ffn_W2"].reshape(E2, NC2, P, P).transpose(2, 0, 1, 3))
    names = ["x", "itok_BS_0_1439", "itok_BS_0_7", "fside_BS_durations", "ident", "bounds", "tab_l", "tab_r",
             "L0_tok_ln_w", "L0_tok_ln_b", "L0_attn_Wq", "relT", "L0_attn_Wkv", "L0_attn_Wo", "L0_attn_bo",
             "w1m", "w2m", "L0_ffn_b2", "L0_ffn_gamma", "L0_ffn_beta", "b1m", "L0_ffn_Wg", "iota",
             "wqk1", "wv1", "L1_attn_Wrv", "b1a", "qscale", "L1_attn_bv", "L1_attn_brv", "wg1", "L1_attn_bg", "valid", "wroT",
             "L1_attn_Wo", "L1_attn_bo", "identb", "maskb",
             "wqkv2", "L1_ffn_Wo", "col2", "L1_ffn_gate_W", "L1_ffn_gate_b", "b1f", "L1_ffn_b2", "w1f", "w2f"]

    nc = bacc.Bacc("TRN2", target_bir_lowering=False, num_devices=1)
    arrays, d = {}, {}
    for name in names:
        v = np.ascontiguousarray(laid[name])
        arrays[name + "_dram"] = v
        d[name] = nc.dram_tensor(name + "_dram", v.shape, mybir.dt.from_np(v.dtype), kind="ExternalInput").ap()
    out = nc.dram_tensor("out_dram", (NB, P, P), F32, kind="ExternalOutput").ap()
    build(nc, d, out)
    return run_bass_kernel_spmd(nc, [arrays], core_ids=[0]).results[0]["out_dram"]
```

```python
from contextlib import ExitStack

import numpy as np

import concourse.bass as bass
from concourse import mybir

F32 = mybir.dt.float32
I32 = mybir.dt.int32
BF16 = mybir.dt.bfloat16
ALU = mybir.AluOpType
ACT = mybir.ActivationFunctionType
AX = mybir.AxisListType

P = 128
NB = 16
NG, GB = 4, 4
BANK = 512
EPS = 1e-5
WEEK, HOUR, DUR, DIFF = (0, 7), (7, 24), (31, 10), (41, 8)
NF = 52
MINUTES = 1440.0
ROUND = 12582912.0
H0, D0 = 8, 64
NT0 = H0 * D0 // P
NREL = 257
E0 = 8
H1, D1 = 8, 16
LH, LD, CH = 4, 16, 64
H2, D2 = 2, 64
E2, FF = 8, 512
NC2 = FF // P


def bounds_by_column():
    lo, hi = np.zeros(49, np.float32), np.zeros(49, np.float32)
    for first, n in (WEEK, DIFF):
        lo[first:first + n] = np.arange(n) - 0.5
        hi[first:first + n] = np.arange(n) + 0.5
    first, n = HOUR
    lo[first:first + n] = 60.0 * np.arange(n) - 0.5
    hi[first:first + n] = 60.0 * np.arange(n) + 59.5
    lo[first], hi[first + n - 1] = -3e38, 3e38
    return lo, hi


def build(nc, d, out):
    ctx = ExitStack()
    with ctx:
        def sb(name, shape, dt=F32):
            return ctx.enter_context(nc.sbuf_tensor(name, shape, dt))

        sems = {}

        def sem(*names):
            for name in names:
                sems[name] = ctx.enter_context(nc.semaphore(name))

        psum = ctx.enter_context(nc.psum_tensor("psum", [P, 8, BANK], F32))
        bank = [psum[:, i, :] for i in range(8)]

        arena = sb("arena", [P, 11024])
        used = {"att0": 0, "att1": 0}

        def carve(part, shape):
            n = int(np.prod(shape))
            view = arena[:, used[part]:used[part] + n]
            used[part] += n
            names = "abcd"[:len(shape)]
            assert used[part] <= 11024
            return view.rearrange(f"p ({' '.join(names)}) -> p {' '.join(names)}", **dict(zip(names, shape))) if len(shape) > 1 else view

        ident = sb("ident", [P, P])
        ids = sb("ids", [NB, 3, P], I32)
        dur = sb("dur", [NB, P])
        tab_l = sb("tab_l", [43, NF])
        tab_r = sb("tab_r", [43, P])
        table = sb("table", [NF, P])
        valT = sb("valT", [P, 6, NB])
        minus_half = sb("minus_half", [P, 8])
        eps = sb("eps", [P, 8])
        h = sb("h", [P, NB, P])
        xT_all = sb("xT_all", [P, NB, P])
        stats = sb("stats", [P, 2, 6])
        mv = sb("mv", [P, 2, 2])
        var_eps = sb("var_eps", [P, 2, 1])
        rstd = sb("rstd", [P, 2, 1])
        xhat = sb("xhat", [P, 2, P])
        wq0 = sb("wq0", [P, H0 * D0])
        wkv0 = sb("wkv0", [P, 2 * H0 * D0])
        wo0 = sb("wo0", [P, NT0, P])
        bo0 = sb("bo0", [P, P])
        relT = sb("relT", [P, NREL])
        relw = sb("relw", [P, 2, P + 7])
        big = sb("big", [P, NB * H0 * P + NB * NT0 * P])
        posT = big[:, 0:NB * H0 * P].rearrange("p (b h n) -> p b h n", b=NB, h=H0)
        qT_all = big[:, NB * H0 * P:].rearrange("p (t b n) -> p t b n", t=NT0, b=NB)
        qTs = carve("att0", [2, NT0, P])
        posTs = carve("att0", [2, H0, P])
        xTs = carve("att0", [2, P])
        kTs = carve("att0", [2, NT0, P])
        vs = sb("vs", [P, 2, H0, D0 + 1])
        negmax = carve("att0", [2, 2, NT0])
        probs = carve("att0", [2, 2, NT0, P])
        probsT = carve("att0", [2, 2, NT0, P])
        rsum = carve("att0", [2, 2, NT0])
        o0 = carve("att0", [2, H0 * D0])
        oT0 = carve("att0", [2, NT0, P])

        qn = arena[:, 4096:6144].rearrange("p (v i t o b) -> p v i t o b", v=2, i=8, t=NT0, o=2)
        val = arena[0:NB, 1024:1792].rearrange("p (f n) -> p f n", f=6)
        tmp = arena[0:NB, 1792:2560].rearrange("p (f n) -> p f n", f=6)
        ln0 = arena[:, 2816:3072].rearrange("p (k n) -> p k n", k=2)
        lohi = arena[:, 3072:3170].rearrange("p (k n) -> p k n", k=2)
        onehotT = arena[0:NF, 0:2 * GB * P].rearrange("p (v n) -> p v n", v=2)
        xhat4 = arena[:, 6144:6144 + 2 * GB * P].rearrange("p (v b n) -> p v b n", v=2, b=GB)
        stats4 = arena[:, 7168:7168 + 12 * NB].rearrange("p (k b c) -> p k b c", k=2, b=NB)
        mv4 = arena[:, 7360:7360 + 4 * NB].rearrange("p (k b c) -> p k b c", k=2, b=NB)
        rstd4 = arena[:, 7424:7424 + 2 * NB].rearrange("p (k b c) -> p k b c", k=2, b=NB)
        above = arena[:, 8192:8192 + NB * NF].rearrange("p (b f) -> p b f", b=NB)
        upto = arena[:, 9216:9216 + NB * NF].rearrange("p (b f) -> p b f", b=NB)
        ysum = arena[:, 9400:9656].rearrange("p (v n) -> p v n", v=2)
        glog = arena[:, 9660:9788].rearrange("p (b e) -> p b e", b=NB)
        g2 = arena[:, 9792:9920].rearrange("p (b e) -> p b e", b=NB)
        top = arena[:, 9984:10496].rearrange("p (k b e) -> p k b e", k=4, b=NB)
        acc = arena[:, 10512:11024].rearrange("p (b n) -> p b n", b=GB)
        w1m = sb("w1m", [P, E0, P])
        w2m = sb("w2m", [P, E0, P])
        b2m = sb("b2m", [P, E0, P])
        gamma = sb("gamma", [P, E0, P])
        beta = sb("beta", [E0, P])
        b1m = sb("b1m", [P, E0])
        wgm = sb("wgm", [P, E0])
        centre = sb("centre", [P, 2, E0])
        iota = sb("iota", [P, E0])
        lgT = big[0:E0, 12288:14336]
        lg = sb("lg", [P, NB, E0])
        tops = sb("tops", [P, 6, NB])
        gates = sb("gates", [P, NB, E0])
        gT = big[0:E0, 4096:6144]
        hid = big[:, 0:2 * E0 * 2 * P].rearrange("p (v e n) -> p v e n", v=2, e=E0)
        work = big[:, 8192:]
        ym = work[:, 0:2048].rearrange("p (v e n) -> p v e n", v=2, e=E0)
        ysq = work[:, 2048:4096].rearrange("p (v e n) -> p v e n", v=2, e=E0)
        yg = work[:, 4096:6144].rearrange("p (v e n) -> p v e n", v=2, e=E0)
        yc = work[:, 6144:8192].rearrange("p (v e n) -> p v e n", v=2, e=E0)
        ysum2 = sb("ysum2", [P, 2, E0])
        yvar = sb("yvar", [P, 2, E0])
        yrstd = sb("yrstd", [P, 2, E0])
        ycoef = sb("ycoef", [P, 2, E0])
        LAT = LH * CH
        wqk1 = sb("wqk1", [P, 4, P])
        wv1 = sb("wv1", [P, P + 1])
        wrv1 = sb("wrv1", [P, LH * LD])
        b1a = sb("b1a", [P, 4])
        rows1 = sb("rows1", [P, H1 + LH])
        qbias = sb("qbias", [P, 2])
        bv1 = sb("bv1", [P, P])
        brv1 = sb("brv1", [P, LH * LD])
        wg1 = sb("wg1", [P, P])
        nbg1 = sb("nbg1", [P, 1])
        valid = sb("valid", [P, 1])
        wroT = sb("wroT", [P, LH * LD + 1])
        wo1 = sb("wo1", [P, P])
        wro1 = sb("wro1", [LH * LD + 1, P])
        bo1 = sb("bo1", [P, P])
        identb = sb("identb", [P, P], BF16)
        maskb = sb("maskb", [P, P + CH], BF16)
        xT1 = carve("att1", [2, P])
        pool1 = carve("att1", [2, 2, CH])
        qT1 = carve("att1", [2, P])
        kT1 = carve("att1", [2, P])
        kx1 = big[:, 9216:11264].rearrange("p (v h n) -> p v h n", v=2, h=H1)
        gkx1 = big[:, 11264:11776].rearrange("p (v h n) -> p v h n", v=2, h=LH)
        rqT1 = carve("att1", [2, P])
        gkT1 = carve("att1", [2, CH])
        nv1, ngv1 = NB * H1 * (D1 + 1), NB * LH * (LD + 1)
        v1 = big[:, 0:nv1].rearrange("p (b h e) -> p b h e", b=NB, h=H1)
        gv1 = big[:, nv1:nv1 + ngv1].rearrange("p (b a o e) -> p b a o e", b=NB, a=2, o=2)
        gx1 = sb("gx1", [P, NB])
        max1 = carve("att1", [2, H1 + LH])
        e1 = big[:, 4096:6656].rearrange("p (v n) -> p v n", v=2)
        pT1 = big[:, 6656:9216].rearrange("p (v n) -> p v n", v=2)
        sum1 = carve("att1", [2, H1 + LH])
        loc1 = carve("att1", [2, P])
        lat1 = carve("att1", [2, LH * LD])
        gw1 = carve("att1", [2, P])
        gd1 = carve("att1", [2, 4])
        cat1 = carve("att1", [2, P + LH * LD + 1])
        catT1 = carve("att1", [2, 2, P])
        wqkv2 = sb("wqkv2", [P, 3 * P])
        wo2 = sb("wo2", [P, P])
        col2 = sb("col2", [P, 4])
        gw2 = sb("gw2", [P, E2])
        gb2 = sb("gb2", [P, E2])
        b1f = sb("b1f", [P, E2, NC2])
        b2f = sb("b2f", [E2, P])
        w1f = big[:, 16384:20480].rearrange("p (e n) -> p e n", e=E2)
        w2f = big[:, 20480:24576].rearrange("p (e f n) -> p e f n", e=E2, f=NC2)
        xT2 = carve("att1", [2, P])
        sq2 = carve("att1", [2, 2 * P])
        ss2 = carve("att1", [2, 2 * H2])
        rn2 = carve("att1", [2, 2 * H2])
        qk2 = carve("att1", [2, 2 * P])
        v2 = big[:, 12288:12288 + NB * H2 * (D2 + 1)].rearrange("p (b h e) -> p b h e", b=NB, h=H2)
        qkT2 = carve("att1", [2, 2, P])
        max2 = carve("att1", [2, H2])
        p2 = carve("att1", [2, H2, P])
        pT2 = carve("att1", [2, H2, P])
        sum2 = carve("att1", [2, H2])
        o2 = carve("att1", [2, P])
        oT2 = carve("att1", [2, P])
        yT2 = carve("att1", [2, P])
        yT_all = xT_all
        gsum = sb("gsum", [P, 2, NB])
        g2T = big[0:E2, 12288:14336]
        hidf = big[:, 0:4096].rearrange("p (v f n) -> p v f n", v=2, f=NC2)

        sem("ld_moe0", "ld_att1", "ld_att2", "ld_moe1", "centred", "lgT_psum", "lgT", "lg_psum", "tops",
            "topexp", "gates", "gT_psum", "gT", "beta_psum", "h_beta", "hid_psum", "hid", "y_psum", "ym", "ysq", "yvar",
            "yrstd", "ycoef", "yg", "yc", "ysum", "h_moe0", "ready1", "wro_psum", "wro1", "xT1", "pool1", "proj1_psum",
            "v1_psum", "k1", "kx1", "v1", "s1_psum", "max1", "sub1", "e1", "pT1_psum", "latT_psum", "pT1", "latT1", "o1_psum",
            "rsum1", "o1", "gd1", "ge1", "gate1a", "gate1b", "gate1", "cat1", "catT1_psum", "catT1", "y1_psum",
            "y1_added", "h1")
        sem("xT2", "qkv2_psum", "sq2", "ss2", "ss2e", "rn2", "qk2", "qkT2_psum", "qkT2", "s2_psum", "max2", "p2",
            "pT2_psum", "pT2", "o2_psum", "rsum2", "o2", "oT2_psum", "oT2", "yT2_psum", "yT2", "yT_all", "gl2_psum",
            "gl2", "act4", "chain4", "g2", "g2T_psum", "g2T", "b2_psum", "acc0", "hf_psum", "hf", "eo_psum", "acc",
            "out_acc")
        sem("ld_tok", "ld_const", "ld_att0", "chain", "trig_in", "log_in", "trig", "log", "val_ready", "valT_psum",
            "table_psum", "table_ready", "onehot", "onehotT_psum", "onehotT", "tok_psum", "tok_stats", "tok_mv",
            "tok_var", "tok_rstd", "tok_xhat", "tok_scaled", "tok_h", "const_ready", "vs_ones", "ln_stats", "ln_mv",
            "ln_var", "ln_rstd", "ln_xhat", "ln_xT_psum", "ln_xT", "q_psum", "q_all", "relw", "qn_even", "qn_odd", "pos_psum",
            "pos_first", "pos_second", "att0_in0", "att0_in1", "k0_psum", "k0", "v0_psum", "v0", "s0_psum", "negmax0", "p0",
            "pT0_psum", "pT0", "o0_psum", "rsum0", "o0", "oT0_psum", "oT0", "y0_psum", "y0_added", "h0", "stored",
            "waited_pe", "waited_dve")
        g = sems

        def steps(eng, lag, step, n=NB):
            first = (lag + 3) // 2
            for t in range(2 * first):
                step(t, t // 2, t % 2)
            with eng.Fori(first, n // 2) as j:
                for u in range(2):
                    step(2 * j + u, j, u)
            for t in range(n, n + lag):
                step(t, t // 2, t % 2)

        def live(t, k, n=NB):
            return not isinstance(t, int) or 0 <= t - k < n

        def later(b, n):
            return not isinstance(b, int) or b >= n

        def apart(eng):
            eng.sem_inc(g["waited_" + ("pe" if eng is nc.tensor else "dve")], 1)

        with nc.Block() as block:

            @block.sync
            def _(sp):
                for i, name in enumerate(("x", "itok_BS_0_1439", "itok_BS_0_7")):
                    sp.dma_start(ids[:, i, :], d[name]).then_inc(g["ld_tok"], 16)
                sp.dma_start(dur[:], d["fside_BS_durations"]).then_inc(g["ld_tok"], 16)
                sp.dma_start(ident[:], d["ident"]).then_inc(g["ld_const"], 16)
                sp.dma_start(lohi.rearrange("p a b -> p (a b)"), d["bounds"].partition_broadcast(P)).then_inc(g["ld_const"], 16)
                sp.dma_start(tab_l[:], d["tab_l"]).then_inc(g["ld_const"], 16)
                sp.dma_start(tab_r[:], d["tab_r"]).then_inc(g["ld_const"], 16)
                sp.dma_start(ln0[:, 0, :], d["L0_tok_ln_w"].partition_broadcast(P)).then_inc(g["ld_const"], 16)
                sp.dma_start(ln0[:, 1, :], d["L0_tok_ln_b"].partition_broadcast(P)).then_inc(g["ld_const"], 16)
                sp.dma_start(wq0[:], d["L0_attn_Wq"]).then_inc(g["ld_att0"], 16)
                sp.dma_start(relT[:], d["relT"]).then_inc(g["ld_att0"], 16)
                sp.dma_start(wkv0[:], d["L0_attn_Wkv"]).then_inc(g["ld_att0"], 16)
                sp.dma_start(wo0[:], d["L0_attn_Wo"].rearrange("(t p) n -> p t n", p=P)).then_inc(g["ld_att0"], 16)
                sp.dma_start(bo0[:], d["L0_attn_bo"].partition_broadcast(P)).then_inc(g["ld_att0"], 16)

                for dst, name in ((w1m[:], "w1m"), (w2m[:], "w2m"), (b2m[:].rearrange("p e n -> p (e n)"), "L0_ffn_b2"),
                                  (gamma[:].rearrange("p e n -> p (e n)"), "L0_ffn_gamma"), (beta[:], "L0_ffn_beta"), (b1m[:], "b1m"),
                                  (wgm[:], "L0_ffn_Wg"), (iota[:], "iota")):
                    src = d[name].partition_broadcast(P) if name in ("L0_ffn_b2", "L0_ffn_gamma", "iota") else d[name]
                    sp.dma_start(dst, src).then_inc(g["ld_moe0"], 16)
                for dst, name in ((wqk1[:], "wqk1"), (wv1[:], "wv1"), (wrv1[:], "L1_attn_Wrv"), (b1a[:], "b1a"), (rows1[:], "rows1"),
                                  (bv1[:], "L1_attn_bv"), (brv1[:], "L1_attn_brv"), (wg1[:], "wg1"), (nbg1[:], "L1_attn_bg"),
                                  (valid[:], "valid"), (wroT[:], "wroT"), (wo1[:], "L1_attn_Wo"), (bo1[:], "L1_attn_bo"),
                                  (identb[:], "identb"), (maskb[:], "maskb")):
                    src = d[name].partition_broadcast(P) if name in ("L1_attn_bv", "L1_attn_brv", "wg1", "L1_attn_bg", "L1_attn_bo") else d[name]
                    sp.dma_start(dst, src).then_inc(g["ld_att1"], 16)
                for dst, name in ((wqkv2[:], "wqkv2"), (wo2[:], "L1_ffn_Wo"), (col2[:], "col2"), (gw2[:], "L1_ffn_gate_W"),
                                  (gb2[:], "L1_ffn_gate_b")):
                    src = d[name].partition_broadcast(P) if name == "L1_ffn_gate_b" else d[name]
                    sp.dma_start(dst, src).then_inc(g["ld_att2"], 16)

                sp.wait_ge(g["pos_first"], NB)
                sp.wait_ge(g["pos_second"], NB)

                def step(t, j, u):
                    if live(t, 0):
                        if later(t, 2):
                            sp.wait_ge(g["s0_psum"], t - 1)
                            sp.wait_ge(g["v0_psum"], t - 1)
                        arrived = g[f"att0_in{u}"]
                        sp.dma_start(xTs[:, u, :], xT_all[:, t, :]).then_inc(arrived, 16)
                        sp.dma_start(qTs[:, u], qT_all[:, :, t, :]).then_inc(arrived, 16)
                        sp.dma_start(posTs[:, u], posT[:, t]).then_inc(arrived, 16)
                steps(sp, 0, step)

                sp.wait_ge(g["s0_psum"], NB)
                for dst, name in ((b1f[:], "b1f"), (b2f[:], "L1_ffn_b2"), (w1f, "w1f"), (w2f, "w2f")):
                    sp.dma_start(dst, d[name]).then_inc(g["ld_moe1"], 16)

                sp.wait_ge(g["ld_moe1"], 64)
                sp.wait_ge(g["ld_att1"], 240)
                sp.wait_ge(g["ld_att2"], 80)

                def store(grp):
                    sp.wait_ge(g["out_acc"], grp + 1)
                    sp.dma_start(out[bass.ds(GB * grp, GB)].rearrange("b p n -> p b n"), acc[:]).then_inc(g["stored"], 16)
                store(0)
                with sp.Fori(1, NG) as grp:
                    store(grp)
                sp.wait_ge(g["stored"], 16 * NG)

            @block.gpsimd
            def _(pool):
                pool.memset(arena[:, 4096:6144], 0.0)
                pool.memset(minus_half[:], -0.5).then_inc(g["const_ready"], 1)
                pool.memset(eps[:, 0:1], EPS)
                pool.memset(eps[:, 1:2], 1.0 + EPS)
                pool.memset(eps[:, 2:3], EPS * EPS)
                pool.memset(eps[:, 4:8], 1e-12).then_inc(g["const_ready"], 1)
                pool.memset(above[:, :, 51:52], 1.0).then_inc(g["const_ready"], 1)
                pool.memset(upto[:, :, 49:52], 1.0).then_inc(g["const_ready"], 1)
                pool.memset(vs[:, :, :, D0:D0 + 1], 1.0).then_inc(g["vs_ones"], 1)
                pool.wait_ge(g["const_ready"], 4)

                def ln_rstd(phase, b, v):
                    n = NB * phase + b + 1
                    pool.wait_ge(g["ln_mv"], n)
                    pool.tensor_tensor(var_eps[:, v], mv[:, v, 1:2], eps[:, 0:1], ALU.add).then_inc(g["ln_var"], 1)
                    pool.wait_ge(g["ln_var"], n)
                    pool.tensor_tensor(rstd[:, v], var_eps[:, v], minus_half[:, 0:1], ALU.pow).then_inc(g["ln_rstd"], 1)

                def rstd_of(k, grp, summed, done):
                    span = slice(GB * grp, GB * grp + GB)
                    pool.tensor_tensor(rstd4[:, k, span], mv4[:, k, span, 1:2], eps[:, 0:1].unsqueeze(1).to_broadcast([P, GB, 1]),
                                       ALU.add).then_inc(g[summed], GB)
                    pool.wait_ge(g[summed], GB * grp + GB)
                    pool.tensor_tensor(rstd4[:, k, span], rstd4[:, k, span], minus_half[:, 0:GB].unsqueeze(2), ALU.pow).then_inc(g[done], GB)

                for t in range(NG + 1):
                    if t >= 1:
                        pool.wait_ge(g["ln_mv"], GB * t)
                        rstd_of(1, t - 1, "ln_var", "ln_rstd")
                    if t < NG:
                        pool.wait_ge(g["tok_mv"], GB * t + GB)
                        rstd_of(0, t, "tok_var", "tok_rstd")

                pool.wait_ge(g["ld_att0"], 80)
                def window(c, u):
                    if later(c, 2):
                        pool.wait_ge(g["pos_psum"], c - 1)
                    pool.tensor_copy(relw[:, u, :], relT[:, bass.ds(P - 7 - 8 * c, P + 7)]).then_inc(g["relw"], 1)
                for c in range(2):
                    window(c, c)
                with pool.Fori(1, NB // 2) as j:
                    for u in range(2):
                        window(2 * j + u, u)

                def att0(t, j, u):
                    if live(t, 3):
                        ln_rstd(1, t - 3, 1 - u)
                steps(pool, 4, att0)

                def moe0(t, j, u):
                    if live(t, 1):
                        b, v = t - 1, 1 - u
                        pool.wait_ge(g["yvar"], b + 1)
                        if later(b, 2):
                            pool.wait_ge(g["ycoef"], b - 1)
                        pool.tensor_tensor(yrstd[:, v], yvar[:, v], minus_half[:], ALU.pow).then_inc(g["yrstd"], 1)
                    if live(t, 0):
                        pool.wait_ge(g["ym"], t + 1)
                        if later(t, 2):
                            pool.wait_ge(g["yc"], t - 1)
                        pool.tensor_tensor(yg[:, u], ym[:, u], gamma[:], ALU.mult).then_inc(g["yg"], 1)
                steps(pool, 1, moe0)

                pool.wait_ge(g["y_psum"], NB)
                pool.memset(gv1, 0.0)
                pool.wait_ge(g["h_moe0"], NB)
                pool.memset(v2[:, :, :, D2:D2 + 1], 1.0)
                pool.memset(v1[:, :, :, D1:D1 + 1], 1.0).then_inc(g["vs_ones"], 1)
                for odd in range(2):
                    pool.wait_ge(g["vs_ones"], 2 + odd)
                    pool.memset(gv1[CH * odd:CH * odd + CH, :, :, odd, LD:LD + 1], 1.0).then_inc(g["vs_ones"], 1)

                def att1(t, j, u):
                    if live(t, 0):
                        ln_rstd(2, t, u)
                    if live(t, 1):
                        b, v = t - 1, 1 - u
                        pool.wait_ge(g["k1"], b + 1)
                        if later(b, 2):
                            pool.wait_ge(g["s1_psum"], b - 1)
                        pool.tensor_tensor(kx1[:, v], kT1[:, v, :].unsqueeze(1).to_broadcast([P, H1, P]),
                                           rows1[:, 0:H1].unsqueeze(2).to_broadcast([P, H1, P]), ALU.mult)
                        pool.tensor_tensor(gkx1[:, v], gkT1[:, v, :].unsqueeze(1).to_broadcast([P, LH, CH]),
                                           rows1[:, H1:].unsqueeze(2).to_broadcast([P, LH, CH]), ALU.mult).then_inc(g["kx1"], 1)
                    if live(t, 0):
                        pool.wait_ge(g["xT1"], t + 1)
                        if later(t, 2):
                            pool.wait_ge(g["v1_psum"], t - 1)
                        pairs = xT1[:, u, :].rearrange("p (c o) -> p c o", o=2)
                        for i in range(2):
                            last = pool.tensor_tensor(pool1[:, u, i, :].unsqueeze(2), pairs[:, :, 0:1], pairs[:, :, 1:2], ALU.add)
                        last.then_inc(g["pool1"], 1)
                steps(pool, 1, att1)

                def att2(t, j, u):
                    if live(t, 2):
                        b, v = t - 2, u
                        pool.wait_ge(g["ss2"], b + 1)
                        if later(b, 2):
                            pool.wait_ge(g["qk2"], b - 1)
                        pool.tensor_tensor(rn2[:, v], ss2[:, v], eps[:, 4:8], ALU.add).then_inc(g["ss2e"], 1)
                        pool.wait_ge(g["ss2e"], b + 1)
                        pool.tensor_tensor(rn2[:, v], rn2[:, v], minus_half[:, 0:4], ALU.pow).then_inc(g["rn2"], 1)
                    if live(t, 0):
                        n = 3 * NB + t + 1
                        pool.wait_ge(g["ln_mv"], n)
                        pool.tensor_tensor(var_eps[:, u], mv[:, u, 1:2], eps[:, 1:2], ALU.mult).then_inc(g["ln_var"], 1)
                        pool.wait_ge(g["ln_var"], 3 * NB + 2 * t + 1)
                        pool.tensor_tensor(var_eps[:, u], var_eps[:, u], eps[:, 2:3], ALU.add).then_inc(g["ln_var"], 1)
                        pool.wait_ge(g["ln_var"], 3 * NB + 2 * t + 2)
                        pool.tensor_tensor(rstd[:, u], var_eps[:, u], minus_half[:, 0:1], ALU.pow).then_inc(g["ln_rstd"], 1)
                steps(pool, 2, att2)

            @block.scalar
            def _(act):
                act.wait_ge(g["log_in"], 1)
                act.activation(tmp[:, 1, :], tmp[:, 0, :], ACT.Ln).then_inc(g["log"], 1)
                act.wait_ge(g["trig_in"], 1)
                act.activation(val[:, 4:6, :], tmp[:, 4:6, :], ACT.Sin).then_inc(g["trig"], 1)
                act.wait_ge(g["table_psum"], 1)
                act.activation(table[:], bank[1][0:NF, 0:P], ACT.Copy).then_inc(g["table_ready"], 1)

                for t in range(NG + 2):
                    if t < NG:
                        act.wait_ge(g["onehotT_psum"], t + 1)
                        if t >= 2:
                            act.wait_ge(g["tok_psum"], t - 1)
                        act.activation(onehotT[:, t % 2, :], bank[t % 2][0:NF, :], ACT.Copy).then_inc(g["onehotT"], 1)
                    if t >= 2:
                        grp = t - 2
                        span = slice(GB * grp, GB * grp + GB)
                        act.wait_ge(g["ln_xT_psum"], GB * grp + GB)
                        act.activation(xT_all[:, span, :], bank[4 + grp % 2], ACT.Copy).then_inc(g["ln_xT"], GB)
                        for tile in range(NT0):
                            act.wait_ge(g["q_psum"], NT0 * grp + tile + 1)
                            act.activation(qT_all[:, tile, span, :], bank[6 + tile % 2], ACT.Copy, scale=float(D0) ** -0.5).then_inc(g["q_all"], 1)

                def pos(t, j, u):
                    if live(t, 0):
                        if later(t, 2):
                            act.wait_ge(g["pos_psum"], t - 1)
                        act.activation(qn[0:64, u, :, :, 0, :], qT_all[0:64, :, :, bass.ds(8 * t, 8)].rearrange("p t b i -> p i t b"), ACT.Copy).then_inc(g["qn_even"], 1)
                    if live(t, 1):
                        c, v = t - 1, 1 - u
                        act.wait_ge(g["pos_psum"], c + 1)
                        act.activation(posT[:, :, :, bass.ds(8 * c, 4)], bank[2 * v].rearrange("p (i h b) -> p b h i", i=4, h=H0), ACT.Copy).then_inc(g["pos_first"], 1)
                act.wait_ge(g["q_all"], NG * NT0)
                steps(act, 1, pos)

                def att0(t, j, u):
                    if live(t, 3):
                        b, v = t - 3, 1 - u
                        act.wait_ge(g["oT0_psum"], b + 1)
                        if later(b, 2):
                            act.wait_ge(g["y0_psum"], b - 1)
                        act.activation(oT0[:, v], bank[0].rearrange("p (t n) -> p t n", t=NT0), ACT.Copy).then_inc(g["oT0"], 1)
                    if live(t, 1):
                        b, v = t - 1, 1 - u
                        act.wait_ge(g["negmax0"], b + 1)
                        if later(b, 2):
                            act.wait_ge(g["pT0_psum"], b - 1)
                        for odd in range(2):
                            for tile in range(NT0):
                                e = act.activation(probs[:, v, odd, tile, :], bank[2 + odd][:, tile * P:(tile + 1) * P],
                                                   ACT.Exp, bias=negmax[:, v, odd, tile:tile + 1])
                        e.then_inc(g["p0"], 1)
                    if live(t, 4):
                        b = t - 4
                        act.wait_ge(g["ln_xT_psum"], NB + b + 1)
                        act.activation(xT_all[:, b, :], bank[7][:, 3 * P:], ACT.Copy).then_inc(g["ln_xT"], 1)
                    if live(t, 0):
                        act.wait_ge(g["k0_psum"], t + 1)
                        if later(t, 2):
                            act.wait_ge(g["s0_psum"], t - 1)
                        act.activation(kTs[:, u], bank[0].rearrange("p (t n) -> p t n", t=NT0), ACT.Copy).then_inc(g["k0"], 1)
                steps(act, 4, att0)

                act.wait_ge(g["lgT_psum"], 1)
                act.activation(lgT.rearrange("p (a n) -> p a n", a=NG), psum[0:E0, 2:6, :], ACT.Copy).then_inc(g["lgT"], 1)
                act.wait_ge(g["tops"], 1)
                act.activation(tops[:, 4, :], tops[:, 3, :], ACT.Exp).then_inc(g["topexp"], 1)
                act.wait_ge(g["ld_moe0"], 128)

                def moe0(t, j, u):
                    for half in range(2):
                        if live(t, 0, NB // 2):
                            for pair in (2 * half, 2 * half + 1):
                                act.wait_ge(g["hid_psum"], 4 * t + pair + 1)
                                if pair == 0 and later(t, 2):
                                    act.wait_ge(g["y_psum"], 2 * t - 2)
                                for e in (2 * pair, 2 * pair + 1):
                                    last = act.activation(hid[:, u, e, :], bank[pair % 2][:, e % 2 * 2 * P:(e % 2 + 1) * 2 * P], ACT.Relu,
                                                          bias=b1m[:, e:e + 1])
                                last.then_inc(g["hid"], 1)
                        if live(t, 1, NB // 2):
                            b = 2 * t - 2 + half
                            act.wait_ge(g["ym"], b + 1)
                            if later(t, 2):
                                act.wait_ge(g["yvar"], b - 1)
                            for e in range(E0):
                                last = act.activation(ysq[:, half, e], ym[:, half, e], ACT.Square, accum_out=ysum2[:, half, e:e + 1])
                            last.then_inc(g["ysq"], 1)
                steps(act, 1, moe0, NB // 2)
                act.wait_ge(g["gT_psum"], 1)
                for a in range(NG):
                    last = act.activation(gT[:, a * GB * P:(a + 1) * GB * P], bank[(0, 1, 6, 7)[a]][0:E0, :], ACT.Copy)
                last.then_inc(g["gT"], 1)

                act.wait_ge(g["ready1"], 1)
                act.wait_ge(g["wro_psum"], 1)
                act.activation(wro1[:], bank[0][0:LH * LD + 1, 0:P], ACT.Copy).then_inc(g["wro1"], 1)

                def att1(t, j, u):
                    if live(t, 1):
                        b, v = t - 1, 1 - u
                        act.wait_ge(g["proj1_psum"], b + 1)
                        if later(b, 2):
                            act.wait_ge(g["s1_psum"], b - 1)
                        act.activation(qT1[:, v, :], bank[0][:, 0:P], ACT.Identity, scale=float(D1) ** -0.5, bias=qbias[:, 0:1])
                        act.activation(kT1[:, v, :], bank[0][:, P:2 * P], ACT.Identity, bias=b1a[:, 1:2])
                        act.activation(rqT1[:, v, :], bank[0][:, 2 * P:3 * P], ACT.Identity, scale=float(LD) ** -0.5, bias=qbias[:, 1:2])
                        act.activation(gkT1[:, v, :], bank[0][:, 3 * P:3 * P + CH], ACT.Identity, scale=0.5, bias=b1a[:, 3:4]).then_inc(g["k1"], 1)
                    if live(t, 5):
                        b, v = t - 5, 1 - u
                        act.wait_ge(g["catT1_psum"], b + 1)
                        if later(b, 2):
                            act.wait_ge(g["y1_psum"], b - 1)
                        act.activation(catT1[:, v, 0, :], bank[0][:, 0:P], ACT.Copy)
                        act.activation(catT1[0:LH * LD + 1, v, 1, :], bank[0][0:LH * LD + 1, P:2 * P], ACT.Copy).then_inc(g["catT1"], 1)
                    if live(t, 3):
                        b, v = t - 3, 1 - u
                        act.wait_ge(g["pT1_psum"], b + 1)
                        if later(b, 2):
                            act.wait_ge(g["o1_psum"], b - 1)
                        act.activation(pT1[:, v, 0:H1 * P], psum[:, 6:8, :].rearrange("p a c -> p (a c)"), ACT.Copy).then_inc(g["pT1"], 1)
                        act.wait_ge(g["latT_psum"], b + 1)
                        if live(t, 0):
                            act.wait_ge(g["ln_xT_psum"], 2 * NB + t + 1)
                        act.activation(pT1[:, v, H1 * P:], bank[1][:, 0:LAT], ACT.Copy).then_inc(g["latT1"], 1)
                    if live(t, 0):
                        act.wait_ge(g["ln_xT_psum"], 2 * NB + t + 1)
                        if later(t, 2):
                            act.wait_ge(g["v1_psum"], t - 1)
                        act.activation(xT1[:, u, :], bank[1][:, LAT:LAT + P], ACT.Copy).then_inc(g["xT1"], 1)
                    if live(t, 2):
                        b, v = t - 2, u
                        act.wait_ge(g["sub1"], b + 1)
                        act.activation(e1[:, v, :], e1[:, v, :], ACT.Exp).then_inc(g["e1"], 1)
                    if live(t, 4):
                        b, v = t - 4, u
                        act.wait_ge(g["gd1"], b + 1)
                        act.activation(gd1[:, v, 1:2], gd1[:, v, 0:1], ACT.Exp, scale=-1.0, bias=nbg1[:]).then_inc(g["ge1"], 1)
                steps(act, 5, att1)

                def att2(t, j, u):
                    if live(t, 6):
                        b, v = t - 6, u
                        act.wait_ge(g["yT2_psum"], b + 1)
                        if later(b, 2):
                            act.wait_ge(g["gl2_psum"], b - 1)
                        act.activation(yT2[:, v, :], bank[6][:, 0:P], ACT.Copy).then_inc(g["yT2"], 1)
                        act.activation(yT_all[:, b, :], bank[6][:, 0:P], ACT.Copy).then_inc(g["yT_all"], 1)
                    if live(t, 4):
                        b, v = t - 4, u
                        act.wait_ge(g["max2"], b + 1)
                        if later(b, 2):
                            act.wait_ge(g["pT2_psum"], b - 1)
                        for hd in range(H2):
                            last = act.activation(p2[:, v, hd, :], bank[2 + hd][:, 0:P], ACT.Exp, bias=max2[:, v, hd:hd + 1])
                        last.then_inc(g["p2"], 1)
                    if live(t, 3):
                        act.wait_ge(g["qkT2_psum"], t - 2)
                    if live(t, 1):
                        b, v = t - 1, 1 - u
                        act.wait_ge(g["ln_xT_psum"], 3 * NB + b + 1)
                        if later(b, 2):
                            act.wait_ge(g["qkv2_psum"], b - 1)
                        act.activation(xT2[:, v, :], bank[1][:, 2 * P:3 * P], ACT.Identity, scale=col2[:, 0:1], bias=col2[:, 1:2]).then_inc(g["xT2"], 1)
                    if live(t, 3):
                        b, v = t - 3, 1 - u
                        if later(b, 2):
                            act.wait_ge(g["s2_psum"], b - 1)
                        for i in range(2):
                            last = act.activation(qkT2[:, v, i, :], bank[1][:, i * P:(i + 1) * P], ACT.Identity, scale=col2[:, 2 + i:3 + i])
                        last.then_inc(g["qkT2"], 1)
                    if live(t, 5):
                        b, v = t - 5, 1 - u
                        act.wait_ge(g["oT2_psum"], b + 1)
                        if later(b, 2):
                            act.wait_ge(g["yT2_psum"], b - 1)
                        act.activation(oT2[:, v, :], bank[6][:, 0:P], ACT.Copy).then_inc(g["oT2"], 1)
                    if live(t, 1):
                        b, v = t - 1, 1 - u
                        act.wait_ge(g["qkv2_psum"], b + 1)
                        if later(b, 2):
                            act.wait_ge(g["ss2"], b - 1)
                        act.activation(sq2[:, v, :], bank[7 * (1 - u)][:, 0:2 * P], ACT.Square).then_inc(g["sq2"], 1)
                steps(act, 6, att2)
                act.wait_ge(g["chain4"], 2)
                act.activation(g2, glog, ACT.Exp).then_inc(g["act4"], 1)
                act.wait_ge(g["g2T_psum"], 1)
                act.activation(g2T.rearrange("p (a n) -> p a n", a=NG), psum[0:E2, 2:6, :], ACT.Copy).then_inc(g["g2T"], 1)

                def hiddenf(grp):
                    for e in range(E2):
                        for f in range(NC2):
                            act.wait_ge(g["hf_psum"], FF // P * (E2 * grp + e) + f + 1)
                            if f == 0 and (e >= 2 or later(grp, 1)):
                                act.wait_ge(g["eo_psum"], E2 * grp + e - 1)
                            act.activation(hidf[:, e % 2, f, :], bank[f], ACT.Gelu_apprx_tanh, bias=b1f[:, e, f:f + 1]).then_inc(g["hf"], 1)
                hiddenf(0)
                with act.Fori(1, NG) as grp:
                    hiddenf(grp)

            @block.vector
            def _(dve):
                chained = [0]

                def link(ins):
                    chained[0] += 1
                    ins.then_inc(g["chain"], 1)
                    dve.wait_ge(g["chain"], chained[0])

                dve.wait_ge(g["ld_tok"], 64)
                link(dve.tensor_scalar(tmp[:, 2, :], dur[:], -1.0, None, ALU.max))
                link(dve.tensor_scalar(tmp[:, 3, :], tmp[:, 2, :], 1.0, None, ALU.add))
                dve.tensor_scalar(tmp[:, 0, :], tmp[:, 3, :], 2.0 ** -64, 2.0 ** 64, ALU.max, ALU.min).then_inc(g["log_in"], 1)
                dve.tensor_copy(val[:, 0:2, :], ids[:, 0:2, :])
                link(dve.tensor_copy(val[:, 3, :], ids[:, 2, :]))
                link(dve.tensor_scalar(tmp[:, 5, :], val[:, 1, :], 1.0 / MINUTES, ROUND, ALU.mult, ALU.add))
                link(dve.tensor_scalar(tmp[:, 5, :], tmp[:, 5, :], ROUND, -MINUTES, ALU.subtract, ALU.mult))
                link(dve.tensor_tensor(tmp[:, 5, :], tmp[:, 5, :], val[:, 1, :], ALU.add))
                link(dve.tensor_scalar(tmp[:, 5, :], tmp[:, 5, :], 2.0 * np.pi / MINUTES, None, ALU.mult))
                link(dve.tensor_scalar(tmp[:, 4, :], tmp[:, 5, :], 3.1415925, -3.1415925, ALU.min, ALU.max))
                link(dve.scalar_tensor_tensor(tmp[:, 5, :], tmp[:, 5, :], -1.0, tmp[:, 5, :], ALU.mult, ALU.max))
                dve.tensor_scalar(tmp[:, 5, :], tmp[:, 5, :], -1.0, np.pi / 2, ALU.mult, ALU.add).then_inc(g["trig_in"], 1)
                link(dve.tensor_scalar(tmp[:, 3, :], tmp[:, 3, :], -1.0, None, ALU.add))
                link(dve.tensor_scalar(val[:, 2, :], tmp[:, 3, :], 0.0, None, ALU.is_equal))
                link(dve.tensor_tensor(tmp[:, 3, :], tmp[:, 3, :], val[:, 2, :], ALU.add))
                link(dve.reciprocal(tmp[:, 3, :], tmp[:, 3, :]))
                link(dve.tensor_tensor(tmp[:, 3, :], tmp[:, 3, :], tmp[:, 2, :], ALU.mult))
                link(dve.tensor_tensor(val[:, 2, :], val[:, 2, :], tmp[:, 2, :], ALU.mult))
                dve.wait_ge(g["log"], 1)
                link(dve.tensor_tensor(tmp[:, 3, :], tmp[:, 3, :], tmp[:, 1, :], ALU.mult))
                link(dve.tensor_tensor(val[:, 2, :], val[:, 2, :], tmp[:, 3, :], ALU.add))
                link(dve.tensor_scalar(tmp[:, 3, :], dur[:], -1.0, 1e30, ALU.is_lt, ALU.mult))
                dve.tensor_tensor(val[:, 2, :], val[:, 2, :], tmp[:, 3, :], ALU.add).then_inc(g["val_ready"], 1)
                dve.wait_ge(g["valT_psum"], 1)
                link(dve.tensor_copy(valT[:], bank[0][:, 0:6 * NB].rearrange("p (f b) -> p f b", f=6)))
                dve.wait_ge(g["ld_const"], 96)
                dve.wait_ge(g["const_ready"], 4)
                for f, (first, n) in enumerate((WEEK, HOUR, DUR, DIFF)):
                    value = valT[:, f, :].unsqueeze(2).to_broadcast([P, NB, n])
                    for dst, side, op in ((above, 0, ALU.is_gt), (upto, 1, ALU.is_le)):
                        limit = lohi[:, side, first:first + n].unsqueeze(1).to_broadcast([P, NB, n])
                        dve.tensor_tensor(dst[:, :, first:first + n], value, limit, op)
                link(dve.tensor_copy(above[:, :, 49:51], valT[:, 4:6, :].rearrange("p f b -> p b f")))

                def ln_stats(phase, b, v):
                    n = NB * phase + b + 1
                    apart(dve)
                    dve.bn_stats(stats[:, v, :], h[:, b, :]).then_inc(g["ln_stats"], 1)
                    dve.wait_ge(g["ln_stats"], n)
                    apart(dve)
                    dve.bn_aggr(mv[:, v, :], stats[:, v, :]).then_inc(g["ln_mv"], 1)

                def ln_xhat(phase, b, v):
                    n = NB * phase + b + 1
                    dve.wait_ge(g["ln_rstd"], n)
                    if phase or later(b, 2):
                        dve.wait_ge(g["ln_xT_psum"], n - 2)
                    dve.tensor_scalar(xhat[:, v, :], h[:, b, :], mv[:, v, 0:1], rstd[:, v], ALU.subtract, ALU.mult).then_inc(g["ln_xhat"], 1)

                dve.tensor_tensor(above, above, upto, ALU.mult).then_inc(g["onehot"], 1)

                def stats_of(k, grp, source, summed, done):
                    apart(dve)
                    for b in range(GB):
                        dve.bn_stats(stats4[:, k, GB * grp + b, :], source(b)).then_inc(g[summed], 1)
                    dve.wait_ge(g[summed], GB * grp + GB)
                    apart(dve)
                    for b in range(GB):
                        last = dve.bn_aggr(mv4[:, k, GB * grp + b, :], stats4[:, k, GB * grp + b, :])
                    last.then_inc(g[done], GB)

                for t in range(NG + 2):
                    if t >= 2:
                        grp = t - 2
                        dve.wait_ge(g["ln_rstd"], GB * grp + GB)
                        if grp >= 2:
                            dve.wait_ge(g["ln_xT_psum"], GB * grp - GB)
                        for b in range(GB):
                            n = GB * grp + b
                            last = dve.tensor_scalar(xhat4[:, grp % 2, b, :], h[:, n, :], mv4[:, 1, n, 0:1], rstd4[:, 1, n], ALU.subtract, ALU.mult)
                        last.then_inc(g["ln_xhat"], GB)
                    if 1 <= t <= NG:
                        grp = t - 1
                        rows = h[:, GB * grp:GB * grp + GB, :]
                        dve.wait_ge(g["tok_rstd"], GB * grp + GB)
                        for b in range(GB):
                            n = GB * grp + b
                            last = dve.tensor_scalar(h[:, n, :], bank[2 + grp % 2][:, b * P:(b + 1) * P], mv4[:, 0, n, 0:1], rstd4[:, 0, n],
                                                     ALU.subtract, ALU.mult)
                        last.then_inc(g["tok_xhat"], 1)
                        dve.wait_ge(g["tok_xhat"], grp + 1)
                        dve.tensor_tensor(rows, rows, ln0[:, 0, :].unsqueeze(1).to_broadcast([P, GB, P]), ALU.mult).then_inc(g["tok_scaled"], 1)
                        dve.wait_ge(g["tok_scaled"], grp + 1)
                        dve.tensor_tensor(rows, rows, ln0[:, 1, :].unsqueeze(1).to_broadcast([P, GB, P]), ALU.add).then_inc(g["tok_h"], 1)
                        dve.wait_ge(g["tok_h"], grp + 1)
                        stats_of(1, grp, lambda b: h[:, GB * grp + b, :], "ln_stats", "ln_mv")
                    if t < NG:
                        dve.wait_ge(g["tok_psum"], t + 1)
                        stats_of(0, t, lambda b: bank[2 + t % 2][:, b * P:(b + 1) * P], "tok_stats", "tok_mv")


                def pos(t, j, u):
                    if live(t, 0):
                        if later(t, 2):
                            dve.wait_ge(g["pos_psum"], t - 1)
                        dve.tensor_copy(qn[64:P, u, :, :, 1, :], qT_all[64:P, :, :, bass.ds(8 * t, 8)].rearrange("p t b i -> p i t b")).then_inc(g["qn_odd"], 1)
                    if live(t, 1):
                        c, v = t - 1, 1 - u
                        dve.wait_ge(g["pos_psum"], c + 1)
                        dve.tensor_copy(posT[:, :, :, bass.ds(8 * c + 4, 4)], bank[2 * v + 1].rearrange("p (i h b) -> p b h i", i=4, h=H0)).then_inc(g["pos_second"], 1)
                dve.wait_ge(g["q_all"], NG * NT0)
                steps(dve, 1, pos)

                dve.wait_ge(g["ld_att0"], 80)
                dve.wait_ge(g["vs_ones"], 1)

                def att0(t, j, u):
                    if live(t, 4):
                        ln_xhat(1, t - 4, u)
                    if live(t, 1):
                        b, v = t - 1, 1 - u
                        dve.wait_ge(g["s0_psum"], b + 1)
                        dve.tensor_reduce(negmax[:, v], psum[:, 2:4, :].rearrange("p a (t r) -> p a t r", r=P), AX.X, ALU.max,
                                          negate=True).then_inc(g["negmax0"], 1)
                        dve.wait_ge(g["v0_psum"], b + 1)
                        if later(b, 2):
                            dve.wait_ge(g["o0_psum"], b - 1)
                        dve.tensor_copy(vs[:, v, :, 0:D0], bank[1].rearrange("p (h e) -> p h e", h=H0)).then_inc(g["v0"], 1)
                    if live(t, 2):
                        b, v = t - 2, u
                        dve.wait_ge(g["pT0_psum"], b + 1)
                        if later(b, 2):
                            dve.wait_ge(g["o0_psum"], b - 1)
                        dve.tensor_copy(probsT[:, v].rearrange("p a t r -> p (a t r)"), psum[:, 4:6, :].rearrange("p a c -> p (a c)")).then_inc(g["pT0"], 1)
                    if live(t, 3):
                        b, v = t - 3, 1 - u
                        dve.wait_ge(g["y0_psum"], b + 1)
                        dve.tensor_tensor(h[:, b, :], h[:, b, :], bank[1][:, 0:P], ALU.add).then_inc(g["y0_added"], 1)
                        dve.wait_ge(g["y0_added"], b + 1)
                        dve.tensor_tensor(h[:, b, :], h[:, b, :], bo0[:], ALU.add).then_inc(g["h0"], 1)
                        dve.wait_ge(g["h0"], b + 1)
                        ln_stats(1, b, v)
                    if live(t, 2):
                        b, v = t - 2, u
                        dve.wait_ge(g["o0_psum"], b + 1)
                        part = psum[:, 6:8, 0:NT0 * (D0 + 1)].rearrange("p a (t e) -> p a t e", t=NT0)
                        dve.reciprocal(rsum[:, v].unsqueeze(3), part[:, :, :, D0:D0 + 1]).then_inc(g["rsum0"], 1)
                        dve.wait_ge(g["rsum0"], b + 1)
                        if later(b, 2):
                            dve.wait_ge(g["oT0_psum"], b - 1)
                        dve.tensor_tensor(o0[:, v].rearrange("p (t a e) -> p a t e", t=NT0, a=2), part[:, :, :, 0:D0],
                                          rsum[:, v].unsqueeze(3).to_broadcast([P, 2, NT0, D0]), ALU.mult).then_inc(g["o0"], 1)
                steps(dve, 4, att0)

                dve.wait_ge(g["ld_moe0"], 128)
                dve.tensor_reduce(centre[:, 0, :], w2m[:], AX.X, ALU.add)
                link(dve.tensor_reduce(centre[:, 1, :], b2m[:], AX.X, ALU.add))
                link(dve.tensor_scalar(centre[:], centre[:], 1.0 / P, None, ALU.mult))
                dve.tensor_tensor(w2m[:], w2m[:], centre[:, 0, :].unsqueeze(2).to_broadcast([P, E0, P]), ALU.subtract)
                dve.tensor_tensor(b2m[:], b2m[:], centre[:, 1, :].unsqueeze(2).to_broadcast([P, E0, P]), ALU.subtract).then_inc(g["centred"], 1)
                dve.wait_ge(g["centred"], 1)

                dve.wait_ge(g["lg_psum"], 1)
                link(dve.tensor_copy(lg[:].rearrange("p b e -> p (b e)"), bank[6][:, 0:NB * E0]))
                experts = iota[:].unsqueeze(1).to_broadcast([P, NB, E0])

                def over(x):
                    return x.unsqueeze(2).to_broadcast([P, NB, E0])

                for k, scores in ((0, lg[:]), (1, top[:, 3])):
                    chosen = top[:, k]
                    link(dve.tensor_reduce(tops[:, k, :], scores, AX.X, ALU.max))
                    link(dve.tensor_tensor(chosen, scores, over(tops[:, k, :]), ALU.is_equal))
                    link(dve.scalar_tensor_tensor(chosen, chosen, -1000.0, experts, ALU.mult, ALU.add))
                    link(dve.tensor_reduce(tops[:, 2, :], chosen, AX.X, ALU.min))
                    link(dve.tensor_tensor(chosen, chosen, over(tops[:, 2, :]), ALU.is_equal))
                    if k == 0:
                        link(dve.scalar_tensor_tensor(top[:, 3], chosen, -3e38, lg[:], ALU.mult, ALU.add))
                dve.tensor_tensor(tops[:, 3, :], tops[:, 1, :], tops[:, 0, :], ALU.subtract).then_inc(g["tops"], 1)
                dve.wait_ge(g["topexp"], 1)
                link(dve.tensor_scalar(tops[:, 5, :], tops[:, 4, :], 1.0, None, ALU.add))
                link(dve.reciprocal(tops[:, 5, :], tops[:, 5, :]))
                link(dve.tensor_tensor(tops[:, 4, :], tops[:, 4, :], tops[:, 5, :], ALU.mult))
                dve.tensor_tensor(top[:, 0], top[:, 0], over(tops[:, 5, :]), ALU.mult)
                link(dve.tensor_tensor(top[:, 1], top[:, 1], over(tops[:, 4, :]), ALU.mult))
                dve.tensor_tensor(gates[:], top[:, 0], top[:, 1], ALU.add).then_inc(g["gates"], 1)

                def moe0(t, j, u):
                    if live(t, 1):
                        b, v = t - 1, 1 - u
                        dve.wait_ge(g["ysq"], b + 1)
                        dve.tensor_scalar(yvar[:, v], ysum2[:, v], 1.0 / P, EPS, ALU.mult, ALU.add).then_inc(g["yvar"], 1)
                    if live(t, 0):
                        dve.wait_ge(g["y_psum"], t + 1)
                        if later(t, 2):
                            dve.wait_ge(g["yg"], t - 1)
                            dve.wait_ge(g["ysq"], t - 1)
                        dve.tensor_tensor(ym[:, u].rearrange("p e n -> p (e n)"), psum[:, 2 + 2 * u:4 + 2 * u, :].rearrange("p a c -> p (a c)"),
                                          b2m[:].rearrange("p e n -> p (e n)"), ALU.add).then_inc(g["ym"], 1)
                    if live(t, 2):
                        b, v = t - 2, u
                        dve.wait_ge(g["yc"], b + 1)
                        dve.tensor_reduce(ysum[:, v, :], yc[:, v].rearrange("p e n -> p n e"), AX.X, ALU.add).then_inc(g["ysum"], 1)
                        dve.wait_ge(g["ysum"], b + 1)
                        dve.tensor_tensor(h[:, b, :], h[:, b, :], ysum[:, v, :], ALU.add).then_inc(g["h_moe0"], 1)
                    if live(t, 1):
                        b, v = t - 1, 1 - u
                        dve.wait_ge(g["yrstd"], b + 1)
                        dve.tensor_tensor(ycoef[:, v], yrstd[:, v], gates[:, b, :], ALU.mult).then_inc(g["ycoef"], 1)
                    if live(t, 1):
                        b, v = t - 1, 1 - u
                        dve.wait_ge(g["ycoef"], b + 1)
                        dve.wait_ge(g["yg"], b + 1)
                        dve.tensor_tensor(yc[:, v], yg[:, v], ycoef[:, v].unsqueeze(2).to_broadcast([P, E0, P]), ALU.mult).then_inc(g["yc"], 1)
                steps(dve, 2, moe0)
                dve.wait_ge(g["beta_psum"], 1)
                dve.wait_ge(g["h_moe0"], NB)
                for part in range(2):
                    last = dve.tensor_tensor(h[:, 8 * part:8 * part + 8, :], h[:, 8 * part:8 * part + 8, :],
                                             psum[:, 6 * part:6 * part + 2, :].rearrange("p a (b n) -> p (a b) n", n=P), ALU.add)
                last.then_inc(g["h_beta"], 1)

                dve.wait_ge(g["ld_att1"], 240)
                link(dve.tensor_scalar(nbg1[:], nbg1[:], -1.0, None, ALU.mult))
                dve.tensor_scalar(qbias[:], b1a[:, 0:3:2], float(D1) ** -0.5, None, ALU.mult).then_inc(g["ready1"], 1)
                dve.wait_ge(g["h_beta"], 1)
                dve.wait_ge(g["vs_ones"], 4)

                def att1(t, j, u):
                    if live(t, 0):
                        ln_stats(2, t, u)
                    if live(t, 2):
                        b, v = t - 2, u
                        dve.wait_ge(g["v1_psum"], b + 1)
                        dve.tensor_tensor(v1[:, b, :, 0:D1], bank[1][:, 0:P].rearrange("p (h e) -> p h e", h=H1),
                                          bv1[:].rearrange("p (h e) -> p h e", h=H1), ALU.add)
                        dve.tensor_copy(gx1[:, bass.ds(b, 1)], bank[1][:, P:P + 1])
                        for odd in range(2):
                            rows = slice(CH * odd, CH * odd + CH)
                            heads = bank[1][rows, P + 1:P + 1 + LH * LD].rearrange("p (a o e) -> p a o e", a=2, o=2)[:, :, odd, :]
                            bias = brv1[rows, :].rearrange("p (a o e) -> p a o e", a=2, o=2)[:, :, odd, :]
                            last = dve.scalar_tensor_tensor(gv1[rows, b, :, odd, 0:LD], heads, 0.5, bias, ALU.mult, ALU.add)
                        last.then_inc(g["v1"], 1)
                    if live(t, 5):
                        b, v = t - 5, 1 - u
                        dve.wait_ge(g["ge1"], b + 1)
                        dve.tensor_scalar(gd1[:, v, 2:3], gd1[:, v, 1:2], 1.0, None, ALU.add).then_inc(g["gate1a"], 1)
                        dve.wait_ge(g["gate1a"], 2 * b + 1)
                        dve.reciprocal(gd1[:, v, 2:3], gd1[:, v, 2:3]).then_inc(g["gate1a"], 1)
                        dve.wait_ge(g["gate1a"], 2 * b + 2)
                        dve.tensor_scalar(gd1[:, v, 3:4], gd1[:, v, 2:3], -1.0, 1.0, ALU.mult, ALU.add).then_inc(g["gate1"], 1)
                        if later(b, 2):
                            dve.wait_ge(g["catT1_psum"], b - 1)
                        dve.tensor_scalar(cat1[:, v, 0:P], loc1[:, v, :], gd1[:, v, 2:3], None, ALU.mult)
                        dve.wait_ge(g["gate1"], b + 1)
                        dve.tensor_scalar(cat1[:, v, P:P + LH * LD], lat1[:, v, :], gd1[:, v, 3:4], None, ALU.mult)
                        dve.tensor_copy(cat1[:, v, P + LH * LD:], gd1[:, v, 3:4]).then_inc(g["cat1"], 1)
                    if live(t, 0):
                        ln_xhat(2, t, u)
                    if live(t, 4):
                        b, v = t - 4, u
                        dve.wait_ge(g["o1_psum"], b + 1)
                        heads = bank[5][:, 0:(H1 + LH) * (D1 + 1)].rearrange("p (h e) -> p h e", h=H1 + LH)
                        dve.reciprocal(sum1[:, v, :].unsqueeze(2), heads[:, :, D1:D1 + 1]).then_inc(g["rsum1"], 1)
                        dve.wait_ge(g["rsum1"], b + 1)
                        dve.tensor_tensor(loc1[:, v, :].rearrange("p (h e) -> p h e", h=H1), heads[:, 0:H1, 0:D1],
                                          sum1[:, v, 0:H1].unsqueeze(2).to_broadcast([P, H1, D1]), ALU.mult)
                        dve.scalar_tensor_tensor(lat1[:, v, :].rearrange("p (h e) -> p h e", h=LH), heads[:, H1:, 0:D1], valid[:],
                                                 sum1[:, v, H1:].unsqueeze(2).to_broadcast([P, LH, LD]), ALU.mult, ALU.mult).then_inc(g["o1"], 1)
                    if live(t, 2):
                        b, v = t - 2, u
                        dve.wait_ge(g["s1_psum"], b + 1)
                        local = psum[:, 2:4, :].rearrange("p a (o r) -> p (a o) r", r=P)
                        latent = bank[4][:, 0:LAT].rearrange("p (a r) -> p a r", r=CH)
                        dve.tensor_reduce(max1[:, v, 0:H1], local, AX.X, ALU.max)
                        dve.tensor_reduce(max1[:, v, H1:], latent, AX.X, ALU.max).then_inc(g["max1"], 1)
                    if live(t, 5):
                        b, v = t - 5, 1 - u
                        dve.wait_ge(g["y1_psum"], b + 1)
                        dve.tensor_tensor(h[:, b, :], h[:, b, :], bank[5][:, 2 * P:3 * P], ALU.add).then_inc(g["y1_added"], 1)
                        dve.wait_ge(g["y1_added"], b + 1)
                        dve.tensor_tensor(h[:, b, :], h[:, b, :], bo1[:], ALU.add).then_inc(g["h1"], 1)
                    if live(t, 2):
                        b, v = t - 2, u
                        dve.wait_ge(g["max1"], b + 1)
                        if later(b, 2):
                            dve.wait_ge(g["latT_psum"], b - 1)
                        dve.tensor_tensor(e1[:, v, 0:H1 * P].rearrange("p (a r) -> p a r", r=P), local,
                                          max1[:, v, 0:H1].unsqueeze(2).to_broadcast([P, H1, P]), ALU.subtract)
                        dve.tensor_tensor(e1[:, v, H1 * P:].rearrange("p (a r) -> p a r", a=4), latent,
                                          max1[:, v, H1:].unsqueeze(2).to_broadcast([P, LH, CH]), ALU.subtract).then_inc(g["sub1"], 1)
                    if live(t, 4):
                        b, v = t - 4, u
                        dve.wait_ge(g["o1"], b + 1)
                        dve.scalar_tensor_tensor(gw1[:, v, :], loc1[:, v, :], 1.0, wg1[:], ALU.mult, ALU.mult,
                                                 accum_out=gd1[:, v, 0:1]).then_inc(g["gate1b"], 1)
                        dve.wait_ge(g["gate1b"], b + 1)
                        dve.tensor_tensor(gd1[:, v, 0:1], gd1[:, v, 0:1], gx1[:, bass.ds(b, 1)], ALU.add).then_inc(g["gd1"], 1)
                steps(dve, 5, att1)

                dve.wait_ge(g["h1"], NB)
                dve.wait_ge(g["ld_att2"], 80)
                link(dve.tensor_scalar(col2[:, 2:3], col2[:, 2:3], float(D2) ** 0.5, None, ALU.mult))

                def att2(t, j, u):
                    if live(t, 2):
                        b, v = t - 2, u
                        dve.wait_ge(g["sq2"], b + 1)
                        if later(b, 2):
                            dve.wait_ge(g["ss2e"], b - 1)
                        dve.tensor_reduce(ss2[:, v], sq2[:, v].rearrange("p (h e) -> p h e", e=D2), AX.X, ALU.add).then_inc(g["ss2"], 1)
                    if live(t, 4):
                        b, v = t - 4, u
                        dve.wait_ge(g["s2_psum"], b + 1)
                        if later(b, 2):
                            dve.wait_ge(g["p2"], b - 1)
                        dve.tensor_reduce(max2[:, v], psum[:, 2:4, 0:P], AX.X, ALU.max, negate=True).then_inc(g["max2"], 1)
                    if live(t, 0):
                        ln_stats(3, t, u)
                    if live(t, 5):
                        b, v = t - 5, 1 - u
                        dve.wait_ge(g["o2_psum"], b + 1)
                        heads = bank[5][:, 0:H2 * (D2 + 1)].rearrange("p (h e) -> p h e", h=H2)
                        dve.reciprocal(sum2[:, v, :].unsqueeze(2), heads[:, :, D2:D2 + 1]).then_inc(g["rsum2"], 1)
                        dve.wait_ge(g["rsum2"], b + 1)
                        if later(b, 2):
                            dve.wait_ge(g["oT2_psum"], b - 1)
                        dve.tensor_tensor(o2[:, v, :].rearrange("p (h e) -> p h e", h=H2), heads[:, :, 0:D2],
                                          sum2[:, v, :].unsqueeze(2).to_broadcast([P, H2, D2]), ALU.mult).then_inc(g["o2"], 1)
                    if live(t, 4):
                        dve.wait_ge(g["pT2_psum"], t - 3)
                    if live(t, 6):
                        b, v = t - 6, u
                        dve.wait_ge(g["gl2_psum"], b + 1)
                        dve.tensor_tensor(glog[:, b, :], bank[4][:, 2 * P:2 * P + E2], gb2[:], ALU.add).then_inc(g["gl2"], 1)
                    if live(t, 4):
                        b, v = t - 4, u
                        if later(b, 2):
                            dve.wait_ge(g["o2_psum"], b - 1)
                        dve.tensor_copy(pT2[:, v].rearrange("p h r -> p (h r)"), bank[4][:, 0:2 * P]).then_inc(g["pT2"], 1)
                    if live(t, 0):
                        ln_xhat(3, t, u)
                    if live(t, 2):
                        b, v = t - 2, u
                        dve.wait_ge(g["rn2"], b + 1)
                        if later(b, 2):
                            dve.wait_ge(g["qkT2_psum"], b - 1)
                        source = bank[7 * u]
                        dve.tensor_tensor(qk2[:, v].rearrange("p (h e) -> p h e", e=D2), source[:, 0:2 * P].rearrange("p (h e) -> p h e", e=D2),
                                          rn2[:, v].unsqueeze(2).to_broadcast([P, 2 * H2, D2]), ALU.mult)
                        dve.tensor_copy(v2[:, b, :, 0:D2], source[:, 2 * P:3 * P].rearrange("p (h e) -> p h e", e=D2)).then_inc(g["qk2"], 1)
                steps(dve, 6, att2)

                dve.wait_ge(g["gl2"], NB)
                dve.tensor_reduce(gsum[:, 0, :], glog, AX.X, ALU.max).then_inc(g["chain4"], 1)
                dve.wait_ge(g["chain4"], 1)
                dve.tensor_tensor(glog, glog, over(gsum[:, 0, :]), ALU.subtract).then_inc(g["chain4"], 1)
                dve.wait_ge(g["act4"], 1)
                link(dve.tensor_reduce(gsum[:, 1, :], g2, AX.X, ALU.add))
                link(dve.reciprocal(gsum[:, 1, :], gsum[:, 1, :]))
                dve.tensor_tensor(g2, g2, over(gsum[:, 1, :]), ALU.mult).then_inc(g["g2"], 1)
                dve.wait_ge(g["b2_psum"], 1)
                dve.tensor_tensor(h[:], h[:], psum[:, 2:6, :].rearrange("p a (b n) -> p (a b) n", n=P), ALU.add).then_inc(g["acc0"], 1)

                dve.wait_ge(g["acc0"], 1)

                def experts2(grp):
                    for e in range(E2):
                        n = E2 * grp + e
                        dve.wait_ge(g["eo_psum"], n + 1)
                        if e > 0:
                            dve.wait_ge(g["acc"], n)
                        elif later(grp, 1):
                            dve.wait_ge(g["stored"], 16 * grp)
                        for u in range(GB):
                            b = GB * grp + u
                            last = dve.scalar_tensor_tensor(acc[:, u, :], bank[4 + e % 2][:, u * P:(u + 1) * P], g2[:, b, e:e + 1],
                                                            h[:, b, :] if e == 0 else acc[:, u, :], ALU.mult, ALU.add)
                        last.then_inc(g["acc"], 1)
                    dve.wait_ge(g["acc"], E2 * grp + E2)
                    dve.sem_inc(g["out_acc"], 1)
                experts2(0)
                with dve.Fori(1, NG) as grp:
                    experts2(grp)

            @block.tensor
            def _(pe):
                pe.wait_ge(g["ld_const"], 96)
                pe.matmul(bank[1][0:NF, 0:P], tab_l[:], tab_r[:], start=True, stop=True).then_inc(g["table_psum"], 1)
                pe.wait_ge(g["trig"], 1)
                pe.wait_ge(g["val_ready"], 1)
                for f in range(6):
                    last = pe.transpose(bank[0][:, f * NB:(f + 1) * NB], val[:, f, :], ident[0:NB, 0:NB])
                last.then_inc(g["valT_psum"], 1)
                pe.wait_ge(g["table_ready"], 1)
                pe.wait_ge(g["ld_att0"], 80)

                def ln_transpose(phase, b, v, dst):
                    pe.wait_ge(g["ln_xhat"], NB * phase + b + 1)
                    pe.transpose(dst[:, 0:P], xhat[:, v, :], ident[:]).then_inc(g["ln_xT_psum"], 1)

                pe.wait_ge(g["onehot"], 1)
                for t in range(NG + 2):
                    if t < NG:
                        if t >= 2:
                            pe.wait_ge(g["onehotT"], t - 1)
                        for b in range(GB):
                            last = pe.transpose(bank[t % 2][0:NF, b * P:(b + 1) * P], above[:, GB * t + b, :], ident[:])
                        last.then_inc(g["onehotT_psum"], 1)
                        pe.wait_ge(g["onehotT"], t + 1)
                        if t >= 2:
                            pe.wait_ge(g["tok_xhat"], t - 1)
                        for b in range(GB):
                            last = pe.matmul(bank[2 + t % 2][:, b * P:(b + 1) * P], onehotT[:, t % 2, b * P:(b + 1) * P], table[:], start=True, stop=True)
                        last.then_inc(g["tok_psum"], 1)
                    if t >= 2:
                        grp = t - 2
                        pe.wait_ge(g["ln_xhat"], GB * grp + GB)
                        if grp >= 2:
                            pe.wait_ge(g["ln_xT"], GB * grp - GB)
                        for b in range(GB):
                            last = pe.transpose(bank[4 + grp % 2][:, b * P:(b + 1) * P], xhat4[:, grp % 2, b, :], ident[:])
                        last.then_inc(g["ln_xT_psum"], GB)
                        pe.wait_ge(g["ln_xT"], GB * grp + GB)
                        for tile in range(NT0):
                            n = NT0 * grp + tile
                            if n >= 2:
                                pe.wait_ge(g["q_all"], n - 1)
                            pe.matmul(bank[6 + tile % 2], wq0[:, tile * P:(tile + 1) * P], xT_all[:, GB * grp:GB * grp + GB, :],
                                      start=True, stop=True).then_inc(g["q_psum"], 1)

                def pos(c, j, u):
                    if live(c, 0):
                        for done in ("qn_even", "qn_odd", "relw"):
                            pe.wait_ge(g[done], c + 1)
                        if later(c, 2):
                            pe.wait_ge(g["pos_first"], c - 1)
                            pe.wait_ge(g["pos_second"], c - 1)
                        for i in range(8):
                            last = pe.matmul(bank[2 * u + i // 4][:, i % 4 * P:(i % 4 + 1) * P], relw[:, u, 7 - i:7 - i + P],
                                             qn[:, u, i].rearrange("p t o b -> p (t o b)"), start=True, stop=True)
                        last.then_inc(g["pos_psum"], 1)
                steps(pe, 0, pos)

                pe.wait_ge(g["pos_first"], NB)
                pe.wait_ge(g["pos_second"], NB)

                def att0(t, j, u):
                    if live(t, 1):
                        b, v = t - 1, 1 - u
                        pe.wait_ge(g[f"att0_in{1 - u}"], 48 * (j + u))
                        pe.wait_ge(g["k0"], b + 1)
                        if later(b, 1):
                            pe.wait_ge(g["p0"], b)
                        for odd in range(2):
                            for tile in range(NT0):
                                pe.matmul(bank[2 + odd][:, tile * P:(tile + 1) * P], posTs[:, v, 2 * tile + odd, :], ident[:],
                                          start=(tile == 0), stop=False, skip_group_check=True)
                        for tile in range(NT0):
                            for odd in range(2):
                                rows = slice(64 * odd, 64 * odd + 64)
                                last = pe.matmul(bank[2 + odd][:, tile * P:(tile + 1) * P], qTs[rows, v, tile, :],
                                                 kTs[rows, v, tile, :], start=False, stop=(tile == NT0 - 1), skip_group_check=True)
                        last.then_inc(g["s0_psum"], 1)
                    if live(t, 3):
                        b, v = t - 3, 1 - u
                        pe.wait_ge(g["o0"], b + 1)
                        for tile in range(NT0):
                            last = pe.transpose(bank[0][:, tile * P:(tile + 1) * P], o0[:, v, tile * P:(tile + 1) * P], ident[:])
                        last.then_inc(g["oT0_psum"], 1)
                    if live(t, 1):
                        if later(t, 4):
                            pe.wait_ge(g["y0_added"], t - 3)
                        elif later(t, 2):
                            pe.wait_ge(g["v0"], t - 1)
                        pe.matmul(bank[1], xTs[:, 1 - u, :], wkv0[:, H0 * D0:], start=True, stop=True).then_inc(g["v0_psum"], 1)
                    if live(t, 2):
                        b, v = t - 2, u
                        pe.wait_ge(g["p0"], b + 1)
                        if later(b, 1):
                            pe.wait_ge(g["pT0"], b)
                        for odd in range(2):
                            for tile in range(NT0):
                                last = pe.transpose(bank[4 + odd][:, tile * P:(tile + 1) * P], probs[:, v, odd, tile, :], ident[:])
                        last.then_inc(g["pT0_psum"], 1)
                    if live(t, 4):
                        b = t - 4
                        pe.wait_ge(g["o0"], (t - 2) if live(t, 3) else NB)
                        if later(b, 1):
                            pe.wait_ge(g["ln_xT"], NB + b)
                        ln_transpose(1, b, u, bank[7][:, 3 * P:])
                    if live(t, 0):
                        if later(t, 3):
                            pe.wait_ge(g["oT0"], t - 2)
                        elif later(t, 1):
                            pe.wait_ge(g["k0"], t)
                        if not isinstance(t, int) or t < 2:
                            pe.wait_ge(g["q_all"], NG * NT0)
                        for tile in range(NT0):
                            last = pe.matmul(bank[0][:, tile * P:(tile + 1) * P], wkv0[:, tile * P:(tile + 1) * P],
                                             xT_all[:, t, :], start=True, stop=True)
                        last.then_inc(g["k0_psum"], 1)
                    if live(t, 3):
                        b, v = t - 3, 1 - u
                        pe.wait_ge(g["oT0"], b + 1)
                        pe.wait_ge(g["v0"], t if live(t, 1) else NB)
                        if not live(t, 1) and later(b, 1):
                            pe.wait_ge(g["y0_added"], b)
                        for tile in range(NT0):
                            last = pe.matmul(bank[1][:, 0:P], oT0[:, v, tile, :], wo0[:, tile, :], start=(tile == 0), stop=(tile == NT0 - 1))
                        last.then_inc(g["y0_psum"], 1)
                    if live(t, 2):
                        b, v = t - 2, u
                        pe.wait_ge(g["pT0"], b + 1)
                        pe.wait_ge(g["v0"], b + 1)
                        if later(b, 1):
                            pe.wait_ge(g["o0"], b)
                        if live(t, 4):
                            pe.wait_ge(g["ln_xT"], NB + t - 3)
                        for odd in range(2):
                            for tile in range(NT0):
                                last = pe.matmul(bank[6 + odd][:, tile * (D0 + 1):(tile + 1) * (D0 + 1)], probsT[:, v, odd, tile, :],
                                                 vs[:, v, 2 * tile + odd, :], start=True, stop=True)
                        last.then_inc(g["o0_psum"], 1)
                steps(pe, 4, att0)

                pe.wait_ge(g["ld_moe0"], 128)
                pe.wait_ge(g["ln_xT"], 2 * NB)
                pe.wait_ge(g["p0"], NB)
                pe.wait_ge(g["pT0"], NB)
                pe.wait_ge(g["o0"], NB)
                for grp in range(NG):
                    last = pe.matmul(bank[2 + grp][0:E0, :], wgm[:], xT_all[:, GB * grp:GB * grp + GB, :], start=True, stop=True)
                last.then_inc(g["lgT_psum"], 1)
                pe.wait_ge(g["lgT"], 1)
                for b in range(NB):
                    last = pe.transpose(bank[6][:, b * E0:(b + 1) * E0], lgT[:, b * P:(b + 1) * P], ident[0:E0, 0:E0])
                last.then_inc(g["lg_psum"], 1)
                pe.wait_ge(g["centred"], 1)
                pe.wait_ge(g["h0"], NB)

                def moe0(t, j, u):
                    for half in range(2):
                        if live(t, 0, NB // 2):
                            for pair in (2 * half, 2 * half + 1):
                                if pair >= 2 or later(t, 1):
                                    pe.wait_ge(g["hid"], 4 * t + pair - 1)
                                for e in (2 * pair, 2 * pair + 1):
                                    last = pe.matmul(bank[pair % 2][:, e % 2 * 2 * P:(e % 2 + 1) * 2 * P], w1m[:, e, :],
                                                     xT_all[:, bass.ds(2 * t, 2), :], start=True, stop=True)
                                last.then_inc(g["hid_psum"], 1)
                        if live(t, 1, NB // 2):
                            if half == 0:
                                pe.wait_ge(g["hid"], 4 * t)
                            if later(t, 2):
                                pe.wait_ge(g["ym"], 2 * t - 3 + half)
                            for e in range(E0):
                                last = pe.matmul(bank[2 + 2 * half + e // 4][:, e % 4 * P:(e % 4 + 1) * P],
                                                 hid[:, 1 - u, e, half * P:(half + 1) * P], w2m[:, e, :], start=True, stop=True)
                            last.then_inc(g["y_psum"], 1)
                steps(pe, 1, moe0, NB // 2)
                pe.wait_ge(g["hid"], 2 * NB)
                pe.wait_ge(g["gates"], 1)
                for b in range(NB):
                    last = pe.transpose(bank[(0, 1, 6, 7)[b // GB]][0:E0, b % GB * P:(b % GB + 1) * P], gates[:, b, :], ident[:])
                last.then_inc(g["gT_psum"], 1)
                pe.wait_ge(g["gT"], 1)
                for b in range(NB):
                    last = pe.matmul(bank[(0, 1, 6, 7)[b // GB]][:, b % GB * P:(b % GB + 1) * P], gT[:, b * P:(b + 1) * P], beta[:],
                                     start=True, stop=True)
                last.then_inc(g["beta_psum"], 1)

                pe.wait_ge(g["ld_att1"], 240)
                pe.wait_ge(g["ym"], NB)
                pe.wait_ge(g["h_beta"], 1)
                pe.matmul(bank[0][0:LH * LD + 1, 0:P], wroT[:], wo1[:], start=True, stop=True).then_inc(g["wro_psum"], 1)
                pe.wait_ge(g["wro1"], 1)

                def att1(t, j, u):
                    if live(t, 1):
                        b, v = t - 1, 1 - u
                        pe.wait_ge(g["xT1"], b + 1)
                        pe.wait_ge(g["pool1"], b + 1)
                        if later(t, 6):
                            pe.wait_ge(g["catT1"], t - 5)
                        elif later(b, 1):
                            pe.wait_ge(g["k1"], b)
                        for i in range(3):
                            pe.matmul(bank[0][:, i * P:(i + 1) * P], wqk1[:, i, :], xT1[:, v, :], start=True, stop=True)
                        pe.matmul(bank[0][:, 3 * P:3 * P + CH], wqk1[:, 3, :], pool1[:, v, 0, :], start=True, stop=True).then_inc(g["proj1_psum"], 1)
                    if live(t, 2):
                        pe.wait_ge(g["k1"], t - 1)
                        pe.wait_ge(g["kx1"], t - 1)
                        if later(t, 3):
                            pe.wait_ge(g["sub1"], t - 2)
                    if live(t, 4):
                        pe.wait_ge(g["pT1"], t - 3)
                        pe.wait_ge(g["latT1"], t - 3)
                        pe.wait_ge(g["v1"], t - 3)
                        if later(t, 6):
                            pe.wait_ge(g["y1_added"], t - 5)
                        elif later(t, 5):
                            pe.wait_ge(g["o1"], t - 4)
                    for part in range(3):
                        if live(t, 2):
                            dst = bank[2 + part][:, 0:BANK if part < 2 else LAT]
                            mask = (maskb[:, 0:P].unsqueeze(1).to_broadcast([P, NT0, P]) if part < 2 else
                                    maskb[:, P:].unsqueeze(1).to_broadcast([P, LH, CH]))
                            queries, keys = (qT1, kx1[:, u, 4 * part:4 * part + 4, :]) if part < 2 else (rqT1, gkx1[:, u])
                            pe.matmul(dst.rearrange("p (h r) -> p h r", h=4), identb[:], mask, start=True, stop=False, skip_group_check=True)
                            last = pe.matmul(dst, queries[:, u, :], keys.rearrange("p h r -> p (h r)"), start=False, stop=True, skip_group_check=True)
                            if part == 2:
                                last.then_inc(g["s1_psum"], 1)
                        if live(t, 4):
                            b = t - 4
                            if part < 2:
                                for hd in range(4 * part, 4 * part + 4):
                                    pe.matmul(bank[5][:, hd * (D1 + 1):(hd + 1) * (D1 + 1)], pT1[:, u, hd * P:(hd + 1) * P], v1[:, b, hd, :],
                                              start=True, stop=True)
                            else:
                                for i in range(2):
                                    c = (H1 + 2 * i) * (D1 + 1)
                                    last = pe.matmul(bank[5][:, c:c + 2 * (LD + 1)], pT1[:, u, (H1 + i) * P:(H1 + i + 1) * P],
                                                     gv1[:, b, i].rearrange("p o e -> p (o e)"), start=True, stop=True)
                                last.then_inc(g["o1_psum"], 1)
                    if live(t, 5):
                        b, v = t - 5, 1 - u
                        pe.wait_ge(g["cat1"], b + 1)
                        if live(t, 1):
                            pe.wait_ge(g["k1"], t)
                        elif later(b, 1):
                            pe.wait_ge(g["catT1"], b)
                        pe.transpose(bank[0][:, 0:P], cat1[:, v, 0:P], ident[:])
                        pe.transpose(bank[0][0:LH * LD + 1, P:2 * P], cat1[:, v, P:], ident[:]).then_inc(g["catT1_psum"], 1)
                    if live(t, 3):
                        b, v = t - 3, 1 - u
                        pe.wait_ge(g["e1"], b + 1)
                        if later(b, 1):
                            pe.wait_ge(g["pT1"], b)
                        for hd in range(H1):
                            last = pe.transpose(bank[6 + hd // 4][:, hd % 4 * P:(hd % 4 + 1) * P], e1[:, v, hd * P:(hd + 1) * P], ident[:])
                        last.then_inc(g["pT1_psum"], 1)
                        if live(t, 2):
                            pe.wait_ge(g["v1"], t - 1)
                        else:
                            pe.wait_ge(g["latT1"], b)
                        for i in range(2):
                            last = pe.transpose(bank[1][:, i * P:(i + 1) * P], e1[:, v, (H1 + i) * P:(H1 + i + 1) * P], ident[:])
                        last.then_inc(g["latT_psum"], 1)
                    if live(t, 0):
                        if live(t, 2) and not live(t, 3):
                            pe.wait_ge(g["v1"], t - 1)
                        if later(t, 1):
                            pe.wait_ge(g["xT1"], t)
                        ln_transpose(2, t, u, bank[1][:, LAT:])
                    if live(t, 5):
                        b, v = t - 5, 1 - u
                        pe.wait_ge(g["catT1"], b + 1)
                        if live(t, 4):
                            pe.wait_ge(g["o1"], t - 3)
                        else:
                            pe.wait_ge(g["y1_added"], b)
                        pe.matmul(bank[5][:, 2 * P:3 * P], catT1[:, v, 0, :], wo1[:], start=True, stop=False)
                        pe.matmul(bank[5][:, 2 * P:3 * P], catT1[0:LH * LD + 1, v, 1, :], wro1[:], start=False, stop=True).then_inc(g["y1_psum"], 1)
                    if live(t, 1):
                        b, v = t - 1, 1 - u
                        if live(t, 0):
                            pe.wait_ge(g["xT1"], t + 1)
                        else:
                            pe.wait_ge(g["latT1"], t - 2)
                        pe.matmul(bank[1][:, 0:P + 1], xT1[:, v, :], wv1[:], start=True, stop=True)
                        pe.matmul(bank[1][:, P + 1:P + 1 + LH * LD], pool1[:, v].rearrange("p a c -> p (a c)"), wrv1[:], start=True, stop=True).then_inc(g["v1_psum"], 1)
                steps(pe, 5, att1)

                pe.wait_ge(g["ld_att2"], 80)
                pe.wait_ge(g["h1"], NB)

                def att2(t, j, u):
                    if live(t, 1):
                        if later(t, 2):
                            pe.wait_ge(g["xT2"], t - 1)
                        if later(t, 4):
                            pe.wait_ge(g["qkT2"], t - 3)
                        ln_transpose(3, t - 1, 1 - u, bank[1][:, 2 * P:3 * P])
                    if live(t, 3):
                        b, v = t - 3, 1 - u
                        pe.wait_ge(g["qk2"], b + 1)
                        if not live(t, 1) and later(b, 1):
                            pe.wait_ge(g["qkT2"], b)
                        for i in range(2):
                            last = pe.transpose(bank[1][:, i * P:(i + 1) * P], qk2[:, v, i * P:(i + 1) * P], ident[:])
                        last.then_inc(g["qkT2_psum"], 1)
                    if live(t, 6):
                        b, v = t - 6, u
                        pe.wait_ge(g["yT2"], b + 1)
                        pe.wait_ge(g["yT_all"], b + 1)
                        pe.wait_ge(g["pT2"], (t - 4) if live(t, 5) else NB)
                        if later(b, 1):
                            pe.wait_ge(g["gl2"], b)
                        pe.matmul(bank[4][:, 2 * P:2 * P + E2], yT2[:, v, :], gw2[:], start=True, stop=True).then_inc(g["gl2_psum"], 1)
                    if live(t, 4):
                        b, v = t - 4, u
                        pe.wait_ge(g["p2"], b + 1)
                        if later(b, 1):
                            pe.wait_ge(g["pT2"], b)
                        for hd in range(H2):
                            last = pe.transpose(bank[4][:, hd * P:(hd + 1) * P], p2[:, v, hd, :], ident[:])
                        last.then_inc(g["pT2_psum"], 1)
                    if live(t, 5):
                        b, v = t - 5, 1 - u
                        pe.wait_ge(g["o2"], b + 1)
                        if later(b, 1):
                            pe.wait_ge(g["yT_all"], b)
                        pe.transpose(bank[6][:, 0:P], o2[:, v, :], ident[:]).then_inc(g["oT2_psum"], 1)
                    if live(t, 1):
                        b, v = t - 1, 1 - u
                        pe.wait_ge(g["xT2"], b + 1)
                        if later(b, 2):
                            pe.wait_ge(g["qk2"], b - 1)
                        pe.matmul(bank[7 * (1 - u)][:, 0:3 * P], xT2[:, v, :], wqkv2[:], start=True, stop=True).then_inc(g["qkv2_psum"], 1)
                    if live(t, 3):
                        b, v = t - 3, 1 - u
                        pe.wait_ge(g["qkT2"], b + 1)
                        if later(b, 1):
                            pe.wait_ge(g["p2"], b)
                        for hd in range(H2):
                            pe.matmul(bank[2 + hd][:, 0:P], identb[:], maskb[:, 0:P], start=True, stop=False, skip_group_check=True)
                        for hd in range(H2):
                            rows = slice(D2 * hd, D2 * hd + D2)
                            last = pe.matmul(bank[2 + hd][:, 0:P], qkT2[rows, v, 0, :], qkT2[rows, v, 1, :], start=False, stop=True, skip_group_check=True)
                        last.then_inc(g["s2_psum"], 1)
                    if live(t, 5):
                        b, v = t - 5, 1 - u
                        pe.wait_ge(g["oT2"], b + 1)
                        pe.matmul(bank[6][:, 0:P], wo2[:], oT2[:, v, :], start=True, stop=True).then_inc(g["yT2_psum"], 1)
                    if live(t, 4):
                        b, v = t - 4, u
                        pe.wait_ge(g["pT2"], b + 1)
                        if later(b, 1):
                            pe.wait_ge(g["o2"], b)
                        for hd in range(H2):
                            last = pe.matmul(bank[5][:, hd * (D2 + 1):(hd + 1) * (D2 + 1)], pT2[:, v, hd, :], v2[:, b, hd, :], start=True, stop=True)
                        last.then_inc(g["o2_psum"], 1)
                steps(pe, 6, att2)

                pe.wait_ge(g["ld_moe1"], 64)
                pe.wait_ge(g["g2"], 1)
                for b in range(NB):
                    last = pe.transpose(bank[2 + b // GB][0:E2, b % GB * P:(b % GB + 1) * P], g2[:, b, :], ident[:])
                last.then_inc(g["g2T_psum"], 1)
                pe.wait_ge(g["g2T"], 1)
                for b in range(NB):
                    last = pe.matmul(bank[2 + b // GB][:, b % GB * P:(b % GB + 1) * P], g2T[:, b * P:(b + 1) * P], b2f[:], start=True, stop=True)
                last.then_inc(g["b2_psum"], 1)

                pe.wait_ge(g["acc0"], 1)

                def up(grp, e):
                    for f in range(NC2):
                        n = NC2 * (E2 * grp + e) + f
                        if e > 0 or later(grp, 1):
                            pe.wait_ge(g["hf"], n - NC2 + 1)
                        pe.matmul(bank[f], w1f[:, e, f * P:(f + 1) * P], yT_all[:, bass.ds(GB * grp, GB), :], start=True, stop=True).then_inc(g["hf_psum"], 1)

                def down(grp, e):
                    n = E2 * grp + e
                    pe.wait_ge(g["hf"], NC2 * n + NC2)
                    if e >= 2 or later(grp, 1):
                        pe.wait_ge(g["acc"], n - 1)
                    for u in range(GB):
                        for f in range(NC2):
                            last = pe.matmul(bank[4 + e % 2][:, u * P:(u + 1) * P], hidf[:, e % 2, f, u * P:(u + 1) * P], w2f[:, e, f, :],
                                             start=(f == 0), stop=(f == NC2 - 1))
                    last.then_inc(g["eo_psum"], 1)

                def group(grp):
                    up(grp, 0)
                    for e in range(E2):
                        if e + 1 < E2:
                            up(grp, e + 1)
                        down(grp, e)
                group(0)
                with pe.Fori(1, NG) as grp:
                    group(grp)


def kernel(**inputs):
    import concourse.bacc as bacc
    import ml_dtypes
    from concourse.bass_utils import run_bass_kernel_spmd

    a = {k: np.asarray(v) for k, v in inputs.items()}

    tab_l = np.zeros((43, NF), np.float32)
    tab_l[0:12, 0:7] = a["L0_tok_W_weekday"].T
    tab_l[12:24, 7:31] = a["L0_tok_W_hour"].T
    tab_l[26:34, 31:41] = a["L0_tok_W_dur"].T
    tab_l[34:42, 41:49] = a["L0_tok_W_tdiff"].T
    tab_l[24, 49] = tab_l[25, 50] = tab_l[42, 51] = 1.0
    tab_r = np.concatenate([a["L0_tok_proj_w"].T, a["L0_tok_proj_b"][None, :]])
    bounds = np.stack(bounds_by_column())
    first, n = DUR
    edges = a["L0_tok_dur_boundaries"]
    bounds[0, first], bounds[1, first + n - 1] = -3e38, 3e38
    bounds[0, first + 1:first + n] = edges[1:]
    bounds[1, first:first + n - 1] = edges[1:]
    rel = a["L0_attn_rel_emb"][::-1].T
    bf16 = ml_dtypes.bfloat16

    def heads_apart(w):
        out = np.zeros((*w.shape[:-1], LH, 32), w.dtype)
        out[..., :LD] = w.reshape(*w.shape[:-1], LH, LD)
        return out.reshape(*w.shape[:-1], P)

    q = "L1_attn_"
    token, key, chunk = np.arange(P)[:, None], np.arange(P)[None, :], np.arange(CH)[None, :]
    causal = np.where(key <= token, 0.0, -1e30)
    before = np.where(chunk < token // 2, 0.0, -1e30)
    laid = dict(
        a, ident=np.eye(P, dtype=np.float32), tab_l=tab_l, tab_r=tab_r, bounds=bounds.reshape(-1), relT=np.concatenate([rel, rel]),
        w1m=a["L0_ffn_W1"].transpose(1, 0, 2), w2m=a["L0_ffn_W2"].transpose(1, 0, 2), L0_ffn_b2=a["L0_ffn_b2"].reshape(-1),
        L0_ffn_gamma=a["L0_ffn_gamma"].reshape(-1), b1m=a["L0_ffn_b1"].T, iota=np.arange(E0, dtype=np.float32),
        wqk1=np.stack([a[q + "Wq"], a[q + "Wk"], heads_apart(a[q + "Wrq"]), heads_apart(a[q + "Wrk"])], 1),
        wv1=np.concatenate([a[q + "Wv"], a[q + "Wg"][:P]], 1),
        b1a=np.stack([a[q + "bq"], a[q + "bk"], heads_apart(a[q + "brq"]), heads_apart(a[q + "brk"])], 1),
        rows1=np.concatenate([np.repeat(np.eye(H1), D1, axis=0), np.repeat(np.eye(LH), P // LH, axis=0)], 1).astype(np.float32),
        wg1=a[q + "Wg"][P:, 0], valid=(np.arange(P) >= 2).astype(np.float32)[:, None],
        wroT=np.concatenate([a[q + "Wro"], a[q + "bro"][None, :]]).T,
        identb=np.eye(P).astype(bf16), maskb=np.concatenate([causal, before], 1).astype(bf16),
        wqkv2=np.concatenate([a["L1_ffn_Wq"], a["L1_ffn_Wk"], a["L1_ffn_Wv"]], 1),
        col2=np.stack([a["L1_ffn_ln_g"], a["L1_ffn_ln_b"], np.tile(a["L1_ffn_qn_g"], H2), np.tile(a["L1_ffn_kn_g"], H2)], 1),
        b1f=a["L1_ffn_b1"].reshape(E2, NC2, P).transpose(2, 0, 1),
        w1f=a["L1_ffn_W1"].transpose(1, 0, 2), w2f=a["L1_ffn_W2"].reshape(E2, NC2, P, P).transpose(2, 0, 1, 3))
    names = ["x", "itok_BS_0_1439", "itok_BS_0_7", "fside_BS_durations", "ident", "bounds", "tab_l", "tab_r",
             "L0_tok_ln_w", "L0_tok_ln_b", "L0_attn_Wq", "relT", "L0_attn_Wkv", "L0_attn_Wo", "L0_attn_bo",
             "w1m", "w2m", "L0_ffn_b2", "L0_ffn_gamma", "L0_ffn_beta", "b1m", "L0_ffn_Wg", "iota",
             "wqk1", "wv1", "L1_attn_Wrv", "b1a", "rows1", "L1_attn_bv", "L1_attn_brv", "wg1", "L1_attn_bg", "valid", "wroT",
             "L1_attn_Wo", "L1_attn_bo", "identb", "maskb",
             "wqkv2", "L1_ffn_Wo", "col2", "L1_ffn_gate_W", "L1_ffn_gate_b", "b1f", "L1_ffn_b2", "w1f", "w2f"]

    nc = bacc.Bacc("TRN2", target_bir_lowering=False, num_devices=1)
    arrays, d = {}, {}
    for name in names:
        v = np.ascontiguousarray(laid[name])
        arrays[name + "_dram"] = v
        d[name] = nc.dram_tensor(name + "_dram", v.shape, mybir.dt.from_np(v.dtype), kind="ExternalInput").ap()
    out = nc.dram_tensor("out_dram", (NB, P, P), F32, kind="ExternalOutput").ap()
    build(nc, d, out)
    return run_bass_kernel_spmd(nc, [arrays], core_ids=[0]).results[0]["out_dram"]
```

```python
from contextlib import ExitStack

import numpy as np

import concourse.bass as bass
from concourse import mybir

F32 = mybir.dt.float32
I32 = mybir.dt.int32
BF16 = mybir.dt.bfloat16
F32R = mybir.dt.float32r
ALU = mybir.AluOpType
ACT = mybir.ActivationFunctionType
AX = mybir.AxisListType

P = 128
NB = 16
NG, GB = 4, 4
BANK = 512
EPS = 1e-5
WEEK, HOUR, DUR, DIFF = (0, 7), (7, 24), (31, 10), (41, 8)
NF = 52
MINUTES = 1440.0
ROUND = 12582912.0
H0, D0 = 8, 64
NT0 = H0 * D0 // P
NREL = 257
E0 = 8
H1, D1 = 8, 16
LH, LD, CH = 4, 16, 64
H2, D2 = 2, 64
E2, FF = 8, 512
NC2 = FF // P


def bounds_by_column():
    lo, hi = np.zeros(49, np.float32), np.zeros(49, np.float32)
    for first, n in (WEEK, DIFF):
        lo[first:first + n] = np.arange(n) - 0.5
        hi[first:first + n] = np.arange(n) + 0.5
    first, n = HOUR
    lo[first:first + n] = 60.0 * np.arange(n) - 0.5
    hi[first:first + n] = 60.0 * np.arange(n) + 59.5
    lo[first], hi[first + n - 1] = -3e38, 3e38
    return lo, hi


def build(nc, d, out):
    ctx = ExitStack()
    with ctx:
        def sb(name, shape, dt=F32):
            return ctx.enter_context(nc.sbuf_tensor(name, shape, dt))

        def sb_split(name, shape):
            with nc.sbuf_tensor(name + "_r", shape, F32R) as over:
                pass
            return sb(name, shape), over

        sems = {}

        def sem(*names):
            for name in names:
                sems[name] = ctx.enter_context(nc.semaphore(name))

        psum = ctx.enter_context(nc.psum_tensor("psum", [P, 8, BANK], F32))
        bank = [psum[:, i, :] for i in range(8)]

        arena = sb("arena", [P, 11024])
        used = {"att0": 0, "att1": 0}

        def carve(part, shape):
            n = int(np.prod(shape))
            view = arena[:, used[part]:used[part] + n]
            used[part] += n
            names = "abcd"[:len(shape)]
            assert used[part] <= 11024
            return view.rearrange(f"p ({' '.join(names)}) -> p {' '.join(names)}", **dict(zip(names, shape))) if len(shape) > 1 else view

        ident = sb("ident", [P, P])
        ids = sb("ids", [NB, 3, P], I32)
        dur = sb("dur", [NB, P])
        tab_l = sb("tab_l", [43, NF])
        tab_r = sb("tab_r", [43, P])
        table = sb("table", [NF, P])
        valT = sb("valT", [P, 6, NB])
        minus_half = sb("minus_half", [P, 8])
        eps = sb("eps", [P, 8])
        h = sb("h", [P, NB, P])
        xT_all, y_hi = sb_split("xT_all", [P, NB, P])
        stats = sb("stats", [P, 2, 6])
        mv = sb("mv", [P, 2, 2])
        var_eps = sb("var_eps", [P, 2, 1])
        rstd = sb("rstd", [P, 2, 1])
        xhat = sb("xhat", [P, 2, P])
        wq0 = sb("wq0", [P, H0 * D0])
        wkv0 = sb("wkv0", [P, 2 * H0 * D0])
        wo0 = sb("wo0", [P, NT0, P])
        bo0 = sb("bo0", [P, P])
        relT = sb("relT", [P, NREL])
        relw = sb("relw", [P, 2, P + 7])
        big, split = sb_split("big", [P, NB * H0 * P + NB * NT0 * P])
        posT = big[:, 0:NB * H0 * P].rearrange("p (b h n) -> p b h n", b=NB, h=H0)
        qT_all = big[:, NB * H0 * P:].rearrange("p (t b n) -> p t b n", t=NT0, b=NB)
        qTs = carve("att0", [2, NT0, P])
        posTs = carve("att0", [2, H0, P])
        xTs = carve("att0", [2, P])
        kTs = carve("att0", [2, NT0, P])
        vs = sb("vs", [P, 2, H0, D0])
        negmax = carve("att0", [2, 2, NT0])
        probs = carve("att0", [2, 2, NT0, P])
        probsT = carve("att0", [2, 2, NT0, P])
        rsum = carve("att0", [2, 2, NT0])
        oT0 = carve("att0", [2, NT0, P])

        qn = arena[:, 4096:6144].rearrange("p (v i t o b) -> p v i t o b", v=2, i=8, t=NT0, o=2)
        val = arena[0:NB, 1024:1792].rearrange("p (f n) -> p f n", f=6)
        tmp = arena[0:NB, 1792:2560].rearrange("p (f n) -> p f n", f=6)
        ln0 = arena[:, 2816:3072].rearrange("p (k n) -> p k n", k=2)
        lohi = arena[:, 3072:3170].rearrange("p (k n) -> p k n", k=2)
        onehotT = arena[0:NF, 0:2 * GB * P].rearrange("p (v n) -> p v n", v=2)
        xhat4 = arena[:, 6144:6144 + 2 * GB * P].rearrange("p (v b n) -> p v b n", v=2, b=GB)
        stats4 = arena[:, 7168:7168 + 12 * NB].rearrange("p (k b c) -> p k b c", k=2, b=NB)
        mv4 = arena[:, 7360:7360 + 4 * NB].rearrange("p (k b c) -> p k b c", k=2, b=NB)
        rstd4 = arena[:, 7424:7424 + 2 * NB].rearrange("p (k b c) -> p k b c", k=2, b=NB)
        above = arena[:, 8192:8192 + NB * NF].rearrange("p (b f) -> p b f", b=NB)
        upto = arena[:, 9216:9216 + NB * NF].rearrange("p (b f) -> p b f", b=NB)
        ysum = arena[:, 9400:9656].rearrange("p (v n) -> p v n", v=2)
        glog = arena[:, 9660:9788].rearrange("p (b e) -> p b e", b=NB)
        g2 = arena[:, 9792:9920].rearrange("p (b e) -> p b e", b=NB)
        top = arena[:, 9984:10496].rearrange("p (k b e) -> p k b e", k=4, b=NB)
        acc = arena[:, 10512:11024].rearrange("p (b n) -> p b n", b=GB)
        wm, y_lo = sb_split("wm", [P, NB, P])
        w1m = wm[:, 0:E0]
        w2m = wm[:, E0:]
        b2m = sb("b2m", [P, E0, P])
        gamma = sb("gamma", [P, E0, P])
        beta = sb("beta", [E0, P])
        b1m = sb("b1m", [P, E0])
        wgm = sb("wgm", [P, E0])
        centre = sb("centre", [P, 2, E0])
        iota = sb("iota", [P, E0])
        lg = sb("lg", [P, NB, E0])
        tops = sb("tops", [P, 6, NB])
        gates = sb("gates", [P, NB, E0])
        gT = big[0:E0, 4096:6144]
        hid = big[:, 0:2 * E0 * 2 * P].rearrange("p (v e n) -> p v e n", v=2, e=E0)
        work = big[:, 8192:]
        ym = work[:, 0:2048].rearrange("p (v e n) -> p v e n", v=2, e=E0)
        ysq = work[:, 2048:4096].rearrange("p (v e n) -> p v e n", v=2, e=E0)
        yg = work[:, 4096:6144].rearrange("p (v e n) -> p v e n", v=2, e=E0)
        yc = work[:, 6144:8192].rearrange("p (v e n) -> p v e n", v=2, e=E0)
        ysum2 = sb("ysum2", [P, 2, E0])
        yvar = sb("yvar", [P, 2, E0])
        yrstd = sb("yrstd", [P, 2, E0])
        ycoef = sb("ycoef", [P, 2, E0])
        LAT = LH * CH
        wqk1 = sb("wqk1", [P, 4, P])
        wv1 = sb("wv1", [P, P + 1])
        wrv1 = sb("wrv1", [P, LH * LD])
        b1a = sb("b1a", [P, 4])
        rows1 = sb("rows1", [P, H1 + LH])
        qbias = sb("qbias", [P, 2])
        bv1 = sb("bv1", [P, P])
        brv1 = sb("brv1", [P, LH * LD])
        wg1 = sb("wg1", [P, P])
        nbg1 = sb("nbg1", [P, 1])
        valid = sb("valid", [P, 1])
        wroT = sb("wroT", [P, LH * LD + 1])
        wo1 = sb("wo1", [P, P])
        wro1 = sb("wro1", [LH * LD + 1, P])
        bo1 = sb("bo1", [P, P])
        identb = sb("identb", [P, P], BF16)
        maskb = sb("maskb", [P, P + CH], BF16)
        xT1 = carve("att1", [2, P])
        pool1 = carve("att1", [2, 2, CH])
        qT1 = carve("att1", [2, P])
        kT1 = carve("att1", [2, P])
        kx1 = big[:, 9216:11264].rearrange("p (v h n) -> p v h n", v=2, h=H1)
        gkx1 = big[:, 11264:11776].rearrange("p (v h n) -> p v h n", v=2, h=LH)
        rqT1 = carve("att1", [2, P])
        gkT1 = carve("att1", [2, CH])
        nv1, ngv1 = NB * H1 * (D1 + 1), NB * LH * (LD + 1)
        v1 = big[:, 0:nv1].rearrange("p (b h e) -> p b h e", b=NB, h=H1)
        gv1 = big[:, nv1:nv1 + ngv1].rearrange("p (b a o e) -> p b a o e", b=NB, a=2, o=2)
        gx1 = sb("gx1", [P, NB])
        max1 = carve("att1", [2, H1 + LH])
        e1 = big[:, 4096:6656].rearrange("p (v n) -> p v n", v=2)
        pT1 = big[:, 6656:9216].rearrange("p (v n) -> p v n", v=2)
        sum1 = carve("att1", [2, H1 + LH])
        loc1 = carve("att1", [2, P])
        lat1 = carve("att1", [2, LH * LD])
        gw1 = carve("att1", [2, P])
        gd1 = carve("att1", [2, 4])
        cat1 = carve("att1", [2, P + LH * LD + 1])
        catT1 = carve("att1", [2, 2, P])
        wqkv2 = sb("wqkv2", [P, 3 * P])
        wo2 = sb("wo2", [P, P])
        col2 = sb("col2", [P, 4])
        gw2 = sb("gw2", [P, E2])
        gb2 = sb("gb2", [P, E2])
        b1f = sb("b1f", [P, E2, NC2])
        b2f = sb("b2f", [E2, P])
        w1f, w1f_hi, w1f_lo = big[:, 16384:20480], split[:, 8192:12288], split[:, 12288:16384]
        w2f = big[:, 20480:24576].rearrange("p (e f n) -> p e f n", e=E2, f=NC2)
        xT2 = carve("att1", [2, P])
        sq2 = carve("att1", [2, 2 * P])
        ss2 = carve("att1", [2, 2 * H2])
        rn2 = carve("att1", [2, 2 * H2])
        qk2 = carve("att1", [2, 2 * P])
        v2 = arena[:, 6656:6656 + NB * H2 * (D2 + 1)].rearrange("p (b h e) -> p b h e", b=NB, h=H2)
        qkT2 = carve("att1", [2, 2, P])
        max2 = carve("att1", [2, H2])
        p2 = carve("att1", [2, H2, P])
        pT2 = carve("att1", [2, H2, P])
        sum2 = carve("att1", [2, H2])
        o2 = carve("att1", [2, P])
        oT2 = carve("att1", [2, P])
        yT2 = carve("att1", [2, P])
        gsum = sb("gsum", [P, 2, NB])
        hidf = big[:, 0:4096].rearrange("p (v f n) -> p v f n", v=2, f=NC2)
        g2T = arena[0:E2, 2048:4096]

        sem("ld_moe0", "ld_att1", "ld_att2", "ld_moe1", "centred", "lg_psum", "tops",
            "topexp", "gates", "gT_psum", "gT", "beta_psum", "h_beta", "hid_psum", "hid", "y_psum", "ym", "ysq", "yvar",
            "yrstd", "ycoef", "yg", "yc", "ysum", "h_moe0", "ready1", "wro_psum", "wro1", "xT1", "pool1", "proj1_psum",
            "v1_psum", "k1", "kx1", "v1", "s1_psum", "max1", "sub1", "e1", "pT1_psum", "latT_psum", "pT1", "latT1", "o1_psum",
            "o1", "gd1", "ge1", "gate1_parts", "gate1_dot", "gate1", "cat1", "catT1_psum", "catT1", "y1_psum",
            "y1_added", "h1")
        sem("xT2", "qkv2_psum", "sq2", "ss2", "ss2e", "rn2", "qk2", "qkT2_psum", "qkT2", "s2_psum", "max2", "p2",
            "pT2_psum", "pT2", "o2_psum", "o2", "oT2_psum", "oT2", "yT2_psum", "yT_all", "gl2_psum",
            "gl2", "act4", "chain4", "g2", "g2T_psum", "g2T", "b2_psum", "h_b2", "w_hi", "w_lo", "y_lo", "hf_psum", "hf", "eo_psum", "acc",
            "out_acc")
        sem("ld_tok", "ld_const", "ld_att0", "chain", "trig_in", "log_in", "trig", "log", "val_ready", "valT_psum",
            "table_psum", "table_ready", "onehot", "onehotT_psum", "onehotT", "tok_psum", "tok_stats", "tok_mv",
            "tok_var", "tok_rstd", "tok_xhat", "tok_h", "const_ready", "vs_ones", "ln_stats", "ln_mv",
            "ln_var", "ln_rstd", "ln_xhat", "ln_xT_psum", "ln_xT", "q_psum", "q_all", "relw", "qn_even", "qn_odd", "pos_psum",
            "pos_first", "pos_second", "att0_in0", "att0_in1", "k0_psum", "k0", "v0_psum", "v0", "s0_psum", "negmax0", "p0",
            "pT0_psum", "pT0", "rsum", "p0_normed", "oT0_psum", "oT0", "y0_psum", "y0_added", "h0", "stored",
            "waited_pe", "waited_dve")
        g = sems

        def steps(eng, lag, step, n=NB):
            first = (lag + 3) // 2
            for t in range(2 * first):
                step(t, t // 2, t % 2)
            with eng.Fori(first, n // 2) as j:
                for u in range(2):
                    step(2 * j + u, j, u)
            for t in range(n, n + lag):
                step(t, t // 2, t % 2)

        def live(t, k, n=NB):
            return not isinstance(t, int) or 0 <= t - k < n

        def later(b, n):
            return not isinstance(b, int) or b >= n

        def f32(view):
            return view.bitcast(F32)

        def apart(eng):
            eng.sem_inc(g["waited_" + ("pe" if eng is nc.tensor else "dve")], 1)

        with nc.Block() as block:

            @block.sync
            def _(sp):
                for i, name in enumerate(("x", "itok_BS_0_1439", "itok_BS_0_7")):
                    sp.dma_start(ids[:, i, :], d[name]).then_inc(g["ld_tok"], 16)
                sp.dma_start(dur[:], d["fside_BS_durations"]).then_inc(g["ld_tok"], 16)
                sp.dma_start(ident[:], d["ident"]).then_inc(g["ld_const"], 16)
                sp.dma_start(lohi.rearrange("p a b -> p (a b)"), d["bounds"].partition_broadcast(P)).then_inc(g["ld_const"], 16)
                sp.dma_start(tab_l[:], d["tab_l"]).then_inc(g["ld_const"], 16)
                sp.dma_start(tab_r[:], d["tab_r"]).then_inc(g["ld_const"], 16)
                sp.dma_start(ln0[:, 0, :], d["L0_tok_ln_w"].partition_broadcast(P)).then_inc(g["ld_const"], 16)
                sp.dma_start(ln0[:, 1, :], d["L0_tok_ln_b"].partition_broadcast(P)).then_inc(g["ld_const"], 16)
                sp.dma_start(wq0[:], d["L0_attn_Wq"]).then_inc(g["ld_att0"], 16)
                sp.dma_start(relT[:], d["relT"]).then_inc(g["ld_att0"], 16)
                sp.dma_start(wkv0[:], d["L0_attn_Wkv"]).then_inc(g["ld_att0"], 16)
                sp.dma_start(wo0[:], d["L0_attn_Wo"].rearrange("(t p) n -> p t n", p=P)).then_inc(g["ld_att0"], 16)
                sp.dma_start(bo0[:], d["L0_attn_bo"].partition_broadcast(P)).then_inc(g["ld_att0"], 16)

                for dst, name in ((w1m, "w1m"), (w2m, "w2m"), (b2m[:].rearrange("p e n -> p (e n)"), "L0_ffn_b2"),
                                  (gamma[:].rearrange("p e n -> p (e n)"), "L0_ffn_gamma"), (beta[:], "L0_ffn_beta"), (b1m[:], "b1m"),
                                  (wgm[:], "L0_ffn_Wg"), (iota[:], "iota")):
                    src = d[name].partition_broadcast(P) if name in ("L0_ffn_b2", "L0_ffn_gamma", "iota") else d[name]
                    sp.dma_start(dst, src).then_inc(g["ld_moe0"], 16)
                for dst, name in ((wqk1[:], "wqk1"), (wv1[:], "wv1"), (wrv1[:], "L1_attn_Wrv"), (b1a[:], "b1a"), (rows1[:], "rows1"),
                                  (bv1[:], "L1_attn_bv"), (brv1[:], "L1_attn_brv"), (wg1[:], "wg1"), (nbg1[:], "L1_attn_bg"),
                                  (valid[:], "valid"), (wroT[:], "wroT"), (wo1[:], "L1_attn_Wo"), (bo1[:], "L1_attn_bo"),
                                  (identb[:], "identb"), (maskb[:], "maskb")):
                    src = d[name].partition_broadcast(P) if name in ("L1_attn_bv", "L1_attn_brv", "wg1", "L1_attn_bg", "L1_attn_bo") else d[name]
                    sp.dma_start(dst, src).then_inc(g["ld_att1"], 16)
                for dst, name in ((wqkv2[:], "wqkv2"), (wo2[:], "L1_ffn_Wo"), (col2[:], "col2"), (gw2[:], "L1_ffn_gate_W"),
                                  (gb2[:], "L1_ffn_gate_b")):
                    src = d[name].partition_broadcast(P) if name == "L1_ffn_gate_b" else d[name]
                    sp.dma_start(dst, src).then_inc(g["ld_att2"], 16)

                sp.wait_ge(g["pos_first"], NB)
                sp.wait_ge(g["pos_second"], NB)

                def step(t, j, u):
                    if live(t, 0):
                        if later(t, 2):
                            sp.wait_ge(g["s0_psum"], t - 1)
                            sp.wait_ge(g["v0_psum"], t - 1)
                        arrived = g[f"att0_in{u}"]
                        sp.dma_start(xTs[:, u, :], xT_all[:, t, :]).then_inc(arrived, 16)
                        sp.dma_start(qTs[:, u], qT_all[:, :, t, :]).then_inc(arrived, 16)
                        sp.dma_start(posTs[:, u], posT[:, t]).then_inc(arrived, 16)
                steps(sp, 0, step)

                sp.wait_ge(g["s0_psum"], NB)
                for dst, name in ((b1f[:], "b1f"), (b2f[:], "L1_ffn_b2"), (w1f.rearrange("p (e n) -> p e n", e=E2), "w1f"), (w2f, "w2f")):
                    sp.dma_start(dst, d[name]).then_inc(g["ld_moe1"], 16)

                sp.wait_ge(g["ld_moe1"], 64)
                sp.wait_ge(g["ld_att1"], 240)
                sp.wait_ge(g["ld_att2"], 80)

                def store(grp):
                    sp.wait_ge(g["out_acc"], grp + 1)
                    sp.dma_start(out[bass.ds(GB * grp, GB)].rearrange("b p n -> p b n"), acc[:]).then_inc(g["stored"], 16)
                store(0)
                with sp.Fori(1, NG) as grp:
                    store(grp)
                sp.wait_ge(g["stored"], 16 * NG)

            @block.gpsimd
            def _(pool):
                pool.memset(arena[:, 4096:6144], 0.0)
                pool.memset(minus_half[:], -0.5).then_inc(g["const_ready"], 1)
                pool.memset(eps[:, 0:1], EPS)
                pool.memset(eps[:, 1:2], 1.0 + EPS)
                pool.memset(eps[:, 2:3], EPS * EPS)
                pool.memset(eps[:, 4:8], 1e-12).then_inc(g["const_ready"], 1)
                pool.memset(above[:, :, 51:52], 1.0).then_inc(g["const_ready"], 1)
                pool.memset(upto[:, :, 49:52], 1.0).then_inc(g["const_ready"], 1)
                pool.wait_ge(g["const_ready"], 4)

                def ln_rstd(phase, b, v):
                    n = NB * phase + b + 1
                    pool.wait_ge(g["ln_mv"], n)
                    pool.tensor_tensor(var_eps[:, v], mv[:, v, 1:2], eps[:, 0:1], ALU.add).then_inc(g["ln_var"], 1)
                    pool.wait_ge(g["ln_var"], n)
                    pool.tensor_tensor(rstd[:, v], var_eps[:, v], minus_half[:, 0:1], ALU.pow).then_inc(g["ln_rstd"], 1)

                def rstd_of(k, grp, summed, done):
                    span = slice(GB * grp, GB * grp + GB)
                    pool.tensor_tensor(rstd4[:, k, span], mv4[:, k, span, 1:2], eps[:, 0:1].unsqueeze(1).to_broadcast([P, GB, 1]),
                                       ALU.add).then_inc(g[summed], GB)
                    pool.wait_ge(g[summed], GB * grp + GB)
                    pool.tensor_tensor(rstd4[:, k, span], rstd4[:, k, span], minus_half[:, 0:GB].unsqueeze(2), ALU.pow).then_inc(g[done], GB)

                for t in range(NG + 1):
                    if t >= 1:
                        pool.wait_ge(g["ln_mv"], GB * t)
                        rstd_of(1, t - 1, "ln_var", "ln_rstd")
                    if t < NG:
                        pool.wait_ge(g["tok_mv"], GB * t + GB)
                        rstd_of(0, t, "tok_var", "tok_rstd")

                pool.wait_ge(g["ld_att0"], 80)
                def window(c, u):
                    if later(c, 2):
                        pool.wait_ge(g["pos_psum"], c - 1)
                    pool.tensor_copy(relw[:, u, :], relT[:, bass.ds(P - 7 - 8 * c, P + 7)]).then_inc(g["relw"], 1)
                for c in range(2):
                    window(c, c)
                with pool.Fori(1, NB // 2) as j:
                    for u in range(2):
                        window(2 * j + u, u)

                def att0(t, j, u):
                    if live(t, 3):
                        ln_rstd(1, t - 3, 1 - u)
                steps(pool, 4, att0)

                def moe0(t, j, u):
                    if live(t, 1):
                        b, v = t - 1, 1 - u
                        pool.wait_ge(g["yvar"], b + 1)
                        if later(b, 2):
                            pool.wait_ge(g["ycoef"], b - 1)
                        pool.tensor_tensor(yrstd[:, v], yvar[:, v], minus_half[:], ALU.pow).then_inc(g["yrstd"], 1)
                    if live(t, 0):
                        pool.wait_ge(g["ym"], t + 1)
                        if later(t, 2):
                            pool.wait_ge(g["yc"], t - 1)
                        pool.tensor_tensor(yg[:, u], ym[:, u], gamma[:], ALU.mult).then_inc(g["yg"], 1)
                steps(pool, 1, moe0)

                pool.wait_ge(g["y_psum"], NB)
                pool.memset(gv1, 0.0)
                pool.wait_ge(g["h_moe0"], NB)
                pool.memset(v2[:, :, :, D2:D2 + 1], 1.0)
                pool.memset(v1[:, :, :, D1:D1 + 1], 1.0).then_inc(g["vs_ones"], 1)
                for odd in range(2):
                    pool.wait_ge(g["vs_ones"], 1 + odd)
                    pool.memset(gv1[CH * odd:CH * odd + CH, :, :, odd, LD:LD + 1], 1.0).then_inc(g["vs_ones"], 1)

                def keys_by_head(b, v):
                    pool.wait_ge(g["k1"], b + 1)
                    if later(b, 2):
                        pool.wait_ge(g["s1_psum"], b - 1)
                    pool.tensor_tensor(kx1[:, v], kT1[:, v, :].unsqueeze(1).to_broadcast([P, H1, P]),
                                       rows1[:, 0:H1].unsqueeze(2).to_broadcast([P, H1, P]), ALU.mult)
                    pool.tensor_tensor(gkx1[:, v], gkT1[:, v, :].unsqueeze(1).to_broadcast([P, LH, CH]),
                                       rows1[:, H1:].unsqueeze(2).to_broadcast([P, LH, CH]), ALU.mult).then_inc(g["kx1"], 1)

                def chunks(t, u):
                    pool.wait_ge(g["xT1"], t + 1)
                    if later(t, 2):
                        pool.wait_ge(g["v1_psum"], t - 1)
                    pairs = xT1[:, u, :].rearrange("p (c o) -> p c o", o=2)
                    for i in range(2):
                        last = pool.tensor_tensor(pool1[:, u, i, :].unsqueeze(2), pairs[:, :, 0:1], pairs[:, :, 1:2], ALU.add)
                    last.then_inc(g["pool1"], 1)

                def att1(t, j, u):
                    if live(t, 0):
                        ln_rstd(2, t, u)
                    if isinstance(t, int) and t == 1:
                        chunks(t, u)
                    if live(t, 1):
                        keys_by_head(t - 1, 1 - u)
                    if live(t, 0) and not (isinstance(t, int) and t == 1):
                        chunks(t, u)
                steps(pool, 1, att1)

                def att2(t, j, u):
                    if live(t, 2):
                        b, v = t - 2, u
                        pool.wait_ge(g["ss2"], b + 1)
                        if later(b, 2):
                            pool.wait_ge(g["qk2"], b - 1)
                        pool.tensor_tensor(rn2[:, v], ss2[:, v], eps[:, 4:8], ALU.add).then_inc(g["ss2e"], 1)
                        pool.wait_ge(g["ss2e"], b + 1)
                        pool.tensor_tensor(rn2[:, v], rn2[:, v], minus_half[:, 0:4], ALU.pow).then_inc(g["rn2"], 1)
                    if live(t, 0):
                        n = 3 * NB + t + 1
                        pool.wait_ge(g["ln_mv"], n)
                        pool.tensor_tensor(var_eps[:, u], mv[:, u, 1:2], eps[:, 1:2], ALU.mult).then_inc(g["ln_var"], 1)
                        pool.wait_ge(g["ln_var"], 3 * NB + 2 * t + 1)
                        pool.tensor_tensor(var_eps[:, u], var_eps[:, u], eps[:, 2:3], ALU.add).then_inc(g["ln_var"], 1)
                        pool.wait_ge(g["ln_var"], 3 * NB + 2 * t + 2)
                        pool.tensor_tensor(rstd[:, u], var_eps[:, u], minus_half[:, 0:1], ALU.pow).then_inc(g["ln_rstd"], 1)
                    if live(t, 1):
                        part = bass.ds(E2 * FF // NB * (t - 1), E2 * FF // NB)
                        pool.wait_ge(g["w_hi"], t)
                        pool.tensor_tensor(w1f_lo[:, part], w1f[:, part], f32(w1f_hi[:, part]), ALU.subtract).then_inc(g["w_lo"], 1)
                    if live(t, 6):
                        b, v = t - 6, u
                        pool.wait_ge(g["yT_all"], b + 1)
                        pool.tensor_tensor(y_lo[:, b, :], yT2[:, v, :], f32(y_hi[:, b, :]), ALU.subtract).then_inc(g["y_lo"], 1)
                steps(pool, 6, att2)

            @block.scalar
            def _(act):
                act.wait_ge(g["log_in"], 1)
                act.activation(tmp[:, 1, :], tmp[:, 0, :], ACT.Ln).then_inc(g["log"], 1)
                act.wait_ge(g["trig_in"], 1)
                act.activation(val[:, 4:6, :], tmp[:, 4:6, :], ACT.Sin).then_inc(g["trig"], 1)
                act.wait_ge(g["table_psum"], 1)
                act.activation(table[:], bank[1][0:NF, 0:P], ACT.Copy).then_inc(g["table_ready"], 1)

                for t in range(NG + 2):
                    if t < NG:
                        act.wait_ge(g["onehotT_psum"], t + 1)
                        if t >= 2:
                            act.wait_ge(g["tok_psum"], t - 1)
                        act.activation(onehotT[:, t % 2, :], bank[t % 2][0:NF, :], ACT.Copy).then_inc(g["onehotT"], 1)
                    if t >= 2:
                        grp = t - 2
                        span = slice(GB * grp, GB * grp + GB)
                        act.wait_ge(g["ln_xT_psum"], GB * grp + GB)
                        act.activation(xT_all[:, span, :], bank[4 + grp % 2], ACT.Copy).then_inc(g["ln_xT"], GB)
                        for tile in range(NT0):
                            act.wait_ge(g["q_psum"], NT0 * grp + tile + 1)
                            act.activation(qT_all[:, tile, span, :], bank[6 + tile % 2], ACT.Copy, scale=float(D0) ** -0.5).then_inc(g["q_all"], 1)

                def pos(t, j, u):
                    if live(t, 0):
                        if later(t, 2):
                            act.wait_ge(g["pos_psum"], t - 1)
                        act.activation(qn[0:64, u, :, :, 0, :], qT_all[0:64, :, :, bass.ds(8 * t, 8)].rearrange("p t b i -> p i t b"), ACT.Copy).then_inc(g["qn_even"], 1)
                    if live(t, 1):
                        c, v = t - 1, 1 - u
                        act.wait_ge(g["pos_psum"], c + 1)
                        act.activation(posT[:, :, :, bass.ds(8 * c, 4)], bank[2 * v].rearrange("p (i h b) -> p b h i", i=4, h=H0), ACT.Copy).then_inc(g["pos_first"], 1)
                act.wait_ge(g["q_all"], NG * NT0)
                steps(act, 1, pos)

                act.activation(rsum[:, 0, 0, 0:1], eps[:, 0:1], ACT.Exp)

                def att0(t, j, u):
                    if live(t, 3):
                        b, v = t - 3, 1 - u
                        act.wait_ge(g["oT0_psum"], b + 1)
                        if later(b, 2):
                            act.wait_ge(g["y0_psum"], b - 1)
                        act.activation(oT0[:, v], bank[6].rearrange("p (t n) -> p t n", t=NT0), ACT.Copy).then_inc(g["oT0"], 1)
                    if live(t, 0):
                        act.wait_ge(g["k0_psum"], t + 1)
                        if later(t, 2):
                            act.wait_ge(g["s0_psum"], t - 1)
                        act.activation(kTs[:, u], bank[0].rearrange("p (t n) -> p t n", t=NT0), ACT.Copy).then_inc(g["k0"], 1)
                    if live(t, 1):
                        b, v = t - 1, 1 - u
                        act.wait_ge(g["negmax0"], b + 1)
                        if later(b, 2):
                            act.wait_ge(g["pT0_psum"], b - 1)
                        for odd in range(2):
                            for tile in range(NT0):
                                e = act.activation(probs[:, v, odd, tile, :], bank[2 + odd][:, tile * P:(tile + 1) * P],
                                                   ACT.Exp, bias=negmax[:, v, odd, tile:tile + 1],
                                                   accum_out=rsum[:, v, odd, tile:tile + 1])
                        e.then_inc(g["p0"], 1)
                    if live(t, 4):
                        b = t - 4
                        act.wait_ge(g["ln_xT_psum"], NB + b + 1)
                        act.activation(xT_all[:, b, :], bank[7][:, 3 * P:], ACT.Copy).then_inc(g["ln_xT"], 1)
                steps(act, 4, att0)

                act.wait_ge(g["ld_moe0"], 128)

                act.wait_ge(g["wro_psum"], 1)
                act.activation(wro1[:], bank[7][0:LH * LD + 1, 0:P], ACT.Copy).then_inc(g["wro1"], 1)

                def weights_transposed(part):
                    act.wait_ge(g["gT_psum"], part + 1)
                    act.activation(gT[:, 8 * P * part:8 * P * (part + 1)].rearrange("p (a n) -> p a n", a=2), psum[0:E0, 6:8, :],
                                   ACT.Copy).then_inc(g["gT"], 1)

                def moe0(t, j, u):
                    for half in range(2):
                        if live(t, 0, NB // 2):
                            for pair in (2 * half, 2 * half + 1):
                                act.wait_ge(g["hid_psum"], 4 * t + pair + 1)
                                if pair == 0 and later(t, 2):
                                    act.wait_ge(g["y_psum"], 2 * t - 2)
                                for e in (2 * pair, 2 * pair + 1):
                                    last = act.activation(hid[:, u, e, :], bank[pair % 2][:, e % 2 * 2 * P:(e % 2 + 1) * 2 * P], ACT.Relu,
                                                          bias=b1m[:, e:e + 1])
                                last.then_inc(g["hid"], 1)
                        if live(t, 1, NB // 2):
                            b = 2 * t - 2 + half
                            act.wait_ge(g["ym"], b + 1)
                            if later(t, 2):
                                act.wait_ge(g["yvar"], b - 1)
                            for e in range(E0):
                                last = act.activation(ysq[:, half, e], ym[:, half, e], ACT.Square, accum_out=ysum2[:, half, e:e + 1])
                            last.then_inc(g["ysq"], 1)
                        if isinstance(t, int) and (t, half) in ((1, 1), (3, 0)):
                            weights_transposed(t // 2)
                        if isinstance(t, int) and (t, half) == (0, 0):
                            act.wait_ge(g["tops"], 1)
                            act.activation(tops[:, 4, :], tops[:, 3, :], ACT.Exp).then_inc(g["topexp"], 1)
                steps(act, 1, moe0, NB // 2)
                act.wait_ge(g["ready1"], 1)

                def att1(t, j, u):
                    if live(t, 1):
                        b, v = t - 1, 1 - u
                        act.wait_ge(g["proj1_psum"], b + 1)
                        if later(b, 2):
                            act.wait_ge(g["s1_psum"], b - 1)
                        act.activation(qT1[:, v, :], bank[0][:, 0:P], ACT.Identity, scale=float(D1) ** -0.5, bias=qbias[:, 0:1])
                        act.activation(kT1[:, v, :], bank[0][:, P:2 * P], ACT.Identity, bias=b1a[:, 1:2])
                        act.activation(rqT1[:, v, :], bank[0][:, 2 * P:3 * P], ACT.Identity, scale=float(LD) ** -0.5, bias=qbias[:, 1:2])
                        act.activation(gkT1[:, v, :], bank[0][:, 3 * P:3 * P + CH], ACT.Identity, scale=0.5, bias=b1a[:, 3:4]).then_inc(g["k1"], 1)
                    if live(t, 5):
                        b, v = t - 5, 1 - u
                        act.wait_ge(g["catT1_psum"], b + 1)
                        if later(b, 2):
                            act.wait_ge(g["y1_psum"], b - 1)
                        act.activation(catT1[:, v, 0, :], bank[0][:, 0:P], ACT.Copy)
                        act.activation(catT1[0:LH * LD + 1, v, 1, :], bank[0][0:LH * LD + 1, P:2 * P], ACT.Copy).then_inc(g["catT1"], 1)
                    if live(t, 3):
                        b, v = t - 3, 1 - u
                        act.wait_ge(g["latT_psum"], b + 1)
                        if later(b, 2):
                            act.wait_ge(g["o1_psum"], b - 1)
                        if live(t, 0):
                            act.wait_ge(g["ln_xT_psum"], 2 * NB + t + 1)
                        act.activation(pT1[:, v, H1 * P:], bank[1][:, 0:LAT], ACT.Copy).then_inc(g["latT1"], 1)
                    if live(t, 0):
                        act.wait_ge(g["ln_xT_psum"], 2 * NB + t + 1)
                        if later(t, 2):
                            act.wait_ge(g["v1_psum"], t - 1)
                        act.activation(xT1[:, u, :], bank[1][:, LAT:LAT + P], ACT.Copy).then_inc(g["xT1"], 1)
                    if live(t, 3):
                        b, v = t - 3, 1 - u
                        act.wait_ge(g["pT1_psum"], b + 1)
                        act.activation(pT1[:, v, 0:H1 * P], psum[:, 6:8, :].rearrange("p a c -> p (a c)"), ACT.Copy).then_inc(g["pT1"], 1)
                    if live(t, 2):
                        b, v = t - 2, u
                        act.wait_ge(g["sub1"], b + 1)
                        act.activation(e1[:, v, :], e1[:, v, :], ACT.Exp).then_inc(g["e1"], 1)
                    if live(t, 4):
                        b, v = t - 4, u
                        act.wait_ge(g["gd1"], b + 1)
                        act.activation(gd1[:, v, 1:2], gd1[:, v, 0:1], ACT.Exp, scale=-1.0, bias=nbg1[:]).then_inc(g["ge1"], 1)
                steps(act, 5, att1)

                act.wait_ge(g["ld_moe1"], 64)
                act.wait_ge(g["h1"], NB)
                def att2(t, j, u):
                    if live(t, 6):
                        b, v = t - 6, u
                        act.wait_ge(g["yT2_psum"], b + 1)
                        if later(b, 2):
                            act.wait_ge(g["gl2_psum"], b - 1)
                            act.wait_ge(g["y_lo"], b - 1)
                        act.activation(yT2[:, v, :], bank[6][:, 0:P], ACT.Copy)
                        act.activation(y_hi[:, b, :], bank[6][:, 0:P], ACT.Copy).then_inc(g["yT_all"], 1)
                    if live(t, 4):
                        b, v = t - 4, u
                        act.wait_ge(g["max2"], b + 1)
                        if later(b, 2):
                            act.wait_ge(g["pT2_psum"], b - 1)
                        for hd in range(H2):
                            last = act.activation(p2[:, v, hd, :], bank[2 + hd][:, 0:P], ACT.Exp, bias=max2[:, v, hd:hd + 1])
                        last.then_inc(g["p2"], 1)
                    if live(t, 3):
                        act.wait_ge(g["qkT2_psum"], t - 2)
                    if live(t, 1):
                        b, v = t - 1, 1 - u
                        act.wait_ge(g["ln_xT_psum"], 3 * NB + b + 1)
                        if later(b, 2):
                            act.wait_ge(g["qkv2_psum"], b - 1)
                        act.activation(xT2[:, v, :], bank[1][:, 2 * P:3 * P], ACT.Identity, scale=col2[:, 0:1], bias=col2[:, 1:2]).then_inc(g["xT2"], 1)
                    if live(t, 3):
                        b, v = t - 3, 1 - u
                        if later(b, 2):
                            act.wait_ge(g["s2_psum"], b - 1)
                        for i in range(2):
                            last = act.activation(qkT2[:, v, i, :], bank[1][:, i * P:(i + 1) * P], ACT.Identity, scale=col2[:, 2 + i:3 + i])
                        last.then_inc(g["qkT2"], 1)
                    if live(t, 5):
                        b, v = t - 5, 1 - u
                        act.wait_ge(g["oT2_psum"], b + 1)
                        if later(b, 2):
                            act.wait_ge(g["yT2_psum"], b - 1)
                        act.activation(oT2[:, v, :], bank[6][:, 0:P], ACT.Copy).then_inc(g["oT2"], 1)
                    if live(t, 1):
                        b, v = t - 1, 1 - u
                        act.wait_ge(g["qkv2_psum"], b + 1)
                        if later(b, 2):
                            act.wait_ge(g["ss2"], b - 1)
                        act.activation(sq2[:, v, :], bank[7 * (1 - u)][:, 0:2 * P], ACT.Square).then_inc(g["sq2"], 1)
                    if live(t, 0):
                        part = bass.ds(E2 * FF // NB * t, E2 * FF // NB)
                        act.activation(w1f_hi[:, part], w1f[:, part], ACT.Copy).then_inc(g["w_hi"], 1)
                steps(act, 6, att2)
                act.wait_ge(g["chain4"], 2)
                act.activation(g2, glog, ACT.Exp).then_inc(g["act4"], 1)

                def hiddenf(grp, e):
                    for f in range(NC2):
                        n = NC2 * (E2 * grp + e) + f
                        act.wait_ge(g["hf_psum"], n + 1)
                        if f == 0 and (e >= 2 or later(grp, 1)):
                            act.wait_ge(g["eo_psum"], E2 * grp + e - 1)
                        act.activation(hidf[:, e % 2, f, :], bank[f], ACT.Gelu_apprx_tanh, bias=b1f[:, e, f:f + 1]).then_inc(g["hf"], 1)

                for e in range(E2):
                    hiddenf(0, e)
                    if e < 2:
                        act.wait_ge(g["g2T_psum"], e + 1)
                        act.activation(g2T[:, 8 * P * e:8 * P * (e + 1)].rearrange("p (a n) -> p a n", a=2), psum[0:E2, 6:8, :],
                                       ACT.Copy).then_inc(g["g2T"], 1)
                with act.Fori(1, NG) as grp:
                    for e in range(E2):
                        hiddenf(grp, e)

            @block.vector
            def _(dve):
                chained = [0]

                def link(ins):
                    chained[0] += 1
                    ins.then_inc(g["chain"], 1)
                    dve.wait_ge(g["chain"], chained[0])

                dve.wait_ge(g["ld_tok"], 64)
                link(dve.tensor_scalar(tmp[:, 2, :], dur[:], -1.0, None, ALU.max))
                link(dve.tensor_scalar(tmp[:, 3, :], tmp[:, 2, :], 1.0, None, ALU.add))
                dve.tensor_scalar(tmp[:, 0, :], tmp[:, 3, :], 2.0 ** -64, 2.0 ** 64, ALU.max, ALU.min).then_inc(g["log_in"], 1)
                dve.tensor_copy(val[:, 0:2, :], ids[:, 0:2, :])
                link(dve.tensor_copy(val[:, 3, :], ids[:, 2, :]))
                link(dve.tensor_scalar(tmp[:, 5, :], val[:, 1, :], 1.0 / MINUTES, ROUND, ALU.mult, ALU.add))
                link(dve.tensor_scalar(tmp[:, 5, :], tmp[:, 5, :], ROUND, -MINUTES, ALU.subtract, ALU.mult))
                link(dve.tensor_tensor(tmp[:, 5, :], tmp[:, 5, :], val[:, 1, :], ALU.add))
                link(dve.tensor_scalar(tmp[:, 5, :], tmp[:, 5, :], 2.0 * np.pi / MINUTES, None, ALU.mult))
                link(dve.tensor_scalar(tmp[:, 4, :], tmp[:, 5, :], 3.1415925, -3.1415925, ALU.min, ALU.max))
                link(dve.scalar_tensor_tensor(tmp[:, 5, :], tmp[:, 5, :], -1.0, tmp[:, 5, :], ALU.mult, ALU.max))
                dve.tensor_scalar(tmp[:, 5, :], tmp[:, 5, :], -1.0, np.pi / 2, ALU.mult, ALU.add).then_inc(g["trig_in"], 1)
                link(dve.tensor_scalar(tmp[:, 3, :], tmp[:, 3, :], -1.0, None, ALU.add))
                link(dve.tensor_scalar(val[:, 2, :], tmp[:, 3, :], 0.0, None, ALU.is_equal))
                link(dve.tensor_tensor(tmp[:, 3, :], tmp[:, 3, :], val[:, 2, :], ALU.add))
                link(dve.reciprocal(tmp[:, 3, :], tmp[:, 3, :]))
                link(dve.tensor_tensor(tmp[:, 3, :], tmp[:, 3, :], tmp[:, 2, :], ALU.mult))
                link(dve.tensor_tensor(val[:, 2, :], val[:, 2, :], tmp[:, 2, :], ALU.mult))
                dve.wait_ge(g["log"], 1)
                link(dve.tensor_tensor(tmp[:, 3, :], tmp[:, 3, :], tmp[:, 1, :], ALU.mult))
                link(dve.tensor_tensor(val[:, 2, :], val[:, 2, :], tmp[:, 3, :], ALU.add))
                link(dve.tensor_scalar(tmp[:, 3, :], dur[:], -1.0, 1e30, ALU.is_lt, ALU.mult))
                dve.tensor_tensor(val[:, 2, :], val[:, 2, :], tmp[:, 3, :], ALU.add).then_inc(g["val_ready"], 1)
                dve.wait_ge(g["valT_psum"], 1)
                link(dve.tensor_copy(valT[:], bank[0][:, 0:6 * NB].rearrange("p (f b) -> p f b", f=6)))
                dve.wait_ge(g["ld_const"], 96)
                dve.wait_ge(g["const_ready"], 4)
                for f, (first, n) in enumerate((WEEK, HOUR, DUR, DIFF)):
                    value = valT[:, f, :].unsqueeze(2).to_broadcast([P, NB, n])
                    for dst, side, op in ((above, 0, ALU.is_gt), (upto, 1, ALU.is_le)):
                        limit = lohi[:, side, first:first + n].unsqueeze(1).to_broadcast([P, NB, n])
                        dve.tensor_tensor(dst[:, :, first:first + n], value, limit, op)
                link(dve.tensor_copy(above[:, :, 49:51], valT[:, 4:6, :].rearrange("p f b -> p b f")))

                def ln_stats(phase, b, v):
                    n = NB * phase + b + 1
                    apart(dve)
                    dve.bn_stats(stats[:, v, :], h[:, b, :]).then_inc(g["ln_stats"], 1)
                    dve.wait_ge(g["ln_stats"], n)
                    apart(dve)
                    dve.bn_aggr(mv[:, v, :], stats[:, v, :]).then_inc(g["ln_mv"], 1)

                def ln_xhat(phase, b, v):
                    n = NB * phase + b + 1
                    dve.wait_ge(g["ln_rstd"], n)
                    if phase or later(b, 2):
                        dve.wait_ge(g["ln_xT_psum"], n - 2)
                    dve.tensor_scalar(xhat[:, v, :], h[:, b, :], mv[:, v, 0:1], rstd[:, v], ALU.subtract, ALU.mult).then_inc(g["ln_xhat"], 1)

                dve.tensor_tensor(above, above, upto, ALU.mult).then_inc(g["onehot"], 1)

                def stats_of(k, grp, source, summed, done):
                    apart(dve)
                    for b in range(GB):
                        dve.bn_stats(stats4[:, k, GB * grp + b, :], source(b)).then_inc(g[summed], 1)
                    dve.wait_ge(g[summed], GB * grp + GB)
                    apart(dve)
                    for b in range(GB):
                        last = dve.bn_aggr(mv4[:, k, GB * grp + b, :], stats4[:, k, GB * grp + b, :])
                    last.then_inc(g[done], GB)

                for t in range(NG + 2):
                    if t >= 2:
                        grp = t - 2
                        dve.wait_ge(g["ln_rstd"], GB * grp + GB)
                        if grp >= 2:
                            dve.wait_ge(g["ln_xT_psum"], GB * grp - GB)
                        for b in range(GB):
                            n = GB * grp + b
                            last = dve.tensor_scalar(xhat4[:, grp % 2, b, :], h[:, n, :], mv4[:, 1, n, 0:1], rstd4[:, 1, n], ALU.subtract, ALU.mult)
                        last.then_inc(g["ln_xhat"], GB)
                    if 1 <= t <= NG:
                        grp = t - 1
                        rows = h[:, GB * grp:GB * grp + GB, :]
                        dve.wait_ge(g["tok_rstd"], GB * grp + GB)
                        for b in range(GB):
                            n = GB * grp + b
                            last = dve.tensor_scalar(h[:, n, :], bank[2 + grp % 2][:, b * P:(b + 1) * P], mv4[:, 0, n, 0:1], rstd4[:, 0, n],
                                                     ALU.subtract, ALU.mult)
                        last.then_inc(g["tok_xhat"], 1)
                        dve.wait_ge(g["tok_xhat"], grp + 1)
                        dve.tensor_tensor(rows, rows, ln0[:, 0, :].unsqueeze(1).to_broadcast([P, GB, P]), ALU.mult).then_inc(g["tok_h"], 1)
                        dve.wait_ge(g["tok_h"], 2 * grp + 1)
                        dve.tensor_tensor(rows, rows, ln0[:, 1, :].unsqueeze(1).to_broadcast([P, GB, P]), ALU.add).then_inc(g["tok_h"], 1)
                        dve.wait_ge(g["tok_h"], 2 * grp + 2)
                        stats_of(1, grp, lambda b: h[:, GB * grp + b, :], "ln_stats", "ln_mv")
                    if t < NG:
                        dve.wait_ge(g["tok_psum"], t + 1)
                        stats_of(0, t, lambda b: bank[2 + t % 2][:, b * P:(b + 1) * P], "tok_stats", "tok_mv")


                def pos(t, j, u):
                    if live(t, 0):
                        if later(t, 2):
                            dve.wait_ge(g["pos_psum"], t - 1)
                        dve.tensor_copy(qn[64:P, u, :, :, 1, :], qT_all[64:P, :, :, bass.ds(8 * t, 8)].rearrange("p t b i -> p i t b")).then_inc(g["qn_odd"], 1)
                    if live(t, 1):
                        c, v = t - 1, 1 - u
                        dve.wait_ge(g["pos_psum"], c + 1)
                        dve.tensor_copy(posT[:, :, :, bass.ds(8 * c + 4, 4)], bank[2 * v + 1].rearrange("p (i h b) -> p b h i", i=4, h=H0)).then_inc(g["pos_second"], 1)
                dve.wait_ge(g["q_all"], NG * NT0)
                steps(dve, 1, pos)

                dve.wait_ge(g["ld_moe0"], 128)
                dve.tensor_reduce(centre[:, 0, :], w2m, AX.X, ALU.add)
                link(dve.tensor_reduce(centre[:, 1, :], b2m[:], AX.X, ALU.add))
                link(dve.tensor_scalar(centre[:], centre[:], 1.0 / P, None, ALU.mult))
                dve.tensor_tensor(w2m, w2m, centre[:, 0, :].unsqueeze(2).to_broadcast([P, E0, P]), ALU.subtract)
                dve.tensor_tensor(b2m[:], b2m[:], centre[:, 1, :].unsqueeze(2).to_broadcast([P, E0, P]), ALU.subtract).then_inc(g["centred"], 1)
                dve.wait_ge(g["centred"], 1)

                dve.wait_ge(g["ld_att0"], 80)

                def att0(t, j, u):
                    if live(t, 4):
                        ln_xhat(1, t - 4, u)
                    if live(t, 1):
                        b, v = t - 1, 1 - u
                        dve.wait_ge(g["s0_psum"], b + 1)
                        dve.tensor_reduce(negmax[:, v], psum[:, 2:4, :].rearrange("p a (t r) -> p a t r", r=P), AX.X, ALU.max,
                                          negate=True).then_inc(g["negmax0"], 1)
                    if live(t, 2):
                        b, v = t - 2, u
                        dve.wait_ge(g["pT0_psum"], b + 1)
                        if later(b, 2):
                            dve.wait_ge(g["oT0_psum"], b - 1)
                        dve.tensor_copy(probsT[:, v].rearrange("p a t r -> p (a t r)"), psum[:, 4:6, :].rearrange("p a c -> p (a c)")).then_inc(g["pT0"], 1)
                    if live(t, 1):
                        b, v = t - 1, 1 - u
                        dve.wait_ge(g["v0_psum"], b + 1)
                        if later(b, 2):
                            dve.wait_ge(g["oT0_psum"], b - 1)
                        dve.tensor_copy(vs[:, v], bank[1].rearrange("p (h e) -> p h e", h=H0)).then_inc(g["v0"], 1)
                        dve.wait_ge(g["p0"], b + 1)
                        dve.reciprocal(rsum[:, v], rsum[:, v]).then_inc(g["rsum"], 1)
                        dve.wait_ge(g["rsum"], b + 1)
                        dve.tensor_tensor(probs[:, v], probs[:, v], rsum[:, v].unsqueeze(3).to_broadcast([P, 2, NT0, P]),
                                          ALU.mult).then_inc(g["p0_normed"], 1)
                    if live(t, 3):
                        b, v = t - 3, 1 - u
                        dve.wait_ge(g["y0_psum"], b + 1)
                        dve.tensor_tensor(h[:, b, :], h[:, b, :], bank[0][:, 0:P], ALU.add).then_inc(g["y0_added"], 1)
                        dve.wait_ge(g["y0_added"], b + 1)
                        dve.tensor_tensor(h[:, b, :], h[:, b, :], bo0[:], ALU.add).then_inc(g["h0"], 1)
                        dve.wait_ge(g["h0"], b + 1)
                        ln_stats(1, b, v)
                steps(dve, 4, att0)

                dve.wait_ge(g["lg_psum"], 1)
                link(dve.tensor_copy(lg[:].rearrange("p b e -> p (b e)"), bank[2][:, 0:NB * E0]))
                experts = iota[:].unsqueeze(1).to_broadcast([P, NB, E0])

                def over(x):
                    return x.unsqueeze(2).to_broadcast([P, NB, E0])

                for k, scores in ((0, lg[:]), (1, top[:, 3])):
                    chosen = top[:, k]
                    link(dve.tensor_reduce(tops[:, k, :], scores, AX.X, ALU.max))
                    link(dve.tensor_tensor(chosen, scores, over(tops[:, k, :]), ALU.is_equal))
                    link(dve.scalar_tensor_tensor(chosen, chosen, -1000.0, experts, ALU.mult, ALU.add))
                    link(dve.tensor_reduce(tops[:, 2, :], chosen, AX.X, ALU.min))
                    link(dve.tensor_tensor(chosen, chosen, over(tops[:, 2, :]), ALU.is_equal))
                    if k == 0:
                        link(dve.scalar_tensor_tensor(top[:, 3], chosen, -3e38, lg[:], ALU.mult, ALU.add))
                dve.tensor_tensor(tops[:, 3, :], tops[:, 1, :], tops[:, 0, :], ALU.subtract).then_inc(g["tops"], 1)
                dve.wait_ge(g["topexp"], 1)
                link(dve.tensor_scalar(tops[:, 5, :], tops[:, 4, :], 1.0, None, ALU.add))
                link(dve.reciprocal(tops[:, 5, :], tops[:, 5, :]))
                link(dve.tensor_tensor(tops[:, 4, :], tops[:, 4, :], tops[:, 5, :], ALU.mult))
                dve.tensor_tensor(top[:, 0], top[:, 0], over(tops[:, 5, :]), ALU.mult)
                link(dve.tensor_tensor(top[:, 1], top[:, 1], over(tops[:, 4, :]), ALU.mult))
                dve.tensor_tensor(gates[:], top[:, 0], top[:, 1], ALU.add).then_inc(g["gates"], 1)

                dve.wait_ge(g["ld_att1"], 240)
                link(dve.tensor_scalar(nbg1[:], nbg1[:], -1.0, None, ALU.mult))
                dve.tensor_scalar(qbias[:], b1a[:, 0:3:2], float(D1) ** -0.5, None, ALU.mult).then_inc(g["ready1"], 1)

                def add_betas(part):
                    rows = h[:, 8 * part:8 * part + 8, :]
                    dve.wait_ge(g["beta_psum"], part + 1)
                    dve.wait_ge(g["h_moe0"], NB if part else 2)
                    dve.tensor_tensor(rows, rows, psum[:, 6:8, :].rearrange("p a (b n) -> p (a b) n", n=P), ALU.add).then_inc(g["h_beta"], 1)
                    dve.wait_ge(g["h_beta"], part + 1)

                def moe0(t, j, u):
                    if live(t, 1):
                        b, v = t - 1, 1 - u
                        dve.wait_ge(g["ysq"], b + 1)
                        dve.tensor_scalar(yvar[:, v], ysum2[:, v], 1.0 / P, EPS, ALU.mult, ALU.add).then_inc(g["yvar"], 1)
                    if live(t, 0):
                        dve.wait_ge(g["y_psum"], t + 1)
                        if later(t, 2):
                            dve.wait_ge(g["yg"], t - 1)
                            dve.wait_ge(g["ysq"], t - 1)
                        dve.tensor_tensor(ym[:, u].rearrange("p e n -> p (e n)"), psum[:, 2 + 2 * u:4 + 2 * u, :].rearrange("p a c -> p (a c)"),
                                          b2m[:].rearrange("p e n -> p (e n)"), ALU.add).then_inc(g["ym"], 1)
                    if live(t, 2):
                        b, v = t - 2, u
                        dve.wait_ge(g["yc"], b + 1)
                        dve.tensor_reduce(ysum[:, v, :], yc[:, v].rearrange("p e n -> p n e"), AX.X, ALU.add).then_inc(g["ysum"], 1)
                        dve.wait_ge(g["ysum"], b + 1)
                        dve.tensor_tensor(h[:, b, :], h[:, b, :], ysum[:, v, :], ALU.add).then_inc(g["h_moe0"], 1)
                    if live(t, 1):
                        b, v = t - 1, 1 - u
                        dve.wait_ge(g["yrstd"], b + 1)
                        dve.tensor_tensor(ycoef[:, v], yrstd[:, v], gates[:, b, :], ALU.mult).then_inc(g["ycoef"], 1)
                    if live(t, 1):
                        b, v = t - 1, 1 - u
                        dve.wait_ge(g["ycoef"], b + 1)
                        dve.wait_ge(g["yg"], b + 1)
                        dve.tensor_tensor(yc[:, v], yg[:, v], ycoef[:, v].unsqueeze(2).to_broadcast([P, E0, P]), ALU.mult).then_inc(g["yc"], 1)
                    if isinstance(t, int) and t == 3:
                        add_betas(0)
                steps(dve, 2, moe0)
                add_betas(1)

                dve.wait_ge(g["h_beta"], 2)
                dve.wait_ge(g["vs_ones"], 3)

                def att1(t, j, u):
                    if live(t, 0):
                        ln_stats(2, t, u)
                    if live(t, 2):
                        b, v = t - 2, u
                        dve.wait_ge(g["v1_psum"], b + 1)
                        dve.tensor_tensor(v1[:, b, :, 0:D1], bank[1][:, 0:P].rearrange("p (h e) -> p h e", h=H1),
                                          bv1[:].rearrange("p (h e) -> p h e", h=H1), ALU.add)
                        dve.tensor_copy(gx1[:, bass.ds(b, 1)], bank[1][:, P:P + 1])
                        for odd in range(2):
                            rows = slice(CH * odd, CH * odd + CH)
                            heads = bank[1][rows, P + 1:P + 1 + LH * LD].rearrange("p (a o e) -> p a o e", a=2, o=2)[:, :, odd, :]
                            bias = brv1[rows, :].rearrange("p (a o e) -> p a o e", a=2, o=2)[:, :, odd, :]
                            last = dve.scalar_tensor_tensor(gv1[rows, b, :, odd, 0:LD], heads, 0.5, bias, ALU.mult, ALU.add)
                        last.then_inc(g["v1"], 1)
                    if live(t, 5):
                        b, v = t - 5, 1 - u
                        dve.wait_ge(g["ge1"], b + 1)
                        dve.tensor_scalar(gd1[:, v, 2:3], gd1[:, v, 1:2], 1.0, None, ALU.add).then_inc(g["gate1_parts"], 1)
                        dve.wait_ge(g["gate1_parts"], 2 * b + 1)
                        dve.reciprocal(gd1[:, v, 2:3], gd1[:, v, 2:3]).then_inc(g["gate1_parts"], 1)
                        dve.wait_ge(g["gate1_parts"], 2 * b + 2)
                        dve.tensor_scalar(gd1[:, v, 3:4], gd1[:, v, 2:3], -1.0, 1.0, ALU.mult, ALU.add).then_inc(g["gate1"], 1)
                        if later(b, 2):
                            dve.wait_ge(g["catT1_psum"], b - 1)
                        dve.tensor_scalar(cat1[:, v, 0:P], loc1[:, v, :], gd1[:, v, 2:3], None, ALU.mult)
                        dve.wait_ge(g["gate1"], b + 1)
                        dve.tensor_scalar(cat1[:, v, P:P + LH * LD], lat1[:, v, :], gd1[:, v, 3:4], None, ALU.mult)
                        dve.tensor_copy(cat1[:, v, P + LH * LD:], gd1[:, v, 3:4]).then_inc(g["cat1"], 1)
                    if live(t, 0):
                        ln_xhat(2, t, u)
                    if live(t, 2):
                        b, v = t - 2, u
                        dve.wait_ge(g["s1_psum"], b + 1)
                        local = psum[:, 2:4, :].rearrange("p a (o r) -> p (a o) r", r=P)
                        latent = bank[4][:, 0:LAT].rearrange("p (a r) -> p a r", r=CH)
                        dve.tensor_reduce(max1[:, v, 0:H1], local, AX.X, ALU.max)
                        dve.tensor_reduce(max1[:, v, H1:], latent, AX.X, ALU.max).then_inc(g["max1"], 1)
                    if live(t, 4):
                        b, v = t - 4, u
                        dve.wait_ge(g["o1_psum"], b + 1)
                        heads = bank[5][:, 0:(H1 + LH) * (D1 + 1)].rearrange("p (h e) -> p h e", h=H1 + LH)
                        dve.reciprocal(sum1[:, v, :].unsqueeze(2), heads[:, :, D1:D1 + 1]).then_inc(g["rsum"], 1)
                        dve.wait_ge(g["rsum"], 1 * NB + b + 1)
                        dve.tensor_tensor(loc1[:, v, :].rearrange("p (h e) -> p h e", h=H1), heads[:, 0:H1, 0:D1],
                                          sum1[:, v, 0:H1].unsqueeze(2).to_broadcast([P, H1, D1]), ALU.mult)
                        dve.scalar_tensor_tensor(lat1[:, v, :].rearrange("p (h e) -> p h e", h=LH), heads[:, H1:, 0:D1], valid[:],
                                                 sum1[:, v, H1:].unsqueeze(2).to_broadcast([P, LH, LD]), ALU.mult, ALU.mult).then_inc(g["o1"], 1)
                    if live(t, 2):
                        b, v = t - 2, u
                        dve.wait_ge(g["max1"], b + 1)
                        if later(b, 2):
                            dve.wait_ge(g["pT1_psum"], b - 1)
                        dve.tensor_tensor(e1[:, v, 0:H1 * P].rearrange("p (a r) -> p a r", r=P), local,
                                          max1[:, v, 0:H1].unsqueeze(2).to_broadcast([P, H1, P]), ALU.subtract)
                        dve.tensor_tensor(e1[:, v, H1 * P:].rearrange("p (a r) -> p a r", a=4), latent,
                                          max1[:, v, H1:].unsqueeze(2).to_broadcast([P, LH, CH]), ALU.subtract).then_inc(g["sub1"], 1)
                    if live(t, 5):
                        b, v = t - 5, 1 - u
                        dve.wait_ge(g["y1_psum"], b + 1)
                        dve.tensor_tensor(h[:, b, :], h[:, b, :], bank[5][:, 2 * P:3 * P], ALU.add).then_inc(g["y1_added"], 1)
                        dve.wait_ge(g["y1_added"], b + 1)
                        dve.tensor_tensor(h[:, b, :], h[:, b, :], bo1[:], ALU.add).then_inc(g["h1"], 1)
                    if live(t, 4):
                        b, v = t - 4, u
                        dve.wait_ge(g["o1"], b + 1)
                        dve.scalar_tensor_tensor(gw1[:, v, :], loc1[:, v, :], 1.0, wg1[:], ALU.mult, ALU.mult,
                                                 accum_out=gd1[:, v, 0:1]).then_inc(g["gate1_dot"], 1)
                        dve.wait_ge(g["gate1_dot"], b + 1)
                        dve.tensor_tensor(gd1[:, v, 0:1], gd1[:, v, 0:1], gx1[:, bass.ds(b, 1)], ALU.add).then_inc(g["gd1"], 1)
                steps(dve, 5, att1)

                dve.wait_ge(g["h1"], NB)
                dve.wait_ge(g["ld_att2"], 80)
                link(dve.tensor_scalar(col2[:, 2:3], col2[:, 2:3], float(D2) ** 0.5, None, ALU.mult))

                def att2(t, j, u):
                    if live(t, 2):
                        b, v = t - 2, u
                        dve.wait_ge(g["sq2"], b + 1)
                        if later(b, 2):
                            dve.wait_ge(g["ss2e"], b - 1)
                        dve.tensor_reduce(ss2[:, v], sq2[:, v].rearrange("p (h e) -> p h e", e=D2), AX.X, ALU.add).then_inc(g["ss2"], 1)
                    if live(t, 4):
                        b, v = t - 4, u
                        dve.wait_ge(g["s2_psum"], b + 1)
                        if later(b, 2):
                            dve.wait_ge(g["p2"], b - 1)
                        dve.tensor_reduce(max2[:, v], psum[:, 2:4, 0:P], AX.X, ALU.max, negate=True).then_inc(g["max2"], 1)
                    if live(t, 0):
                        ln_stats(3, t, u)
                    if live(t, 5):
                        b, v = t - 5, 1 - u
                        dve.wait_ge(g["o2_psum"], b + 1)
                        heads = bank[5][:, 0:H2 * (D2 + 1)].rearrange("p (h e) -> p h e", h=H2)
                        dve.reciprocal(sum2[:, v, :].unsqueeze(2), heads[:, :, D2:D2 + 1]).then_inc(g["rsum"], 1)
                        dve.wait_ge(g["rsum"], 2 * NB + b + 1)
                        if later(b, 2):
                            dve.wait_ge(g["oT2_psum"], b - 1)
                        dve.tensor_tensor(o2[:, v, :].rearrange("p (h e) -> p h e", h=H2), heads[:, :, 0:D2],
                                          sum2[:, v, :].unsqueeze(2).to_broadcast([P, H2, D2]), ALU.mult).then_inc(g["o2"], 1)
                    if live(t, 4):
                        dve.wait_ge(g["pT2_psum"], t - 3)
                    if live(t, 6):
                        b, v = t - 6, u
                        dve.wait_ge(g["gl2_psum"], b + 1)
                        dve.tensor_tensor(glog[:, b, :], bank[4][:, 2 * P:2 * P + E2], gb2[:], ALU.add).then_inc(g["gl2"], 1)
                    if live(t, 4):
                        b, v = t - 4, u
                        if later(b, 2):
                            dve.wait_ge(g["o2_psum"], b - 1)
                        dve.tensor_copy(pT2[:, v].rearrange("p h r -> p (h r)"), bank[4][:, 0:2 * P]).then_inc(g["pT2"], 1)
                    if live(t, 0):
                        ln_xhat(3, t, u)
                    if live(t, 2):
                        b, v = t - 2, u
                        dve.wait_ge(g["rn2"], b + 1)
                        if later(b, 2):
                            dve.wait_ge(g["qkT2_psum"], b - 1)
                        source = bank[7 * u]
                        dve.tensor_tensor(qk2[:, v].rearrange("p (h e) -> p h e", e=D2), source[:, 0:2 * P].rearrange("p (h e) -> p h e", e=D2),
                                          rn2[:, v].unsqueeze(2).to_broadcast([P, 2 * H2, D2]), ALU.mult)
                        dve.tensor_copy(v2[:, b, :, 0:D2], source[:, 2 * P:3 * P].rearrange("p (h e) -> p h e", e=D2)).then_inc(g["qk2"], 1)
                steps(dve, 6, att2)

                dve.wait_ge(g["gl2"], NB)
                dve.tensor_reduce(gsum[:, 0, :], glog, AX.X, ALU.max).then_inc(g["chain4"], 1)
                dve.wait_ge(g["chain4"], 1)
                dve.tensor_tensor(glog, glog, over(gsum[:, 0, :]), ALU.subtract).then_inc(g["chain4"], 1)
                dve.wait_ge(g["act4"], 1)
                link(dve.tensor_reduce(gsum[:, 1, :], g2, AX.X, ALU.add))
                link(dve.reciprocal(gsum[:, 1, :], gsum[:, 1, :]))
                dve.tensor_tensor(g2, g2, over(gsum[:, 1, :]), ALU.mult).then_inc(g["g2"], 1)

                def experts2(grp):
                    for e in range(E2):
                        n = E2 * grp + e
                        if isinstance(grp, int) and grp == 0 and e < 2:
                            rows = h[:, 8 * e:8 * e + 8, :]
                            dve.wait_ge(g["b2_psum"], e + 1)
                            dve.tensor_tensor(rows, rows, psum[:, 6:8, :].rearrange("p a (b n) -> p (a b) n", n=P), ALU.add).then_inc(g["h_b2"], 1)
                            dve.wait_ge(g["h_b2"], e + 1)
                        dve.wait_ge(g["eo_psum"], n + 1)
                        if e > 0:
                            dve.wait_ge(g["acc"], n)
                        elif later(grp, 1):
                            dve.wait_ge(g["stored"], 16 * grp)
                        for u in range(GB):
                            b = GB * grp + u
                            last = dve.scalar_tensor_tensor(acc[:, u, :], bank[4 + e % 2][:, u * P:(u + 1) * P], g2[:, b, e:e + 1],
                                                            h[:, b, :] if e == 0 else acc[:, u, :], ALU.mult, ALU.add)
                        last.then_inc(g["acc"], 1)
                    dve.wait_ge(g["acc"], E2 * grp + E2)
                    dve.sem_inc(g["out_acc"], 1)
                experts2(0)
                with dve.Fori(1, NG) as grp:
                    experts2(grp)

            @block.tensor
            def _(pe):
                pe.wait_ge(g["ld_const"], 96)
                pe.matmul(bank[1][0:NF, 0:P], tab_l[:], tab_r[:], start=True, stop=True).then_inc(g["table_psum"], 1)
                pe.wait_ge(g["trig"], 1)
                pe.wait_ge(g["val_ready"], 1)
                for f in range(6):
                    last = pe.transpose(bank[0][:, f * NB:(f + 1) * NB], val[:, f, :], ident[0:NB, 0:NB])
                last.then_inc(g["valT_psum"], 1)
                pe.wait_ge(g["table_ready"], 1)
                pe.wait_ge(g["ld_att0"], 80)

                def ln_transpose(phase, b, v, dst):
                    pe.wait_ge(g["ln_xhat"], NB * phase + b + 1)
                    pe.transpose(dst[:, 0:P], xhat[:, v, :], ident[:]).then_inc(g["ln_xT_psum"], 1)

                pe.wait_ge(g["onehot"], 1)
                for t in range(NG + 2):
                    if t < NG:
                        if t >= 2:
                            pe.wait_ge(g["onehotT"], t - 1)
                        for b in range(GB):
                            last = pe.transpose(bank[t % 2][0:NF, b * P:(b + 1) * P], above[:, GB * t + b, :], ident[:])
                        last.then_inc(g["onehotT_psum"], 1)
                        pe.wait_ge(g["onehotT"], t + 1)
                        if t >= 2:
                            pe.wait_ge(g["tok_xhat"], t - 1)
                        for b in range(GB):
                            last = pe.matmul(bank[2 + t % 2][:, b * P:(b + 1) * P], onehotT[:, t % 2, b * P:(b + 1) * P], table[:], start=True, stop=True)
                        last.then_inc(g["tok_psum"], 1)
                    if t >= 2:
                        grp = t - 2
                        pe.wait_ge(g["ln_xhat"], GB * grp + GB)
                        if grp >= 2:
                            pe.wait_ge(g["ln_xT"], GB * grp - GB)
                        for b in range(GB):
                            last = pe.transpose(bank[4 + grp % 2][:, b * P:(b + 1) * P], xhat4[:, grp % 2, b, :], ident[:])
                        last.then_inc(g["ln_xT_psum"], GB)
                        pe.wait_ge(g["ln_xT"], GB * grp + GB)
                        for tile in range(NT0):
                            n = NT0 * grp + tile
                            if n >= 2:
                                pe.wait_ge(g["q_all"], n - 1)
                            pe.matmul(bank[6 + tile % 2], wq0[:, tile * P:(tile + 1) * P], xT_all[:, GB * grp:GB * grp + GB, :],
                                      start=True, stop=True).then_inc(g["q_psum"], 1)

                def pos(c, j, u):
                    if live(c, 0):
                        for done in ("qn_even", "qn_odd", "relw"):
                            pe.wait_ge(g[done], c + 1)
                        if later(c, 2):
                            pe.wait_ge(g["pos_first"], c - 1)
                            pe.wait_ge(g["pos_second"], c - 1)
                        for i in range(8):
                            last = pe.matmul(bank[2 * u + i // 4][:, i % 4 * P:(i % 4 + 1) * P], relw[:, u, 7 - i:7 - i + P],
                                             qn[:, u, i].rearrange("p t o b -> p (t o b)"), start=True, stop=True)
                        last.then_inc(g["pos_psum"], 1)
                steps(pe, 0, pos)

                pe.wait_ge(g["pos_first"], NB)
                pe.wait_ge(g["pos_second"], NB)

                def routing(first, end):
                    pe.wait_ge(g["ld_moe0"], 128)
                    pe.wait_ge(g["p0"], NB)
                    pe.wait_ge(g["ln_xT"], NB + end)
                    for b in range(first, end):
                        last = pe.matmul(bank[2][:, b * E0:(b + 1) * E0], xT_all[:, b, :], wgm[:], start=True, stop=True)
                    if end == NB:
                        last.then_inc(g["lg_psum"], 1)

                def att0(t, j, u):
                    if live(t, 1):
                        b, v = t - 1, 1 - u
                        pe.wait_ge(g[f"att0_in{1 - u}"], 48 * (j + u))
                        pe.wait_ge(g["k0"], b + 1)
                        if later(b, 1):
                            pe.wait_ge(g["p0"], b)
                        for odd in range(2):
                            for tile in range(NT0):
                                pe.matmul(bank[2 + odd][:, tile * P:(tile + 1) * P], posTs[:, v, 2 * tile + odd, :], ident[:],
                                          start=(tile == 0), stop=False, skip_group_check=True)
                        for tile in range(NT0):
                            for odd in range(2):
                                rows = slice(64 * odd, 64 * odd + 64)
                                last = pe.matmul(bank[2 + odd][:, tile * P:(tile + 1) * P], qTs[rows, v, tile, :],
                                                 kTs[rows, v, tile, :], start=False, stop=(tile == NT0 - 1), skip_group_check=True)
                        last.then_inc(g["s0_psum"], 1)
                    if live(t, 0):
                        if later(t, 4):
                            pe.wait_ge(g["y0_added"], t - 3)
                        elif later(t, 1):
                            pe.wait_ge(g["k0"], t)
                        if not isinstance(t, int) or t < 2:
                            pe.wait_ge(g["q_all"], NG * NT0)
                        for tile in range(NT0):
                            last = pe.matmul(bank[0][:, tile * P:(tile + 1) * P], wkv0[:, tile * P:(tile + 1) * P],
                                             xT_all[:, t, :], start=True, stop=True)
                        last.then_inc(g["k0_psum"], 1)
                    if live(t, 2):
                        b, v = t - 2, u
                        pe.wait_ge(g["p0_normed"], b + 1)
                        if later(b, 1):
                            pe.wait_ge(g["pT0"], b)
                        for odd in range(2):
                            for tile in range(NT0):
                                last = pe.transpose(bank[4 + odd][:, tile * P:(tile + 1) * P], probs[:, v, odd, tile, :], ident[:])
                        last.then_inc(g["pT0_psum"], 1)
                    if live(t, 1):
                        if later(t, 2):
                            pe.wait_ge(g["v0"], t - 1)
                        pe.matmul(bank[1], xTs[:, 1 - u, :], wkv0[:, H0 * D0:], start=True, stop=True).then_inc(g["v0_psum"], 1)
                    if live(t, 4):
                        b = t - 4
                        if later(b, 1):
                            pe.wait_ge(g["ln_xT"], NB + b)
                        ln_transpose(1, b, u, bank[7][:, 3 * P:])
                    if live(t, 3):
                        b, v = t - 3, 1 - u
                        pe.wait_ge(g["oT0"], b + 1)
                        if live(t, 0):
                            pe.wait_ge(g["k0"], t + 1)
                        else:
                            pe.wait_ge(g["y0_added"], b)
                        for tile in range(NT0):
                            last = pe.matmul(bank[0][:, 0:P], oT0[:, v, tile, :], wo0[:, tile, :], start=(tile == 0), stop=(tile == NT0 - 1))
                        last.then_inc(g["y0_psum"], 1)
                    if live(t, 2):
                        b, v = t - 2, u
                        pe.wait_ge(g["pT0"], b + 1)
                        pe.wait_ge(g["v0"], b + 1)
                        if later(b, 1):
                            pe.wait_ge(g["oT0"], b)
                        for tile in range(NT0):
                            for odd in range(2):
                                last = pe.matmul(bank[6][64 * odd:64 * odd + 64, tile * P:(tile + 1) * P], vs[:, v, 2 * tile + odd, :],
                                                 probsT[:, v, odd, tile, :], start=True, stop=True)
                        last.then_inc(g["oT0_psum"], 1)
                    if isinstance(t, int) and t > NB:
                        routing(0 if t == NB + 1 else t - 5, t - 4)
                steps(pe, 4, att0)

                routing(NB - 1, NB)

                pe.wait_ge(g["pT0"], NB)
                pe.wait_ge(g["oT0"], NB)
                pe.wait_ge(g["ld_att1"], 240)
                pe.matmul(bank[7][0:LH * LD + 1, 0:P], wroT[:], wo1[:], start=True, stop=True).then_inc(g["wro_psum"], 1)
                pe.wait_ge(g["centred"], 1)
                pe.wait_ge(g["h0"], NB)

                def weights_transposed(part):
                    pe.wait_ge(g["gates"], 1)
                    pe.wait_ge(g["wro1"], 1)
                    if part:
                        pe.wait_ge(g["h_beta"], part)
                    for b in range(8):
                        last = pe.transpose(bank[6 + b // GB][0:E0, b % GB * P:(b % GB + 1) * P], gates[:, 8 * part + b, :], ident[:])
                    last.then_inc(g["gT_psum"], 1)

                def betas(part):
                    pe.wait_ge(g["gT"], part + 1)
                    for b in range(8):
                        n = 8 * part + b
                        last = pe.matmul(bank[6 + b // GB][:, b % GB * P:(b % GB + 1) * P], gT[:, n * P:(n + 1) * P], beta[:], start=True, stop=True)
                    last.then_inc(g["beta_psum"], 1)

                def moe0(t, j, u):
                    if isinstance(t, int) and t == 3:
                        weights_transposed(1)
                    for half in range(2):
                        if live(t, 0, NB // 2):
                            for pair in (2 * half, 2 * half + 1):
                                if pair >= 2 or later(t, 1):
                                    pe.wait_ge(g["hid"], 4 * t + pair - 1)
                                for e in (2 * pair, 2 * pair + 1):
                                    last = pe.matmul(bank[pair % 2][:, e % 2 * 2 * P:(e % 2 + 1) * 2 * P], w1m[:, e, :],
                                                     xT_all[:, bass.ds(2 * t, 2), :], start=True, stop=True)
                                last.then_inc(g["hid_psum"], 1)
                        if live(t, 1, NB // 2):
                            if half == 0:
                                pe.wait_ge(g["hid"], 4 * t)
                            if later(t, 2):
                                pe.wait_ge(g["ym"], 2 * t - 3 + half)
                            for e in range(E0):
                                last = pe.matmul(bank[2 + 2 * half + e // 4][:, e % 4 * P:(e % 4 + 1) * P],
                                                 hid[:, 1 - u, e, half * P:(half + 1) * P], w2m[:, e, :], start=True, stop=True)
                            last.then_inc(g["y_psum"], 1)
                    if isinstance(t, int) and t in (2, 3):
                        betas(t - 2)
                    if isinstance(t, int) and t == 1:
                        weights_transposed(0)
                steps(pe, 1, moe0, NB // 2)

                pe.wait_ge(g["ld_att1"], 240)
                pe.wait_ge(g["ym"], NB)
                pe.wait_ge(g["h_beta"], 2)

                def att1(t, j, u):
                    if live(t, 1):
                        b, v = t - 1, 1 - u
                        pe.wait_ge(g["xT1"], b + 1)
                        pe.wait_ge(g["pool1"], b + 1)
                        if later(t, 6):
                            pe.wait_ge(g["catT1"], t - 5)
                        elif later(b, 1):
                            pe.wait_ge(g["k1"], b)
                        for i in range(3):
                            pe.matmul(bank[0][:, i * P:(i + 1) * P], wqk1[:, i, :], xT1[:, v, :], start=True, stop=True)
                        pe.matmul(bank[0][:, 3 * P:3 * P + CH], wqk1[:, 3, :], pool1[:, v, 0, :], start=True, stop=True).then_inc(g["proj1_psum"], 1)
                    if live(t, 2):
                        pe.wait_ge(g["k1"], t - 1)
                        pe.wait_ge(g["kx1"], t - 1)
                        if later(t, 3):
                            pe.wait_ge(g["sub1"], t - 2)
                    for part in range(3):
                        if live(t, 2):
                            dst = bank[2 + part][:, 0:BANK if part < 2 else LAT]
                            mask = (maskb[:, 0:P].unsqueeze(1).to_broadcast([P, NT0, P]) if part < 2 else
                                    maskb[:, P:].unsqueeze(1).to_broadcast([P, LH, CH]))
                            queries, keys = (qT1, kx1[:, u, 4 * part:4 * part + 4, :]) if part < 2 else (rqT1, gkx1[:, u])
                            pe.matmul(dst.rearrange("p (h r) -> p h r", h=4), identb[:], mask, start=True, stop=False, skip_group_check=True)
                            last = pe.matmul(dst, queries[:, u, :], keys.rearrange("p h r -> p (h r)"), start=False, stop=True, skip_group_check=True)
                            if part == 2:
                                last.then_inc(g["s1_psum"], 1)
                        if live(t, 4):
                            b = t - 4
                            if part == 0:
                                pe.wait_ge(g["pT1"], b + 1)
                                pe.wait_ge(g["latT1"], b + 1)
                                pe.wait_ge(g["v1"], b + 1)
                                if later(b, 2):
                                    pe.wait_ge(g["y1_added"], b - 1)
                                elif later(b, 1):
                                    pe.wait_ge(g["o1"], b)
                            if part < 2:
                                for hd in range(4 * part, 4 * part + 4):
                                    pe.matmul(bank[5][:, hd * (D1 + 1):(hd + 1) * (D1 + 1)], pT1[:, u, hd * P:(hd + 1) * P], v1[:, b, hd, :],
                                              start=True, stop=True)
                            else:
                                for i in range(2):
                                    c = (H1 + 2 * i) * (D1 + 1)
                                    last = pe.matmul(bank[5][:, c:c + 2 * (LD + 1)], pT1[:, u, (H1 + i) * P:(H1 + i + 1) * P],
                                                     gv1[:, b, i].rearrange("p o e -> p (o e)"), start=True, stop=True)
                                last.then_inc(g["o1_psum"], 1)
                    if live(t, 5):
                        b, v = t - 5, 1 - u
                        pe.wait_ge(g["cat1"], b + 1)
                        if live(t, 1):
                            pe.wait_ge(g["k1"], t)
                        elif later(b, 1):
                            pe.wait_ge(g["catT1"], b)
                        pe.transpose(bank[0][:, 0:P], cat1[:, v, 0:P], ident[:])
                        pe.transpose(bank[0][0:LH * LD + 1, P:2 * P], cat1[:, v, P:], ident[:]).then_inc(g["catT1_psum"], 1)
                    if live(t, 3):
                        b, v = t - 3, 1 - u
                        pe.wait_ge(g["e1"], b + 1)
                        if live(t, 2):
                            pe.wait_ge(g["v1"], t - 1)
                        else:
                            pe.wait_ge(g["latT1"], b)
                        for i in range(2):
                            last = pe.transpose(bank[1][:, i * P:(i + 1) * P], e1[:, v, (H1 + i) * P:(H1 + i + 1) * P], ident[:])
                        last.then_inc(g["latT_psum"], 1)
                    if live(t, 0):
                        if live(t, 2) and not live(t, 3):
                            pe.wait_ge(g["v1"], t - 1)
                        if later(t, 1):
                            pe.wait_ge(g["xT1"], t)
                        ln_transpose(2, t, u, bank[1][:, LAT:])
                    if live(t, 3):
                        b, v = t - 3, 1 - u
                        if later(b, 1):
                            pe.wait_ge(g["pT1"], b)
                        for hd in range(H1):
                            last = pe.transpose(bank[6 + hd // 4][:, hd % 4 * P:(hd % 4 + 1) * P], e1[:, v, hd * P:(hd + 1) * P], ident[:])
                        last.then_inc(g["pT1_psum"], 1)
                    if live(t, 1):
                        b, v = t - 1, 1 - u
                        if live(t, 0):
                            pe.wait_ge(g["xT1"], t + 1)
                        else:
                            pe.wait_ge(g["latT1"], t - 2)
                        pe.matmul(bank[1][:, 0:P + 1], xT1[:, v, :], wv1[:], start=True, stop=True)
                        pe.matmul(bank[1][:, P + 1:P + 1 + LH * LD], pool1[:, v].rearrange("p a c -> p (a c)"), wrv1[:], start=True, stop=True).then_inc(g["v1_psum"], 1)
                    if live(t, 5):
                        b, v = t - 5, 1 - u
                        pe.wait_ge(g["catT1"], b + 1)
                        if live(t, 4):
                            pe.wait_ge(g["o1"], t - 3)
                        else:
                            pe.wait_ge(g["y1_added"], b)
                        pe.matmul(bank[5][:, 2 * P:3 * P], catT1[:, v, 0, :], wo1[:], start=True, stop=False)
                        pe.matmul(bank[5][:, 2 * P:3 * P], catT1[0:LH * LD + 1, v, 1, :], wro1[:], start=False, stop=True).then_inc(g["y1_psum"], 1)
                steps(pe, 5, att1)

                pe.wait_ge(g["ld_att2"], 80)
                pe.wait_ge(g["h1"], NB)

                def att2(t, j, u):
                    if live(t, 1):
                        if later(t, 2):
                            pe.wait_ge(g["xT2"], t - 1)
                        if later(t, 4):
                            pe.wait_ge(g["qkT2"], t - 3)
                        ln_transpose(3, t - 1, 1 - u, bank[1][:, 2 * P:3 * P])
                    if live(t, 3):
                        b, v = t - 3, 1 - u
                        pe.wait_ge(g["qk2"], b + 1)
                        if not live(t, 1) and later(b, 1):
                            pe.wait_ge(g["qkT2"], b)
                        for i in range(2):
                            last = pe.transpose(bank[1][:, i * P:(i + 1) * P], qk2[:, v, i * P:(i + 1) * P], ident[:])
                        last.then_inc(g["qkT2_psum"], 1)
                    if live(t, 6):
                        b, v = t - 6, u
                        pe.wait_ge(g["yT_all"], b + 1)
                        pe.wait_ge(g["pT2"], (t - 4) if live(t, 5) else NB)
                        if later(b, 1):
                            pe.wait_ge(g["gl2"], b)
                        pe.matmul(bank[4][:, 2 * P:2 * P + E2], yT2[:, v, :], gw2[:], start=True, stop=True).then_inc(g["gl2_psum"], 1)
                    if live(t, 4):
                        b, v = t - 4, u
                        pe.wait_ge(g["p2"], b + 1)
                        if later(b, 1):
                            pe.wait_ge(g["pT2"], b)
                        for hd in range(H2):
                            last = pe.transpose(bank[4][:, hd * P:(hd + 1) * P], p2[:, v, hd, :], ident[:])
                        last.then_inc(g["pT2_psum"], 1)
                    if live(t, 5):
                        b, v = t - 5, 1 - u
                        pe.wait_ge(g["o2"], b + 1)
                        if later(b, 1):
                            pe.wait_ge(g["yT_all"], b)
                        pe.transpose(bank[6][:, 0:P], o2[:, v, :], ident[:]).then_inc(g["oT2_psum"], 1)
                    if live(t, 1):
                        b, v = t - 1, 1 - u
                        pe.wait_ge(g["xT2"], b + 1)
                        if later(b, 2):
                            pe.wait_ge(g["qk2"], b - 1)
                        pe.matmul(bank[7 * (1 - u)][:, 0:3 * P], xT2[:, v, :], wqkv2[:], start=True, stop=True).then_inc(g["qkv2_psum"], 1)
                    if live(t, 3):
                        b, v = t - 3, 1 - u
                        pe.wait_ge(g["qkT2"], b + 1)
                        if later(b, 1):
                            pe.wait_ge(g["p2"], b)
                        for hd in range(H2):
                            pe.matmul(bank[2 + hd][:, 0:P], identb[:], maskb[:, 0:P], start=True, stop=False, skip_group_check=True)
                        for hd in range(H2):
                            rows = slice(D2 * hd, D2 * hd + D2)
                            last = pe.matmul(bank[2 + hd][:, 0:P], qkT2[rows, v, 0, :], qkT2[rows, v, 1, :], start=False, stop=True, skip_group_check=True)
                        last.then_inc(g["s2_psum"], 1)
                    if live(t, 5):
                        b, v = t - 5, 1 - u
                        pe.wait_ge(g["oT2"], b + 1)
                        pe.matmul(bank[6][:, 0:P], wo2[:], oT2[:, v, :], start=True, stop=True).then_inc(g["yT2_psum"], 1)
                    if live(t, 4):
                        b, v = t - 4, u
                        pe.wait_ge(g["pT2"], b + 1)
                        if later(b, 1):
                            pe.wait_ge(g["o2"], b)
                        for hd in range(H2):
                            last = pe.matmul(bank[5][:, hd * (D2 + 1):(hd + 1) * (D2 + 1)], pT2[:, v, hd, :], v2[:, b, hd, :], start=True, stop=True)
                        last.then_inc(g["o2_psum"], 1)
                steps(pe, 6, att2)

                pe.wait_ge(g["w_lo"], NB)
                pe.wait_ge(g["y_lo"], NB)
                pe.wait_ge(g["gl2"], NB)

                def up(grp, e):
                    for f in range(NC2):
                        n = NC2 * (E2 * grp + e) + f
                        if e > 0 or later(grp, 1):
                            pe.wait_ge(g["hf"], n - NC2 + 1)
                        cols, span = slice(e * FF + f * P, e * FF + (f + 1) * P), bass.ds(GB * grp, GB)
                        pe.matmul(bank[f], w1f_hi[:, cols], y_hi[:, span, :], start=True, stop=False)
                        pe.matmul(bank[f], w1f_lo[:, cols], y_hi[:, span, :], start=False, stop=False)
                        pe.matmul(bank[f], w1f_hi[:, cols], y_lo[:, span, :], start=False, stop=True).then_inc(g["hf_psum"], 1)

                def down(grp, e):
                    n = E2 * grp + e
                    pe.wait_ge(g["hf"], NC2 * n + NC2)
                    if e >= 2 or later(grp, 1):
                        pe.wait_ge(g["acc"], n - 1)
                    for u in range(GB):
                        for f in range(NC2):
                            last = pe.matmul(bank[4 + e % 2][:, u * P:(u + 1) * P], hidf[:, e % 2, f, u * P:(u + 1) * P], w2f[:, e, f, :],
                                             start=(f == 0), stop=(f == NC2 - 1))
                    last.then_inc(g["eo_psum"], 1)

                def weights_transposed(part):
                    pe.wait_ge(g["g2"], 1)
                    if part:
                        pe.wait_ge(g["h_b2"], part)
                    for b in range(8):
                        last = pe.transpose(bank[6 + b // GB][0:E2, b % GB * P:(b % GB + 1) * P], g2[:, 8 * part + b, :], ident[:])
                    last.then_inc(g["g2T_psum"], 1)

                def second_biases(part):
                    pe.wait_ge(g["g2T"], part + 1)
                    for b in range(8):
                        n = 8 * part + b
                        last = pe.matmul(bank[6 + b // GB][:, b % GB * P:(b % GB + 1) * P], g2T[:, n * P:(n + 1) * P], b2f[:], start=True, stop=True)
                    last.then_inc(g["b2_psum"], 1)

                def group(grp, more):
                    for e in range(E2):
                        beginning = isinstance(grp, int) and grp == 0 and e < 2
                        if beginning:
                            weights_transposed(e)
                        if e + 1 < E2:
                            up(grp, e + 1)
                        elif more:
                            up(grp + 1, 0)
                        if beginning:
                            second_biases(e)
                        down(grp, e)
                up(0, 0)
                group(0, True)
                with pe.Fori(1, NG - 1) as grp:
                    group(grp, True)
                group(NG - 1, False)


def kernel(**inputs):
    import concourse.bacc as bacc
    import ml_dtypes
    from concourse.bass_utils import run_bass_kernel_spmd

    a = {k: np.asarray(v) for k, v in inputs.items()}

    tab_l = np.zeros((43, NF), np.float32)
    tab_l[0:12, 0:7] = a["L0_tok_W_weekday"].T
    tab_l[12:24, 7:31] = a["L0_tok_W_hour"].T
    tab_l[26:34, 31:41] = a["L0_tok_W_dur"].T
    tab_l[34:42, 41:49] = a["L0_tok_W_tdiff"].T
    tab_l[24, 49] = tab_l[25, 50] = tab_l[42, 51] = 1.0
    tab_r = np.concatenate([a["L0_tok_proj_w"].T, a["L0_tok_proj_b"][None, :]])
    bounds = np.stack(bounds_by_column())
    first, n = DUR
    edges = a["L0_tok_dur_boundaries"]
    bounds[0, first], bounds[1, first + n - 1] = -3e38, 3e38
    bounds[0, first + 1:first + n] = edges[1:]
    bounds[1, first:first + n - 1] = edges[1:]
    rel = a["L0_attn_rel_emb"][::-1].T
    bf16 = ml_dtypes.bfloat16

    def heads_apart(w):
        out = np.zeros((*w.shape[:-1], LH, 32), w.dtype)
        out[..., :LD] = w.reshape(*w.shape[:-1], LH, LD)
        return out.reshape(*w.shape[:-1], P)

    q = "L1_attn_"
    token, key, chunk = np.arange(P)[:, None], np.arange(P)[None, :], np.arange(CH)[None, :]
    causal = np.where(key <= token, 0.0, -1e30)
    before = np.where(chunk < token // 2, 0.0, -1e30)
    laid = dict(
        a, ident=np.eye(P, dtype=np.float32), tab_l=tab_l, tab_r=tab_r, bounds=bounds.reshape(-1), relT=np.concatenate([rel, rel]),
        w1m=a["L0_ffn_W1"].transpose(1, 0, 2), w2m=a["L0_ffn_W2"].transpose(1, 0, 2), L0_ffn_b2=a["L0_ffn_b2"].reshape(-1),
        L0_ffn_gamma=a["L0_ffn_gamma"].reshape(-1), b1m=a["L0_ffn_b1"].T, iota=np.arange(E0, dtype=np.float32),
        wqk1=np.stack([a[q + "Wq"], a[q + "Wk"], heads_apart(a[q + "Wrq"]), heads_apart(a[q + "Wrk"])], 1),
        wv1=np.concatenate([a[q + "Wv"], a[q + "Wg"][:P]], 1),
        b1a=np.stack([a[q + "bq"], a[q + "bk"], heads_apart(a[q + "brq"]), heads_apart(a[q + "brk"])], 1),
        rows1=np.concatenate([np.repeat(np.eye(H1), D1, axis=0), np.repeat(np.eye(LH), P // LH, axis=0)], 1).astype(np.float32),
        wg1=a[q + "Wg"][P:, 0], valid=(np.arange(P) >= 2).astype(np.float32)[:, None],
        wroT=np.concatenate([a[q + "Wro"], a[q + "bro"][None, :]]).T,
        identb=np.eye(P).astype(bf16), maskb=np.concatenate([causal, before], 1).astype(bf16),
        wqkv2=np.concatenate([a["L1_ffn_Wq"], a["L1_ffn_Wk"], a["L1_ffn_Wv"]], 1),
        col2=np.stack([a["L1_ffn_ln_g"], a["L1_ffn_ln_b"], np.tile(a["L1_ffn_qn_g"], H2), np.tile(a["L1_ffn_kn_g"], H2)], 1),
        b1f=a["L1_ffn_b1"].reshape(E2, NC2, P).transpose(2, 0, 1),
        w1f=a["L1_ffn_W1"].transpose(1, 0, 2), w2f=a["L1_ffn_W2"].reshape(E2, NC2, P, P).transpose(2, 0, 1, 3))
    names = ["x", "itok_BS_0_1439", "itok_BS_0_7", "fside_BS_durations", "ident", "bounds", "tab_l", "tab_r",
             "L0_tok_ln_w", "L0_tok_ln_b", "L0_attn_Wq", "relT", "L0_attn_Wkv", "L0_attn_Wo", "L0_attn_bo",
             "w1m", "w2m", "L0_ffn_b2", "L0_ffn_gamma", "L0_ffn_beta", "b1m", "L0_ffn_Wg", "iota",
             "wqk1", "wv1", "L1_attn_Wrv", "b1a", "rows1", "L1_attn_bv", "L1_attn_brv", "wg1", "L1_attn_bg", "valid", "wroT",
             "L1_attn_Wo", "L1_attn_bo", "identb", "maskb",
             "wqkv2", "L1_ffn_Wo", "col2", "L1_ffn_gate_W", "L1_ffn_gate_b", "b1f", "L1_ffn_b2", "w1f", "w2f"]

    nc = bacc.Bacc("TRN2", target_bir_lowering=False, num_devices=1)
    arrays, d = {}, {}
    for name in names:
        v = np.ascontiguousarray(laid[name])
        arrays[name + "_dram"] = v
        d[name] = nc.dram_tensor(name + "_dram", v.shape, mybir.dt.from_np(v.dtype), kind="ExternalInput").ap()
    out = nc.dram_tensor("out_dram", (NB, P, P), F32, kind="ExternalOutput").ap()
    build(nc, d, out)
    return run_bass_kernel_spmd(nc, [arrays], core_ids=[0]).results[0]["out_dram"]
```
